# Optimizing a Trainium2 kernel written in Bass

```python
import numpy as np
import jax
import jax.numpy as jnp

def _softmax(x, axis=-1):
    return jax.nn.softmax(x, axis=axis)

def _gelu(x):
    return jax.nn.gelu(x, approximate=True)

def _silu(x):
    return jax.nn.silu(x)

def _sigmoid(x):
    return jax.nn.sigmoid(x)

def _layernorm(x, axis=-1, eps=1e-05):
    m = jnp.mean(x, axis=axis, keepdims=True)
    v = jnp.var(x, axis=axis, keepdims=True)
    return (x - m) / jnp.sqrt(v + eps)

def _scatter_add(tgt, idx, src, axis=0):
    return tgt.at[idx].add(src)

def _segment_sum(src, seg, n):
    return jax.ops.segment_sum(src, seg, n)
kernel_name = 'mk_gnn_resnorm_d4_gnn_r32_0d0b38'

def setup_inputs(seed: int=0):
    np.random.seed(seed)
    _w = jnp.asarray

    def _rec_inputs():
        import jax
        import jax.numpy as jnp
        _gk = jax.random.key(seed)
        x = -6.415e-05 + 1 * jax.random.normal(jax.random.fold_in(_gk, 1), (625, 512), jnp.float32)
        src = jax.random.randint(jax.random.fold_in(_gk, 2), (10000,), 0, 625, jnp.int32)
        dst = jnp.minimum((625 * jax.random.uniform(jax.random.fold_in(_gk, 3), (10000,)) ** 2.0).astype(jnp.int32), 19999)
        _o = jnp.argsort(dst, stable=True)
        src = src[_o]
        dst = dst[_o]
        edge_attr_8 = -0.000521468 + 0.999954 * jax.random.normal(jax.random.fold_in(_gk, 12), (10000, 8), jnp.float32)
        edge_attr_8_n2 = -0.000521468 + 0.999954 * jax.random.normal(jax.random.fold_in(_gk, 13), (10000, 8), jnp.float32)
        node_vec1 = jax.random.uniform(jax.random.fold_in(_gk, 15), (625, 1), jnp.float32, 0.0, 0.999957)
        return (x, src, dst, edge_attr_8, edge_attr_8_n2, node_vec1)
    x, src, dst, edge_attr_8, edge_attr_8_n2, node_vec1 = _rec_inputs()

    def _L0_gnn_setup():
        import jax, jax.numpy as jnp
        import numpy as np
        N = 625
        E = 20000
        D = 512
        H = 8
        DH = D // H
        EPS = 1e-05

        def layer_norm(x, g, b):
            mu = x.mean(-1, keepdims=True)
            var = ((x - mu) ** 2).mean(-1, keepdims=True)
            return (x - mu) * jax.lax.rsqrt(var + EPS) * g + b
        key = jax.random.key(seed)
        ks = jax.random.split(key, 12)
        return dict(node_feature=jax.random.normal(ks[0], (N, D), jnp.float32), src=jax.random.randint(ks[1], (E,), 0, N, dtype=jnp.int32), dst=jax.random.randint(ks[2], (E,), 0, N, dtype=jnp.int32), dist_attn=jax.random.normal(ks[3], (E, H), jnp.float32), path_attn=jax.random.normal(ks[4], (E, H), jnp.float32), Wqkv=jax.random.normal(ks[5], (D, 3 * D), jnp.float32) / np.float32(np.sqrt(D)), bqkv=jnp.zeros((3 * D,), jnp.float32), Wo=jax.random.normal(ks[6], (D, D), jnp.float32) / np.float32(np.sqrt(D)), bo=jnp.zeros((D,), jnp.float32), ln1_g=jnp.ones((D,), jnp.float32), ln1_b=jnp.zeros((D,), jnp.float32), W1=jax.random.normal(ks[7], (D, 4 * D), jnp.float32) / np.float32(np.sqrt(D)), b1=jnp.zeros((4 * D,), jnp.float32), W2=jax.random.normal(ks[8], (4 * D, D), jnp.float32) / np.float32(np.sqrt(4 * D)), b2=jnp.zeros((D,), jnp.float32), ln2_g=jnp.ones((D,), jnp.float32), ln2_b=jnp.zeros((D,), jnp.float32))
    _L0_gnn_all = _L0_gnn_setup()
    _L0_gnn_in = {k: v for k, v in _L0_gnn_all.items() if k in ('Wqkv', 'bqkv', 'Wo', 'bo', 'ln1_g', 'ln1_b', 'W1', 'b1', 'W2', 'b2', 'ln2_g', 'ln2_b')}
    del _L0_gnn_all

    def _L1_gnn_setup():
        import jax, jax.numpy as jnp
        import numpy as np
        N_NODES = 40962
        LATENT_DIM = 512
        N_EDGES = 20481
        NUM_BLOCKS = 4
        NUM_HEADS = 4
        NUM_FREQ = 32
        BASE_PERIOD = 16
        NOISE_EMB_DIM = 16
        EPS = 1e-05

        def _cond_layer_norm(x, cond, sw, sb, bw, bb):
            mu = jnp.mean(x, axis=-1, keepdims=True)
            var = jnp.var(x, axis=-1, keepdims=True)
            xn = (x - mu) * jax.lax.rsqrt(var + EPS)
            scale = cond @ sw + sb
            bias = cond @ bw + bb
            return xn * (1.0 + scale) + bias

        def _sparse_attention(x, src, dst, wq, bq, wk, bk, wv, bv, wo, bo):
            N, D = x.shape
            H, Dh = (NUM_HEADS, D // NUM_HEADS)
            q = (x @ wq + bq).reshape(N, H, Dh) * Dh ** (-0.5)
            k = (x @ wk + bk).reshape(N, H, Dh)
            v = (x @ wv + bv).reshape(N, H, Dh)
            scores = jnp.einsum('ehd,ehd->eh', q[src], k[dst])
            smax = jax.ops.segment_max(scores, src, num_segments=N)
            ex = jnp.exp(scores - smax[src])
            denom = jax.ops.segment_sum(ex, src, num_segments=N)
            attn = ex / denom[src]
            out = jax.ops.segment_sum(attn[:, :, None] * v[dst], src, num_segments=N)
            return out.reshape(N, D) @ wo + bo

        def _forward(x, edge_index, noise_levels, f_w1, f_b1, f_w2, f_b2, s1_w, s1_b, b1_w, b1_b, wq, bq, wk, bk, wv, bv, wo, bo, s2_w, s2_b, b2_w, b2_b, m_w1, m_b1, m_w2, m_b2):
            src, dst = (edge_index[0], edge_index[1])
            freqs = jnp.arange(1, NUM_FREQ + 1, dtype=x.dtype) * (2.0 * np.pi / BASE_PERIOD)
            ph = noise_levels * freqs
            emb = jnp.concatenate([jnp.sin(ph), jnp.cos(ph)], axis=-1)
            cond = jax.nn.silu(emb @ f_w1 + f_b1) @ f_w2 + f_b2
            for i in range(NUM_BLOCKS):
                y = _cond_layer_norm(x, cond, s1_w[i], s1_b[i], b1_w[i], b1_b[i])
                y = _sparse_attention(y, src, dst, wq[i], bq[i], wk[i], bk[i], wv[i], bv[i], wo[i], bo[i])
                x = x + y
                y = _cond_layer_norm(x, cond, s2_w[i], s2_b[i], b2_w[i], b2_b[i])
                y = jax.nn.relu(y @ m_w1[i] + m_b1[i]) @ m_w2[i] + m_b2[i]
                x = x + y
            return x
        key = jax.random.key(seed)
        ks = jax.random.split(key, 20)

        def w(k, shape, s=0.02):
            return jax.random.normal(k, shape, dtype=jnp.float32) * s
        D, B, C = (LATENT_DIM, NUM_BLOCKS, NOISE_EMB_DIM)
        z = lambda *s: jnp.zeros(s, jnp.float32)
        return {'latent_mesh_nodes': jax.random.normal(ks[0], (N_NODES, D), dtype=jnp.float32), 'edge_index': jax.random.randint(ks[1], (2, N_EDGES), 0, N_NODES, dtype=jnp.int32), 'noise_levels': jax.random.uniform(ks[2], (N_NODES, 1), dtype=jnp.float32), 'f_w1': w(ks[3], (2 * NUM_FREQ, C)), 'f_b1': z(C), 'f_w2': w(ks[4], (C, C)), 'f_b2': z(C), 's1_w': w(ks[5], (B, C, D)), 's1_b': z(B, D), 'b1_w': w(ks[6], (B, C, D)), 'b1_b': z(B, D), 'wq': w(ks[7], (B, D, D)), 'bq': z(B, D), 'wk': w(ks[8], (B, D, D)), 'bk': z(B, D), 'wv': w(ks[9], (B, D, D)), 'bv': z(B, D), 'wo': w(ks[10], (B, D, D)), 'bo': z(B, D), 's2_w': w(ks[11], (B, C, D)), 's2_b': z(B, D), 'b2_w': w(ks[12], (B, C, D)), 'b2_b': z(B, D), 'm_w1': w(ks[13], (B, D, D)), 'm_b1': z(B, D), 'm_w2': w(ks[14], (B, D, D)), 'm_b2': z(B, D)}
    _L1_gnn_all = _L1_gnn_setup()
    _L1_gnn_in = {k: v for k, v in _L1_gnn_all.items() if k in ('f_w1', 'f_b1', 'f_w2', 'f_b2', 's1_w', 's1_b', 'b1_w', 'b1_b', 'wq', 'bq', 'wk', 'bk', 'wv', 'bv', 'wo', 'bo', 's2_w', 's2_b', 'b2_w', 'b2_b', 'm_w1', 'm_b1', 'm_w2', 'm_b2')}
    del _L1_gnn_all

    def _L2_gnn_setup():
        import jax, jax.numpy as jnp
        import numpy as np
        N = 50000
        E = 12500
        D_IN = 512
        D_HID = 64
        D_OUT = 512
        key = jax.random.key(seed)
        k1, k2, k3, k4 = jax.random.split(key, 4)
        x = jax.random.normal(k1, (N, D_IN), dtype=jnp.float32)
        edge_index = jax.random.randint(k2, (2, E), 0, N, dtype=jnp.int64)
        W1 = jax.random.normal(k3, (D_IN, D_HID), dtype=jnp.float32) * (1.0 / np.sqrt(D_IN))
        b1 = jnp.zeros((D_HID,), dtype=jnp.float32)
        W2 = jax.random.normal(k4, (D_HID, D_OUT), dtype=jnp.float32) * (1.0 / np.sqrt(D_HID))
        b2 = jnp.zeros((D_OUT,), dtype=jnp.float32)
        return {'x': x, 'edge_index': edge_index, 'W1': W1, 'b1': b1, 'W2': W2, 'b2': b2}
    _L2_gnn_all = _L2_gnn_setup()
    _L2_gnn_in = {k: v for k, v in _L2_gnn_all.items() if k in ('W1', 'b1', 'W2', 'b2')}
    del _L2_gnn_all

    def _L3_gnn_setup():
        import jax, jax.numpy as jnp
        import numpy as np
        N, E, H, D_IN, D_PRIME = (50000, 25000, 8, 512, 64)

        def _segment_softmax(scores, seg, num_segments):
            smax = jax.ops.segment_max(scores, seg, num_segments=num_segments)
            ex = jnp.exp(scores - smax[seg])
            denom = jax.ops.segment_sum(ex, seg, num_segments=num_segments)
            return ex / denom[seg]
        key = jax.random.key(seed)
        ks = jax.random.split(key, 6)
        x = jax.random.normal(ks[0], (N, D_IN), dtype=jnp.float32)
        edge_index = jax.random.randint(ks[1], (2, E), 0, N)
        Ws = jax.random.normal(ks[2], (H, D_IN, D_PRIME), dtype=jnp.float32) * 0.05
        Wb = jax.random.normal(ks[3], (H, D_PRIME), dtype=jnp.float32) * 0.05
        a_w = jax.random.normal(ks[4], (H, 2 * D_PRIME), dtype=jnp.float32) * 0.05
        a_b = jax.random.normal(ks[5], (H,), dtype=jnp.float32) * 0.05
        return dict(x=x, edge_index=edge_index, Ws=Ws, Wb=Wb, a_w=a_w, a_b=a_b)
    _L3_gnn_all = _L3_gnn_setup()
    _L3_gnn_in = {k: v for k, v in _L3_gnn_all.items() if k in ('Ws', 'Wb', 'a_w', 'a_b')}
    del _L3_gnn_all
    return {'x': x, 'src': src, 'dst': dst, 'edge_attr_8': edge_attr_8, 'edge_attr_8_n2': edge_attr_8_n2, 'node_vec1': node_vec1, 'L0_gnn_Wqkv': _L0_gnn_in['Wqkv'], 'L0_gnn_bqkv': _L0_gnn_in['bqkv'], 'L0_gnn_Wo': _L0_gnn_in['Wo'], 'L0_gnn_bo': _L0_gnn_in['bo'], 'L0_gnn_ln1_g': _L0_gnn_in['ln1_g'], 'L0_gnn_ln1_b': _L0_gnn_in['ln1_b'], 'L0_gnn_W1': _L0_gnn_in['W1'], 'L0_gnn_b1': _L0_gnn_in['b1'], 'L0_gnn_W2': _L0_gnn_in['W2'], 'L0_gnn_b2': _L0_gnn_in['b2'], 'L0_gnn_ln2_g': _L0_gnn_in['ln2_g'], 'L0_gnn_ln2_b': _L0_gnn_in['ln2_b'], 'L1_gnn_f_w1': _L1_gnn_in['f_w1'], 'L1_gnn_f_b1': _L1_gnn_in['f_b1'], 'L1_gnn_f_w2': _L1_gnn_in['f_w2'], 'L1_gnn_f_b2': _L1_gnn_in['f_b2'], 'L1_gnn_s1_w': _L1_gnn_in['s1_w'], 'L1_gnn_s1_b': _L1_gnn_in['s1_b'], 'L1_gnn_b1_w': _L1_gnn_in['b1_w'], 'L1_gnn_b1_b': _L1_gnn_in['b1_b'], 'L1_gnn_wq': _L1_gnn_in['wq'], 'L1_gnn_bq': _L1_gnn_in['bq'], 'L1_gnn_wk': _L1_gnn_in['wk'], 'L1_gnn_bk': _L1_gnn_in['bk'], 'L1_gnn_wv': _L1_gnn_in['wv'], 'L1_gnn_bv': _L1_gnn_in['bv'], 'L1_gnn_wo': _L1_gnn_in['wo'], 'L1_gnn_bo': _L1_gnn_in['bo'], 'L1_gnn_s2_w': _L1_gnn_in['s2_w'], 'L1_gnn_s2_b': _L1_gnn_in['s2_b'], 'L1_gnn_b2_w': _L1_gnn_in['b2_w'], 'L1_gnn_b2_b': _L1_gnn_in['b2_b'], 'L1_gnn_m_w1': _L1_gnn_in['m_w1'], 'L1_gnn_m_b1': _L1_gnn_in['m_b1'], 'L1_gnn_m_w2': _L1_gnn_in['m_w2'], 'L1_gnn_m_b2': _L1_gnn_in['m_b2'], 'L2_gnn_W1': _L2_gnn_in['W1'], 'L2_gnn_b1': _L2_gnn_in['b1'], 'L2_gnn_W2': _L2_gnn_in['W2'], 'L2_gnn_b2': _L2_gnn_in['b2'], 'L3_gnn_Ws': _L3_gnn_in['Ws'], 'L3_gnn_Wb': _L3_gnn_in['Wb'], 'L3_gnn_a_w': _L3_gnn_in['a_w'], 'L3_gnn_a_b': _L3_gnn_in['a_b']}

def reference(x, src, dst, edge_attr_8, edge_attr_8_n2, node_vec1, L0_gnn_Wqkv, L0_gnn_bqkv, L0_gnn_Wo, L0_gnn_bo, L0_gnn_ln1_g, L0_gnn_ln1_b, L0_gnn_W1, L0_gnn_b1, L0_gnn_W2, L0_gnn_b2, L0_gnn_ln2_g, L0_gnn_ln2_b, L1_gnn_f_w1, L1_gnn_f_b1, L1_gnn_f_w2, L1_gnn_f_b2, L1_gnn_s1_w, L1_gnn_s1_b, L1_gnn_b1_w, L1_gnn_b1_b, L1_gnn_wq, L1_gnn_bq, L1_gnn_wk, L1_gnn_bk, L1_gnn_wv, L1_gnn_bv, L1_gnn_wo, L1_gnn_bo, L1_gnn_s2_w, L1_gnn_s2_b, L1_gnn_b2_w, L1_gnn_b2_b, L1_gnn_m_w1, L1_gnn_m_b1, L1_gnn_m_w2, L1_gnn_m_b2, L2_gnn_W1, L2_gnn_b1, L2_gnn_W2, L2_gnn_b2, L3_gnn_Ws, L3_gnn_Wb, L3_gnn_a_w, L3_gnn_a_b):
    import jax
    import jax.numpy as jnp

    def _L0_gnn_ref(node_feature, src, dst, dist_attn, path_attn, Wqkv, bqkv, Wo, bo, ln1_g, ln1_b, W1, b1, W2, b2, ln2_g, ln2_b):
        import jax, jax.numpy as jnp
        import numpy as np
        N = 625
        E = 20000
        D = 512
        H = 8
        DH = D // H
        EPS = 1e-05

        def layer_norm(x, g, b):
            mu = x.mean(-1, keepdims=True)
            var = ((x - mu) ** 2).mean(-1, keepdims=True)
            return (x - mu) * jax.lax.rsqrt(var + EPS) * g + b
        h = layer_norm(node_feature, ln1_g, ln1_b)
        qkv = (h @ Wqkv + bqkv).reshape(N, 3, H, DH)
        q = qkv[:, 0] * D ** (-0.5)
        k = qkv[:, 1]
        v = qkv[:, 2]
        logits = jnp.einsum('ehd,ehd->eh', q[src], k[dst])
        a = logits + dist_attn + path_attn
        mx = jax.ops.segment_max(a, dst, num_segments=N)
        e = jnp.exp(a - mx[dst])
        s = jax.ops.segment_sum(e, dst, num_segments=N)
        sa = e / s[dst]
        msg = v[src] * sa[:, :, None]
        agg = jax.ops.segment_sum(msg, dst, num_segments=N).reshape(N, D)
        x = agg @ Wo + bo
        h1 = node_feature + x
        h2 = layer_norm(h1, ln2_g, ln2_b)
        h2 = jax.nn.gelu(h2 @ W1 + b1, approximate=False) @ W2 + b2
        return h1 + h2

    def _L1_gnn_ref(latent_mesh_nodes, edge_index, noise_levels, f_w1, f_b1, f_w2, f_b2, s1_w, s1_b, b1_w, b1_b, wq, bq, wk, bk, wv, bv, wo, bo, s2_w, s2_b, b2_w, b2_b, m_w1, m_b1, m_w2, m_b2):
        import jax, jax.numpy as jnp
        import numpy as np
        N_NODES = 40962
        LATENT_DIM = 512
        N_EDGES = 20481
        NUM_BLOCKS = 4
        NUM_HEADS = 4
        NUM_FREQ = 32
        BASE_PERIOD = 16
        NOISE_EMB_DIM = 16
        EPS = 1e-05

        def _cond_layer_norm(x, cond, sw, sb, bw, bb):
            mu = jnp.mean(x, axis=-1, keepdims=True)
            var = jnp.var(x, axis=-1, keepdims=True)
            xn = (x - mu) * jax.lax.rsqrt(var + EPS)
            scale = cond @ sw + sb
            bias = cond @ bw + bb
            return xn * (1.0 + scale) + bias

        def _sparse_attention(x, src, dst, wq, bq, wk, bk, wv, bv, wo, bo):
            N, D = x.shape
            H, Dh = (NUM_HEADS, D // NUM_HEADS)
            q = (x @ wq + bq).reshape(N, H, Dh) * Dh ** (-0.5)
            k = (x @ wk + bk).reshape(N, H, Dh)
            v = (x @ wv + bv).reshape(N, H, Dh)
            scores = jnp.einsum('ehd,ehd->eh', q[src], k[dst])
            smax = jax.ops.segment_max(scores, src, num_segments=N)
            ex = jnp.exp(scores - smax[src])
            denom = jax.ops.segment_sum(ex, src, num_segments=N)
            attn = ex / denom[src]
            out = jax.ops.segment_sum(attn[:, :, None] * v[dst], src, num_segments=N)
            return out.reshape(N, D) @ wo + bo

        def _forward(x, edge_index, noise_levels, f_w1, f_b1, f_w2, f_b2, s1_w, s1_b, b1_w, b1_b, wq, bq, wk, bk, wv, bv, wo, bo, s2_w, s2_b, b2_w, b2_b, m_w1, m_b1, m_w2, m_b2):
            src, dst = (edge_index[0], edge_index[1])
            freqs = jnp.arange(1, NUM_FREQ + 1, dtype=x.dtype) * (2.0 * np.pi / BASE_PERIOD)
            ph = noise_levels * freqs
            emb = jnp.concatenate([jnp.sin(ph), jnp.cos(ph)], axis=-1)
            cond = jax.nn.silu(emb @ f_w1 + f_b1) @ f_w2 + f_b2
            for i in range(NUM_BLOCKS):
                y = _cond_layer_norm(x, cond, s1_w[i], s1_b[i], b1_w[i], b1_b[i])
                y = _sparse_attention(y, src, dst, wq[i], bq[i], wk[i], bk[i], wv[i], bv[i], wo[i], bo[i])
                x = x + y
                y = _cond_layer_norm(x, cond, s2_w[i], s2_b[i], b2_w[i], b2_b[i])
                y = jax.nn.relu(y @ m_w1[i] + m_b1[i]) @ m_w2[i] + m_b2[i]
                x = x + y
            return x
        return _forward(latent_mesh_nodes, edge_index, noise_levels, f_w1, f_b1, f_w2, f_b2, s1_w, s1_b, b1_w, b1_b, wq, bq, wk, bk, wv, bv, wo, bo, s2_w, s2_b, b2_w, b2_b, m_w1, m_b1, m_w2, m_b2)

    def _L2_gnn_ref(x, edge_index, W1, b1, W2, b2):
        import jax, jax.numpy as jnp
        import numpy as np
        N = 50000
        E = 12500
        D_IN = 512
        D_HID = 64
        D_OUT = 512
        h = jax.nn.relu(x @ W1 + b1) @ W2 + b2
        row, col = (edge_index[0], edge_index[1])
        agg = jax.ops.segment_sum(h[col], row, num_segments=h.shape[0])
        return h + agg

    def _L3_gnn_ref(x, edge_index, Ws, Wb, a_w, a_b):
        import jax, jax.numpy as jnp
        import numpy as np
        N, E, H, D_IN, D_PRIME = (50000, 25000, 8, 512, 64)

        def _segment_softmax(scores, seg, num_segments):
            smax = jax.ops.segment_max(scores, seg, num_segments=num_segments)
            ex = jnp.exp(scores - smax[seg])
            denom = jax.ops.segment_sum(ex, seg, num_segments=num_segments)
            return ex / denom[seg]
        v_src, v_tgt = (edge_index[0], edge_index[1])
        n = x.shape[0]
        outs = []
        for h in range(Ws.shape[0]):
            Wx = x @ Ws[h] + Wb[h]
            d = Wx.shape[-1]
            s = Wx[v_tgt] @ a_w[h, :d] + Wx[v_src] @ a_w[h, d:] + a_b[h]
            s = jax.nn.leaky_relu(s, negative_slope=0.2)
            alpha = _segment_softmax(s, v_tgt, n)
            outs.append(jax.ops.segment_sum(alpha[:, None] * Wx[v_src], v_tgt, num_segments=n))
        return jnp.stack(outs, axis=1).reshape(n, -1)
    edge_index = jnp.stack([src, dst])
    x = _layernorm(x + _L0_gnn_ref(x, src, dst, edge_attr_8, edge_attr_8_n2, L0_gnn_Wqkv, L0_gnn_bqkv, L0_gnn_Wo, L0_gnn_bo, L0_gnn_ln1_g, L0_gnn_ln1_b, L0_gnn_W1, L0_gnn_b1, L0_gnn_W2, L0_gnn_b2, L0_gnn_ln2_g, L0_gnn_ln2_b), axis=-1)
    x = _layernorm(x + _L1_gnn_ref(x, edge_index, node_vec1, L1_gnn_f_w1, L1_gnn_f_b1, L1_gnn_f_w2, L1_gnn_f_b2, L1_gnn_s1_w, L1_gnn_s1_b, L1_gnn_b1_w, L1_gnn_b1_b, L1_gnn_wq, L1_gnn_bq, L1_gnn_wk, L1_gnn_bk, L1_gnn_wv, L1_gnn_bv, L1_gnn_wo, L1_gnn_bo, L1_gnn_s2_w, L1_gnn_s2_b, L1_gnn_b2_w, L1_gnn_b2_b, L1_gnn_m_w1, L1_gnn_m_b1, L1_gnn_m_w2, L1_gnn_m_b2), axis=-1)
    x = _layernorm(x + _L2_gnn_ref(x, edge_index, L2_gnn_W1, L2_gnn_b1, L2_gnn_W2, L2_gnn_b2), axis=-1)
    x = _layernorm(x + _L3_gnn_ref(x, edge_index, L3_gnn_Ws, L3_gnn_Wb, L3_gnn_a_w, L3_gnn_a_b), axis=-1)
    return x

_drawn_inputs = setup_inputs


def setup_inputs(seed=0):
    import zlib

    import numpy as np

    out = dict(_drawn_inputs(seed))
    spreads = {'L0_gnn_bqkv': (0.0, 0.1),
     'L0_gnn_bo': (0.0, 0.1),
     'L0_gnn_ln1_g': (1.0, 0.6),
     'L0_gnn_ln1_b': (0.0, 0.1),
     'L0_gnn_b1': (0.0, 0.289),
     'L0_gnn_b2': (0.0, 0.1),
     'L0_gnn_ln2_g': (1.0, 0.6),
     'L0_gnn_ln2_b': (0.0, 0.1),
     'L1_gnn_f_b1': (0.0, 0.8),
     'L1_gnn_f_b2': (0.0, 0.8),
     'L1_gnn_s1_b': (0.0, 0.8),
     'L1_gnn_b1_b': (0.0, 0.35),
     'L1_gnn_bq': (0.0, 0.8),
     'L1_gnn_bk': (0.0, 2.0),
     'L1_gnn_bv': (0.0, 0.1),
     'L1_gnn_bo': (0.0, 0.1),
     'L1_gnn_s2_b': (0.0, 0.8),
     'L1_gnn_b2_b': (0.0, 0.667),
     'L1_gnn_m_b1': (0.0, 0.302),
     'L1_gnn_m_b2': (0.0, 0.1),
     'L2_gnn_b1': (0.0, 0.1),
     'L2_gnn_b2': (0.0, 0.1)}
    factors = {'node_vec1': 8.0,
     'L1_gnn_f_w1': 8.0,
     'L1_gnn_f_w2': 8.0,
     'L1_gnn_s1_w': 8.0,
     'L1_gnn_b1_w': 8.0,
     'L1_gnn_wq': 8.0,
     'L1_gnn_wk': 8.0,
     'L1_gnn_s2_w': 8.0,
     'L1_gnn_b2_w': 8.0,
     'L3_gnn_a_w': 6.879,
     'L3_gnn_a_b': 200.0}
    for name, (base, spread) in spreads.items():
        noise = np.random.default_rng([zlib.crc32(name.encode()), seed]).standard_normal(out[name].shape)
        drawn = base * np.exp(spread * noise) if base else spread * noise
        out[name] = jnp.asarray(drawn.astype(out[name].dtype))
    for name, factor in factors.items():
        out[name] = (out[name] * factor).astype(out[name].dtype)
    return out
```

```python
import concourse.bass as bass
from concourse import mybir
from contextlib import ExitStack

NODES, EDGES, D = 625, 10000, 512
TILE = 125
NT = NODES // TILE
CHUNKS = EDGES // TILE
FT = D // 128
DH0, H0 = 64, 8
FF0 = 4 * D // 128
LAYERS, H1, DH1 = 4, 4, 128
COND, NFREQ = 16, 32
HID2 = 64
H3, DH3 = 8, 64
EPS = 1e-5
BIG = 1.0e30
HALF = 4
TAIL = NODES - 512

COLS = {}
_n = 0
for _name, _width in (("ln1_g", FT), ("ln1_b", FT), ("ln2_g", FT), ("ln2_b", FT), ("bq", FT), ("bk", FT), ("b1", FF0),
                      ("f_b1", 1), ("f_b2", 1), ("c_b1", 1), ("freq", 1), ("turn", 1), ("angle", 1),
                      ("layers", LAYERS * 7 * FT)):
    COLS[_name] = _n
    _n += _width
NCOLS = _n
S1B, B1B, BQ, BK, S2B, B2B, MB1 = (FT * k for k in range(7))


class PsumRing:

    def __init__(self, ps, filled, evacuated, keys, opened=0):
        self.ps, self.filled, self.evacuated = ps, filled, evacuated
        self.order = {k: n for n, k in enumerate(keys)}
        self.total = len(self.order)
        self.turn = None
        self.opened = opened

    def view(self, key, p=TILE):
        s = self.order[key] % 4
        return self.ps[0:p, 1024 * s:1024 * s + 1024]

    def uses(self, s):
        return (self.total - s + 3) // 4

    def _value(self, local, per_turn):
        return local if self.turn is None else self.turn * per_turn + local

    def open(self, pe):
        for s in range(4):
            pe.sem_inc(self.evacuated[s], self.opened)

    def claim(self, pe, key):
        n = self.order[key]
        if n >= 4 or self.turn is not None:
            pe.wait_ge(self.evacuated[n % 4], self._value(n // 4 + self.opened, self.uses(n % 4)))

    def fill(self, matmul):
        matmul.then_inc(self.filled, 1)

    def wait_filled(self, eng, key):
        eng.wait_ge(self.filled, self._value(self.order[key] + 1, self.total))

    def release(self, key, instruction):
        instruction.then_inc(self.evacuated[self.order[key] % 4], 1)

    def wait_evacuated(self, eng, key):
        n = self.order[key]
        eng.wait_ge(self.evacuated[n % 4], self._value(n // 4 + 1 + self.opened, self.uses(n % 4)))


class Chain:

    def __init__(self, semaphore):
        self.semaphore, self.count, self.turn, self.per_turn = semaphore, 0, None, 0

    def __call__(self, eng, instruction):
        instruction.then_inc(self.semaphore, 1)
        self.count += 1
        eng.wait_ge(self.semaphore, self.count if self.turn is None else self.turn * self.per_turn + self.count)


def build(nc, x, src_t, dst_t, attr_a, attr_b, noise, cols_d,
          w_qkv, w_o0, w_up0, w_down0, rows0,
          f_w1, f_w2, cond_w, wq, wk, wv, wo, m_w1, m_w2, rows1,
          c_w1, c_w2, c_b2, ws3, rows3, ab3, out):
    f32, bf16, f16 = mybir.dt.float32, mybir.dt.bfloat16, mybir.dt.float16
    i32, u32 = mybir.dt.int32, mybir.dt.uint32
    ALU, ACT, AX = mybir.AluOpType, mybir.ActivationFunctionType, mybir.AxisListType

    logits_d = nc.dram_tensor("logits_scratch", (NODES * NODES, H0), f32, kind="Internal").ap()
    v0_d = nc.dram_tensor("value_scratch", (NODES, D), f32, kind="Internal").ap()
    x1_d = nc.dram_tensor("block_input_scratch", (NODES, D), f32, kind="Internal").ap()

    with ExitStack() as ctx:
        def sem(name):
            return ctx.enter_context(nc.semaphore(name))

        def sbuf(name, shape, dt=f32):
            return ctx.enter_context(nc.sbuf_tensor(name, shape, dt))

        ARENA_WORDS = 47940
        arena = sbuf("arena", [128, ARENA_WORDS])

        def at(offset, *dims, p=128, p0=0):
            size = 1
            for d in dims:
                size *= d
            flat = arena[p0:p0 + p, offset:offset + size]
            if len(dims) == 1:
                return flat
            names = "abcd"[:len(dims)]
            return flat.rearrange("p (" + " ".join(names) + ") -> p " + " ".join(names), **dict(zip(names, dims)))

        R_X, R_Y, R_V, R_Q, R_K, R_O = (2560 * k for k in range(6))
        R_P = 15360
        R_PT = R_P + 2 * NT * NODES
        R_LC = R_PT + 2 * NT * NODES
        R_C = R_LC + NT * NODES
        R_W = R_C + NT * NODES
        R_B = R_W + 6 * FT * D

        X = at(R_X, NT, D, p=TILE)
        YT = at(R_Y, FT, NODES)
        V = at(R_V, NT, D, p=TILE)
        XN = V
        QT = at(R_Q, FT, NODES)
        KT = at(R_K, FT, NODES)
        OT = at(R_O, FT, NODES)
        P = at(R_P, 2, NT, NODES, p=TILE)
        PT = at(R_PT, 2, NT * NT * TILE, p=TILE)
        LC = at(R_LC, NT, NODES, p=TILE)
        C2 = at(R_C, NT, NODES, p=TILE)
        ROWS = at(R_B, 3, D, p=TILE)
        WQKV = at(R_P, FT, 3 * D)
        STAGE = [at(R_P + 6144, NODES, H0, p=TILE), at(R_W, NODES, H0, p=TILE)]
        MASK = at(R_W + 5000, NT, NODES, p=TILE)
        WO0 = at(R_W + 8192, FT, D)
        TEMP = at(R_W + 10240, 3, NODES, p=TILE)
        ATTR = at(R_LC, 2, CHUNKS * H0, p=TILE)
        OH16 = at(R_LC + 1280, 2 * 1250, p=TILE).bitcast(bf16).rearrange("p (k r n) -> p k r n", k=2, r=4)
        OH32 = at(R_Q, HALF, NODES, p=TILE)
        MSG = at(R_K, HALF, D, p=TILE)
        VG = at(R_P, 2, HALF, D, p=TILE)
        HT0 = at(R_V, FF0, NODES)
        WUP0 = at(R_P, FT, 4 * D)
        WDN0 = at(R_W, FF0, D)
        M1, M2, WO, WV, WK, WQ = (at(R_W + FT * D * k, FT, D) for k in range(6))
        SC = KT
        BI = {1: OT, 2: QT}
        HT = QT
        XIN = at(R_O, NT, D, p=TILE)
        WS3 = at(R_W, FT, D)
        OUT3 = XIN
        PROD = at(R_K, 2, D, p=TILE)
        HID2T = at(R_Q, NODES, p=HID2)
        AW = at(R_W + FT * D, 3, D, p=TILE)

        cols = sbuf("cols", [128, NCOLS])
        cols1 = sbuf("cols_plus_one", [128, LAYERS * 7 * FT])
        ident = sbuf("ident", [128, 128])
        iota16 = sbuf("iota_row", [128, NODES], f16)
        src_i = sbuf("src_idx", [TILE, CHUNKS], i32)
        dst_i = sbuf("dst_idx", [TILE, CHUNKS], i32)
        src_f = sbuf("src_f", [TILE, CHUNKS])
        dst_f = sbuf("dst_f", [TILE, CHUNKS])
        pair_f = sbuf("pair_f", [TILE, CHUNKS])
        pair_i = sbuf("pair_idx", [TILE, CHUNKS], i32)
        idx_ring = sbuf("idx_ring", [TILE, 2, 2, HALF], i32)
        lg_ring = sbuf("logit_ring", [TILE, 2, HALF * H0])
        sum_ring = sbuf("edge_logits", [TILE, 2, HALF * H0])
        p_ring = sbuf("edge_probs", [TILE, 2, HALF * H0])
        gmax = sbuf("attr_max", [TILE, 2])
        zero16 = sbuf("zero16", [1, 512], bf16)
        zero32 = sbuf("zero32", [1, 512])
        stats = sbuf("bn_stats", [TILE, NT, 6])
        mv = sbuf("mean_var", [TILE, NT, 2])
        rstd = sbuf("rstd", [TILE, NT])
        vare = sbuf("var_eps", [TILE, NT])
        lnc = sbuf("ln_consts", [TILE, 2])
        negm = sbuf("neg_max", [TILE, 2, NT])
        psums = sbuf("prob_sums", [TILE, 2, NT])
        rinv = sbuf("prob_rinv", [TILE, 2, NT])
        has1 = sbuf("has_edge_src", [TILE, NT])
        has2 = sbuf("has_edge_dst", [TILE, NT])
        negm0 = sbuf("neg_max0", [TILE, 3])
        den = sbuf("den", [TILE, NT, H0])
        rden = sbuf("rden", [TILE, NT, H0])
        condT = sbuf("condT", [128, NODES])
        condw = sbuf("cond_weights", [128, D])
        fw1 = sbuf("f_w1", [2 * NFREQ, COND])
        fw2 = sbuf("f_w2", [COND, 128])
        cw1 = sbuf("c_w1", [128, FT, HID2])
        cw2 = sbuf("c_w2", [HID2, D])
        g_bc = sbuf("g_column", [TILE, NT, TILE])
        fcol = sbuf("f_cols", [TILE, NT, H3])
        gcol = sbuf("g_cols", [TILE, NT, H3])
        ab = sbuf("ab3", [TILE, H3])
        NOISE, PHASE, TURNS, EMB = (at(R_O + 640 * k, NODES, p=2 * NFREQ) for k in range(4))
        HIDC = at(R_O, NODES, p=COND)
        LTMP = at(R_P + 8192, NT, NODES, p=TILE)
        XIN0 = at(R_LC - 2560, NT, D, p=TILE)
        ps = ctx.enter_context(nc.psum_tensor("ps", [128, 4096], f32))

        S = {}

        def sig(name):
            if name not in S:
                S[name] = sem(name)
            return S[name]

        def ring(name, keys, opened=0):
            return PsumRing(ps, sig(name + "_filled"), [sig(f"{name}_evacuated{s}") for s in range(4)], keys, opened)

        PAIRS = [(0, 1), (2, 3), (4,)]
        TGROUPS = [range(8 * n, min(8 * n + 8, NT * NT)) for n in range(4)]
        A = ring("front", [("hid",), ("cond",)]
                 + [("t", k) for k in range(FT)]
                 + [(n, k) for k in range(FT) for n in "qk"]
                 + [("v", n) for n in range(3)]
                 + [("s", j, h) for j in range(NT) for h in range(H0)]
                 + [("c1", n) for n in range(4)]
                 + [("at", k) for k in range(FT)] + [("o", n) for n in range(3)]
                 + [("t2", k) for k in range(FT)]
                 + [("up", f) for f in range(FF0)] + [("down", n) for n in range(3)])

        def attend(h):
            return [("pt", h, n) for n in range(4)] + [("av", h)]

        def scores(h):
            return [("q", h), ("k", h)] + [("s", h, i) for i in range(NT)]

        def conditioning(n):
            return [(name, n, k) for k in range(FT) for name in ("scale", "bias")]

        B = ring("layer", conditioning(1) + [("t", 1, k) for k in range(FT)]
                 + scores(0) + scores(1) + [("v", n) for n in range(3)] + attend(0)
                 + scores(2) + attend(1) + scores(3) + attend(2) + conditioning(2) + attend(3)
                 + [("o", n) for n in range(3)]
                 + [("t", 2, k) for k in range(FT)]
                 + [("m1", f) for f in range(FT)] + [("m2", n) for n in range(3)], opened=1)

        def attend3(h):
            return [("pt", h, n) for n in range(4)] + [("av", h)]

        C = ring("back", [("t", 2, k) for k in range(FT)] + [("hid",)] + [("h", n) for n in range(3)]
                 + [("agg", n) for n in range(3)]
                 + [("t", 3, k) for k in range(FT)] + [("wx", n) for n in range(3)]
                 + [("g", 0)] + [k for h in range(H3) for k in ([("g", h + 1)] if h + 1 < H3 else []) + attend3(h)])

        pe_chain, dve_chain, pool_chain, act_chain = (Chain(sig(n + "_chain")) for n in ("pe", "dve", "pool", "act"))
        dve_loop_chain, pool_loop_chain = Chain(sig("dve_loop_chain")), Chain(sig("pool_loop_chain"))

        block = ctx.enter_context(nc.Block())

        def part_wait(eng, name):
            eng.sem_inc(sig("parted_" + name), 1)

        def rows_view(dram):
            return dram.rearrange("(t p) n -> p t n", p=TILE)

        def feat_view(dram):
            return dram.rearrange("(k p) n -> p k n", p=128)

        def spread(dram_row, p=TILE):
            return dram_row.partition_broadcast(p)

        @block.sync
        def _(sp):
            def load(dst, src, name):
                sp.dma_start(dst, src).then_inc(sig("ld_" + name), 16)

            load(X, rows_view(x), "x")
            load(src_i[:, :], src_t, "idx")
            load(dst_i[:, :], dst_t, "idx")
            load(cols[:, :], cols_d, "cols")
            load(NOISE, noise.rearrange("n o -> o n").partition_broadcast(2 * NFREQ), "noise")
            load(fw1[:, :], f_w1, "fw")
            load(fw2[:, :], f_w2, "fw")
            load(WQKV, feat_view(w_qkv), "wqkv")
            load(ROWS, rows0.partition_broadcast(TILE), "rows0")
            load(ATTR[:, 0, :], attr_a, "attr")
            load(ATTR[:, 1, :], attr_b, "attr")
            load(WO0, feat_view(w_o0), "wo0")
            load(cw1[:, :, :], feat_view(c_w1), "c")
            load(cw2[:, :], c_w2, "c")
            load(ab[:, :], ab3.partition_broadcast(TILE), "c")
            for q in range(4):
                load(condw[32 * q:32 * q + COND, :], cond_w[q, 0, :, :], "condw")
            for n in range(3):
                A.wait_evacuated(sp, ("v", n))
            sp.dma_start(rows_view(v0_d), V).then_inc(sig("v0_stored"), 16)
            lg_v = logits_d.rearrange("(j p s) h -> j p (s h)", j=NT, p=TILE)
            for j in range(NT):
                sp.wait_ge(sig("stage_ready"), H0 * (j + 1))
                sp.dma_start(lg_v[j], STAGE[j % 2].rearrange("p s h -> p (s h)")).then_inc(sig(f"stage_stored{j % 2}"), 16)
            sp.wait_ge(sig("stage_stored1"), 16 * (NT // 2))
            load(WDN0, feat_view(w_down0), "wdown0")
            sp.wait_ge(sig("stage_stored0"), 16 * ((NT + 1) // 2))
            sp.wait_ge(sig("msg_ready"), CHUNKS)
            load(WUP0, feat_view(w_up0), "wup0")
            sp.wait_ge(sig("lc_ready"), 1)
            load(XIN0, rows_view(x), "x0")
            A.wait_filled(sp, ("o", 2))
            w_of = {"wq": (WQ, wq), "wk": (WK, wk), "wv": (WV, wv), "wo": (WO, wo), "m1": (M1, m_w1), "m2": (M2, m_w2)}

            def load_weight(name, layer):
                dst, src = w_of[name]
                load(dst, src[layer].rearrange("a (k p) n -> p (a k) n", p=128), name)

            def load_row(n, layer):
                load(ROWS[:, n, :], rows1[n, layer, :].partition_broadcast(TILE), f"row{n}")

            load_weight("wq", slice(0, 1))
            load_weight("wk", slice(0, 1))
            A.wait_filled(sp, ("down", 2))
            sp.wait_ge(sig("residual_biased"), 2)
            for name in ("wv", "wo", "m1", "m2"):
                load_weight(name, slice(0, 1))
            for n in range(3):
                load_row(n, slice(0, 1))
            sp.wait_ge(sig("x1_ready"), NT)
            sp.dma_start(rows_view(x1_d), X).then_inc(sig("x1_stored"), 16)
            with sp.Fori(0, LAYERS - 1) as i:
                B.turn = i
                nxt = bass.ds(i + 1, 1)
                B.wait_filled(sp, ("q", 3))
                load_weight("wq", nxt)
                B.wait_filled(sp, ("k", 3))
                load_weight("wk", nxt)
                B.wait_filled(sp, ("v", 2))
                load_weight("wv", nxt)
                B.wait_evacuated(sp, ("v", 2))
                load_row(0, nxt)
                B.wait_filled(sp, ("bias", 2, FT - 1))
                for q in range(4):
                    load(condw[32 * q:32 * q + COND, :], cond_w[q, nxt, :, :].rearrange("a c n -> (a c) n"), "condw")
                sp.wait_ge(sig("residual_biased1"), 2 * i + 1)
                load_row(1, nxt)
                B.wait_filled(sp, ("o", 2))
                load_weight("wo", nxt)
                B.wait_filled(sp, ("m1", FT - 1))
                load_weight("m1", nxt)
                sp.wait_ge(sig("residual_biased1"), 2 * i + 2)
                load_row(2, nxt)
                B.wait_filled(sp, ("m2", 2))
                load_weight("m2", nxt)
            B.turn = LAYERS - 1
            B.wait_filled(sp, ("q", 3))
            sp.wait_ge(sig("residual_biased1"), 2 * LAYERS)
            load(ROWS[:, 0, :], c_b2.partition_broadcast(TILE), "rows3")
            B.wait_filled(sp, ("m2", 2))
            load(WS3, feat_view(ws3), "ws3")
            load(AW, rows3.partition_broadcast(TILE), "aw")
            sp.wait_ge(sig("x1_stored"), 16)
            load(XIN, rows_view(x1_d), "x1")
            sp.wait_ge(sig("out_ready"), NT)
            sp.dma_start(rows_view(out), X).then_inc(sig("out_stored"), 16)
            sp.wait_ge(sig("out_stored"), 16)

        @block.gpsimd
        def _(pool):
            g = nc.gpsimd
            g.memset(zero16[:, :], 0.0)
            g.memset(zero32[:, :], 0.0).then_inc(sig("zeros_ready"), 1)
            g.memset(lnc[:, 0:1], EPS)
            g.memset(lnc[:, 1:2], -0.5)
            g.iota(iota16[:, :], pattern=[[1, NODES]], base=0, channel_multiplier=0,
                   allow_small_or_imprecise_dtypes=True).then_inc(sig("iota_ready"), 1)
            pool_chain(pool, g.memset(ident[:, :], 0.0))
            g.affine_select(out=ident[:, :], in_=ident[:, :], compare_op=ALU.not_equal, fill=1.0, base=0,
                            pattern=[[-1, 128]], channel_multiplier=1).then_inc(sig("ident_ready"), 1)

            def powers(sems, chain, base):
                var_ready, rstd_ready = sems
                for t in range(NT):
                    pool.wait_ge(var_ready, base + t + 1)
                    chain(pool, g.tensor_tensor(vare[:, t:t + 1], mv[:, t, 1:2], lnc[:, 0:1], ALU.add))
                    g.tensor_tensor(rstd[:, t:t + 1], vare[:, t:t + 1], lnc[:, 1:2], ALU.pow).then_inc(rstd_ready, 1)

            front = (sig("var_ready"), sig("rstd_ready"))
            powers(front, pool_chain, 0)
            pool.wait_ge(sig("gmax_part"), 1)
            g.partition_all_reduce(gmax[:, 1:2], gmax[:, 0:1], TILE, bass.bass_isa.ReduceOp.max).then_inc(sig("gmax_all"), 1)
            pool.wait_ge(sig("xn_ready"), NT)
            pool.wait_ge(sig("ld_rows0"), 16)
            g.tensor_tensor(X, X, ROWS[:, 1:2, :].to_broadcast([TILE, NT, D]), ALU.add).then_inc(sig("residual_biased"), 1)
            for j in range(2):
                pool.wait_ge(sig(f"stage_stored{j}"), 16 * ((NT + 1 - j) // 2))
            pool.wait_ge(sig("v0_stored"), 16)
            pool.wait_ge(sig("pairs_ready"), 1)
            pool.sem_inc(sig("gather_slot_free"), 2)
            with pool.Fori(0, CHUNKS // (2 * HALF)) as i:
                for hf in range(2):
                    pool.wait_ge(sig("gather_slot_free"), 2 * i + (hf + 1))
                    now = bass.ds(2 * HALF * i + HALF * hf, HALF)
                    g.tensor_copy(idx_ring[:, hf, 0, :], src_i[:, now])
                    g.tensor_copy(idx_ring[:, hf, 1, :], pair_i[:, now]).then_inc(sig("idx_copied"), 1)
                    pool.wait_ge(sig("idx_copied"), 2 * i + (hf + 1))
                    part_wait(pool, "pool")
                    for u in range(HALF):
                        g.indirect_dma_start(VG[:, hf, u, :], None, v0_d,
                                             bass.IndirectOffsetOnAxis(ap=idx_ring[:, hf, 0, u:u + 1], axis=0)
                                             ).then_inc(sig(f"gathered{hf}"), 16)
                        g.indirect_dma_start(lg_ring[:, hf, u * H0:(u + 1) * H0], None, logits_d,
                                             bass.IndirectOffsetOnAxis(ap=idx_ring[:, hf, 1, u:u + 1], axis=0)
                                             ).then_inc(sig(f"gathered{hf}"), 16)
            powers(front, pool_chain, NT)
            pool.wait_ge(sig("xn_ready"), 2 * NT)
            g.tensor_tensor(X, X, ROWS[:, 2:3, :].to_broadcast([TILE, NT, D]), ALU.add).then_inc(sig("residual_biased"), 1)
            powers(front, pool_chain, 2 * NT)
            pool.wait_ge(sig("x1_stored"), 16)
            with pool.Fori(0, LAYERS) as i:
                B.turn = i
                pool_loop_chain.turn, pool_loop_chain.per_turn = i, 2 * NT
                for n in (1, 2):
                    powers((sig("var_ready1"), sig("rstd_ready1")), pool_loop_chain, 2 * NT * i + NT * (n - 1))
                    pool.wait_ge(sig("xn_ready1"), 2 * NT * i + NT * n)
                    pool.wait_ge(sig(f"ld_row{n}"), 16 * i + 16)
                    g.tensor_tensor(X, X, ROWS[:, n:n + 1, :].to_broadcast([TILE, NT, D]), ALU.add
                                    ).then_inc(sig("residual_biased1"), 1)
                    if n == 1:
                        for h in range(H1):
                            pool.wait_ge(sig("rinv_ready"), H1 * i + h + 1)
                            part_wait(pool, "pool")
                            for t in range(NT):
                                g.tensor_scalar(P[:, h % 2, t, :], P[:, h % 2, t, :], rinv[:, h % 2, t:t + 1], None,
                                                ALU.mult).then_inc(sig("probs_normalised"), 1)
            assert pool_loop_chain.count == pool_loop_chain.per_turn
            for n in range(3):
                powers((sig("var_ready3"), sig("rstd_ready3")), pool_chain, n * NT)

        @block.scalar
        def _(act):
            a = nc.scalar

            def col(name, k=0, p=128):
                return cols[0:p, COLS[name] + k:COLS[name] + k + 1]

            act.wait_ge(sig("emb_ready"), 1)
            a.activation(EMB, TURNS, ACT.Sin).then_inc(sig("sin_ready"), 1)
            A.wait_filled(act, ("hid",))
            act.wait_ge(sig("sin_ready"), 1)
            A.release(("hid",), a.activation(HIDC, A.view(("hid",), COND)[:, 0:NODES], ACT.Silu, bias=col("f_b1", 0, COND)))
            A.wait_filled(act, ("cond",))
            A.release(("cond",), a.activation(condT[:, :], A.view(("cond",), 128)[:, 0:NODES], ACT.Identity,
                                              bias=col("f_b2")))
            for k in range(FT):
                A.wait_filled(act, ("k", k))
                A.release(("k", k), a.activation(KT[:, k, :], A.view(("k", k), 128)[:, 0:NODES], ACT.Identity,
                                                 bias=col("bk", k)))
            for n in range(NT * H0):
                j, h = divmod(n, H0)
                A.wait_evacuated(act, ("s", j, h))
                if h == 0 and j >= 2:
                    act.wait_ge(sig(f"stage_stored{j % 2}"), 16 * (j // 2))
                a.activation(STAGE[j % 2][:, :, h], TEMP[:, n % 3, :], ACT.Identity, scale=-1.0,
                             bias=negm0[:, n % 3:n % 3 + 1]).then_inc(sig("stage_ready"), 1)
            with act.Fori(0, CHUNKS // (2 * HALF)) as i:
                for hf in range(2):
                    act.wait_ge(sig("edge_logits_ready"), 2 * i + hf + 1)
                    act.wait_ge(sig("msg_slot_free"), 2 * HALF * i + (HALF * hf + 1))
                    a.activation(p_ring[:, hf, :], sum_ring[:, hf, :], ACT.Exp).then_inc(sig("edge_probs_ready"), 1)
            act.wait_ge(sig("lc_half"), 1)
            a.activation(LC, LC, ACT.Ln).then_inc(sig("ln_done"), 1)
            for k in range(0, FT, 2):
                A.wait_filled(act, ("at", k))
                A.release(("at", k), a.activation(YT[:, k, :], A.view(("at", k), 128)[:, 0:NODES], ACT.Copy))
            for f in range(FF0):
                A.wait_filled(act, ("up", f))
                A.release(("up", f), a.activation(HT0[:, f, :], A.view(("up", f), 128)[:, 0:NODES], ACT.Gelu,
                                                  bias=col("b1", f)))

            def evac_columns(key, dst, bias, func=ACT.Identity):
                B.wait_filled(act, key)
                B.release(key, a.activation(dst, B.view(key, 128)[:, 0:NODES], func, bias=bias))

            with act.Fori(0, LAYERS) as i:
                B.turn = i

                def lcol(kind, k, table=cols, base=COLS["layers"]):
                    return table[:, bass.ds(i * (7 * FT) + (base + kind + k), 1)]

                def make_conditioning(n):
                    for k in range(FT):
                        evac_columns(("scale", n, k), SC[:, k, :], lcol((S1B, S2B)[n - 1], k, cols1, 0))
                        evac_columns(("bias", n, k), BI[n][:, k, :], lcol((B1B, B2B)[n - 1], k))

                def exps(h):
                    evac_columns(("k", h), KT[:, h, :], lcol(BK, h))
                    for t in range(NT):
                        B.wait_evacuated(act, ("s", h, t))
                        a.activation(P[:, h % 2, t, :], P[:, h % 2, t, :], ACT.Exp, scale=-1.0,
                                     bias=negm[:, h % 2, t:t + 1], accum_out=psums[:, h % 2, t:t + 1]
                                     ).then_inc(sig("exps_done"), 1)

                def outputs(h):
                    for n in (0, 2):
                        B.wait_filled(act, ("pt", h, n))
                        B.release(("pt", h, n), a.activation(
                            PT[:, h % 2, 1000 * n:1000 * n + 1000].rearrange("p (b c) -> p b c", b=2),
                            B.view(("pt", h, n)).rearrange("p (b c) -> p b c", b=2)[:, :, 0:500], ACT.Copy))
                    B.wait_filled(act, ("av", h))
                    B.release(("av", h), a.activation(OT[:, h, :], B.view(("av", h), 128)[:, 0:NODES], ACT.Copy))

                make_conditioning(1)
                exps(0)
                exps(1)
                outputs(0)
                exps(2)
                outputs(1)
                exps(3)
                outputs(2)
                make_conditioning(2)
                outputs(3)
                for f in range(FT):
                    evac_columns(("m1", f), HT[:, f, :], lcol(MB1, f), ACT.Relu)
            act.wait_ge(sig("lc2_half"), 1)
            a.activation(LC, LC, ACT.Ln).then_inc(sig("ln_done"), 1)
            for k in range(0, FT, 2):
                C.wait_filled(act, ("t", 2, k))
                C.release(("t", 2, k), a.activation(YT[:, k, :], C.view(("t", 2, k), 128)[:, 0:NODES], ACT.Copy))
            C.wait_filled(act, ("hid",))
            C.release(("hid",), a.activation(HID2T, C.view(("hid",), HID2)[:, 0:NODES], ACT.Relu, bias=col("c_b1", 0, HID2)))
            for k in range(0, FT, 2):
                C.wait_filled(act, ("t", 3, k))
                C.release(("t", 3, k), a.activation(YT[:, k, :], C.view(("t", 3, k), 128)[:, 0:NODES], ACT.Copy))
            act.wait_ge(sig("fg_ready"), 1)

            def edge_sums(h):
                C.wait_filled(act, ("g", h))
                if h >= 2:
                    C.wait_filled(act, ("pt", h - 2, 3))
                for t in range(NT):
                    z = a.activation(P[:, h % 2, t, :], C.view(("g", h))[:, 0:NODES], ACT.Identity, bias=fcol[:, t, h:h + 1])
                    if t < NT - 1:
                        z.then_inc(sig("z_ready"), 1)
                    else:
                        C.release(("g", h), z)

            edge_sums(0)
            for h in range(H3):
                if h + 1 < H3:
                    edge_sums(h + 1)
                for t in range(NT):
                    act.wait_ge(sig("leaky_done"), NT * h + t + 1)
                    a.activation(P[:, h % 2, t, :], P[:, h % 2, t, :], ACT.Exp, scale=-1.0, bias=negm[:, h % 2, t:t + 1],
                                 accum_out=psums[:, h % 2, t:t + 1]).then_inc(sig("exps_done3"), 1)
                for n in (0, 2):
                    C.wait_filled(act, ("pt", h, n))
                    C.release(("pt", h, n), a.activation(
                        PT[:, h % 2, 1000 * n:1000 * n + 1000].rearrange("p (b c) -> p b c", b=2),
                        C.view(("pt", h, n)).rearrange("p (b c) -> p b c", b=2)[:, :, 0:500], ACT.Copy))

        @block.vector
        def _(dve):
            v = nc.vector
            MAGIC = 12582912.0
            PI2 = (6.28125, 0.0019350051879882812, 3.0199159819567194e-07)

            def col(name, k=0, p=128):
                return cols[0:p, COLS[name] + k:COLS[name] + k + 1]

            def norm(sems, base, dst, before=None, chain=dve_chain, done=None):
                var_ready, rstd_ready, xn_ready = sems
                for t in range(NT + 1):
                    if t < NT:
                        if before:
                            before(t)
                        chain(dve, v.bn_stats(stats[:, t, :], X[:, t, :]))
                        part_wait(dve, "dve")
                        v.bn_aggr(mv[:, t, :], stats[:, t, :]).then_inc(var_ready, 1)
                    if t >= 1:
                        dve.wait_ge(rstd_ready, base + t)
                        v.tensor_scalar(dst[:, t - 1, :], X[:, t - 1, :], mv[:, t - 1, 0:1], rstd[:, t - 1:t],
                                        ALU.subtract, ALU.mult).then_inc(done or xn_ready, 1)

            front = (sig("var_ready"), sig("rstd_ready"), sig("xn_ready"))
            dve.wait_ge(sig("ld_noise"), 16)
            dve.wait_ge(sig("ld_cols"), 16)
            v.tensor_scalar(cols1[:, :], cols[:, COLS["layers"]:NCOLS], 1.0, None, ALU.add)
            E = 2 * NFREQ
            dve_chain(dve, v.tensor_scalar(PHASE, NOISE, col("freq", 0, E), None, ALU.mult))
            dve_chain(dve, v.tensor_scalar(TURNS, PHASE, 0.15915494309189535, None, ALU.mult))
            dve_chain(dve, v.tensor_scalar(TURNS, TURNS, col("turn", 0, E), None, ALU.add))
            dve_chain(dve, v.tensor_scalar(TURNS, TURNS, MAGIC, None, ALU.add))
            dve_chain(dve, v.tensor_scalar(TURNS, TURNS, MAGIC, None, ALU.subtract))
            for part in PI2:
                dve_chain(dve, v.scalar_tensor_tensor(PHASE, TURNS, -part, PHASE, ALU.mult, ALU.add))
            dve_chain(dve, v.tensor_scalar(PHASE, PHASE, col("angle", 0, E), None, ALU.add))
            v.tensor_scalar(TURNS, PHASE, 3.1415925, -3.1415925, ALU.min, ALU.max).then_inc(sig("emb_ready"), 1)
            dve.wait_ge(sig("ld_idx"), 32)
            v.tensor_copy(src_f[:, :], src_i[:, :])
            dve_chain(dve, v.tensor_copy(dst_f[:, :], dst_i[:, :]))
            dve_chain(dve, v.scalar_tensor_tensor(pair_f[:, :], dst_f[:, :], float(NODES), src_f[:, :], ALU.mult, ALU.add))
            v.tensor_copy(pair_i[:, :], pair_f[:, :]).then_inc(sig("pairs_ready"), 1)
            dve.wait_ge(sig("ld_attr"), 32)
            dve_chain(dve, v.tensor_tensor(ATTR[:, 0, :], ATTR[:, 0, :], ATTR[:, 1, :], ALU.add))
            v.reduce_max(gmax[:, 0:1], ATTR[:, 0, :], AX.X).then_inc(sig("gmax_part"), 1)
            dve.wait_ge(sig("ld_x"), 16)
            norm(front, 0, XN)
            dve.wait_ge(sig("gmax_all"), 1)
            dve_chain(dve, v.tensor_scalar(ATTR[:, 0, :], ATTR[:, 0, :], gmax[:, 1:2], None, ALU.subtract))
            for k in range(FT):
                A.wait_filled(dve, ("t", k))
                A.release(("t", k), v.tensor_scalar(YT[:, k, :], A.view(("t", k), 128)[:, 0:NODES],
                                                    col("ln1_g", k), col("ln1_b", k), ALU.mult, ALU.add))
            for k in range(FT):
                A.wait_filled(dve, ("q", k))
                A.release(("q", k), v.tensor_scalar(QT[:, k, :], A.view(("q", k), 128)[:, 0:NODES],
                                                    col("bq", k), float(D) ** -0.5, ALU.add, ALU.mult))

            def bank_view(r, key, pair):
                return r.view(key).rearrange("p (b c) -> p b c", b=2)[:, 0:len(pair), :]

            def row_bias(r, key, pair, dst, row):
                r.wait_filled(dve, key)
                r.release(key, v.tensor_tensor(dst[:, pair[0]:pair[-1] + 1, :], bank_view(r, key, pair),
                                               row.to_broadcast([TILE, len(pair), D]), ALU.add))

            dve.wait_ge(sig("ld_rows0"), 16)
            for n, pair in enumerate(PAIRS):
                row_bias(A, ("v", n), pair, V, ROWS[:, 0:1, :])
            dve.wait_ge(sig("iota_ready"), 1)
            with dve.Fori(0, CHUNKS // 4) as i:
                for u in range(4):
                    dve.wait_ge(sig("onehot_slot_free"), 4 * i + (u + 1))
                    c = bass.ds(4 * i + u, 1)
                    v.tensor_scalar(OH16[:, 0, u, :], iota16[0:TILE, :], dst_f[:, c], None, ALU.is_equal)
                    v.tensor_scalar(OH16[:, 1, u, :], iota16[0:TILE, :], src_f[:, c], None, ALU.is_equal
                                    ).then_inc(sig("onehot_ready"), 1)
            dve.wait_ge(sig("counts_done"), 1)
            for j in range(NT):
                v.tensor_copy(C2[:, j, 0:512], ps[0:TILE, 512 * j:512 * j + 512])
                at_tail = 2560 + TAIL * j if j < 4 else 3072
                last = v.tensor_copy(C2[:, j, 512:NODES], ps[0:TILE, at_tail:at_tail + TAIL])
            last.then_inc(sig("counts_ready"), 1)
            dve.wait_ge(sig("counts_ready"), 1)
            dve_chain(dve, v.tensor_scalar(MASK, C2, 0.5, -BIG, ALU.is_lt, ALU.mult))
            for n in range(NT * H0):
                j, h = divmod(n, H0)
                A.wait_filled(dve, ("s", j, h))
                if n >= 3:
                    dve.wait_ge(sig("stage_ready"), n - 2)
                A.release(("s", j, h), v.tensor_tensor_reduce(
                    out=TEMP[:, n % 3, :], in0=A.view(("s", j, h))[:, 0:NODES], in1=MASK[:, j, :], scale=-1.0, scalar=3.0e38,
                    op0=ALU.add, op1=ALU.min, accum_out=negm0[:, n % 3:n % 3 + 1]))
            with dve.Fori(0, CHUNKS // (2 * HALF)) as i:
                for hf in range(2):
                    dve.wait_ge(sig(f"gathered{hf}"), 32 * HALF * i + 32 * HALF)
                    now = bass.ds(2 * HALF * H0 * i + HALF * H0 * hf, HALF * H0)
                    v.tensor_tensor(sum_ring[:, hf, :], lg_ring[:, hf, :], ATTR[:, 0, now], ALU.add
                                    ).then_inc(sig("edge_logits_ready"), 1)
                    for u in range(HALF):
                        dve.wait_ge(sig("msg_slot_free"), 2 * HALF * i + (HALF * hf + u + 2))
                        v.tensor_scalar(OH32[:, u, :], iota16[0:TILE, :], dst_f[:, bass.ds(2 * HALF * i + (HALF * hf + u), 1)],
                                        None, ALU.is_equal)
                        if u == 0:
                            dve.wait_ge(sig("edge_probs_ready"), 2 * i + hf + 1)
                        v.tensor_tensor(MSG[:, u, :].rearrange("p (h d) -> p h d", h=H0),
                                        VG[:, hf, u, :].rearrange("p (h d) -> p h d", h=H0),
                                        p_ring[:, hf, u * H0:(u + 1) * H0].unsqueeze(2).to_broadcast([TILE, H0, DH0]),
                                        ALU.mult).then_inc(sig("msg_ready"), 1)
                    dve.wait_ge(sig("msg_ready"), 2 * HALF * i + (HALF * hf + HALF))
                    dve.sem_inc(sig("gather_slot_free"), 1)
            dve.wait_ge(sig("agg_done"), 1)
            dve_chain(dve, v.tensor_scalar(den[:, :, :], ps[0:TILE, 2560:2560 + NT * H0].rearrange("p (j h) -> p j h", j=NT),
                                           1.0e-37, None, ALU.max))
            dve_chain(dve, v.reciprocal(rden[:, :, :], den[:, :, :]))
            for j in range(NT):
                last = v.tensor_tensor(V[:, j, :].rearrange("p (h d) -> p h d", h=H0),
                                       ps[0:TILE, 512 * j:512 * j + 512].rearrange("p (h d) -> p h d", h=H0),
                                       rden[:, j, :].unsqueeze(2).to_broadcast([TILE, H0, DH0]), ALU.mult)
            last.then_inc(sig("agg_ready"), 1)

            def make_log_counts(counts, name):
                dve_chain(dve, v.tensor_scalar(LTMP, counts, 0.5, -BIG, ALU.is_lt, ALU.mult))
                v.tensor_scalar(LC, counts, 1.0, None, ALU.max).then_inc(sig(name), 1)

            for n in range(4):
                A.wait_filled(dve, ("c1", n))
                size = len(TGROUPS[n])
                flat = at(R_LC, NT * NODES, p=TILE)
                if size == 8:
                    last = v.tensor_copy(flat[:, 1000 * n:1000 * n + 1000].rearrange("p (b c) -> p b c", b=2),
                                         A.view(("c1", n)).rearrange("p (b c) -> p b c", b=2)[:, :, 0:500])
                else:
                    last = v.tensor_copy(flat[:, 1000 * n:1000 * n + TILE], A.view(("c1", n))[:, 0:TILE])
                A.release(("c1", n), last)
            A.wait_evacuated(dve, ("c1", 3))
            make_log_counts(LC, "lc_half")
            for k in range(1, FT, 2):
                A.wait_filled(dve, ("at", k))
                A.release(("at", k), v.tensor_copy(YT[:, k, :], A.view(("at", k), 128)[:, 0:NODES]))
            dve.wait_ge(sig("ln_done"), 1)
            dve_chain(dve, v.tensor_tensor(LC, LC, LTMP, ALU.add))
            dve_chain(dve, v.tensor_reduce(has1[:, :], LC, AX.X, ALU.max))
            v.tensor_scalar(has1[:, :], has1[:, :], -0.5 * BIG, None, ALU.is_gt).then_inc(sig("lc_ready"), 1)

            def add_rows(r, name, chain, n_bias):
                def before(t):
                    n = t // 2
                    if t == 2 * n:
                        r.wait_filled(dve, (name, n))
                        pair = PAIRS[n]
                        ins = v.tensor_tensor(X[:, pair[0]:pair[-1] + 1, :], X[:, pair[0]:pair[-1] + 1, :],
                                              bank_view(r, (name, n), pair), ALU.add)
                        r.release((name, n), ins)
                        r.wait_evacuated(dve, (name, n))
                return before

            dve.wait_ge(sig("residual_biased"), 1)
            norm(front, NT, XN, add_rows(A, "o", dve_chain, 0))
            for k in range(FT):
                A.wait_filled(dve, ("t2", k))
                A.release(("t2", k), v.tensor_scalar(YT[:, k, :], A.view(("t2", k), 128)[:, 0:NODES],
                                                     col("ln2_g", k), col("ln2_b", k), ALU.mult, ALU.add))
            dve.wait_ge(sig("residual_biased"), 2)
            dve.wait_ge(sig("ld_x0"), 16)
            add_down = add_rows(A, "down", dve_chain, 1)

            def block0_end(t):
                add_down(t)
                dve_chain(dve, v.tensor_tensor(X[:, t, :], X[:, t, :], XIN0[:, t, :], ALU.add))

            norm(front, 2 * NT, X, block0_end, done=sig("x1_ready"))
            dve.wait_ge(sig("x1_ready"), NT)

            with dve.Fori(0, LAYERS) as i:
                B.turn = i
                dve_loop_chain.turn, dve_loop_chain.per_turn = i, 2 * NT + 2 * FT + H1

                def lcol(kind, k):
                    return cols[:, bass.ds(i * (7 * FT) + (COLS["layers"] + kind + k), 1)]

                mid = (sig("var_ready1"), sig("rstd_ready1"), sig("xn_ready1"))

                def apply_conditioning(n):
                    for k in range(FT):
                        B.wait_evacuated(dve, ("scale", n, k))
                        B.wait_evacuated(dve, ("bias", n, k))
                        B.wait_filled(dve, ("t", n, k))
                        dve_loop_chain(dve, v.tensor_tensor(YT[:, k, :], B.view(("t", n, k), 128)[:, 0:NODES], SC[:, k, :],
                                                            ALU.mult))
                        B.release(("t", n, k), v.tensor_tensor(YT[:, k, :], YT[:, k, :], BI[n][:, k, :], ALU.add))

                def queries(h):
                    B.wait_filled(dve, ("q", h))
                    B.release(("q", h), v.tensor_scalar(QT[:, h, :], B.view(("q", h), 128)[:, 0:NODES], lcol(BQ, h),
                                                        float(DH1) ** -0.5, ALU.add, ALU.mult))

                def masked(h):
                    if h >= 2:
                        B.wait_filled(dve, ("pt", h - 2, 3))
                    for t in range(NT):
                        B.wait_filled(dve, ("s", h, t))
                        part_wait(dve, "dve")
                        B.release(("s", h, t), v.tensor_tensor_reduce(
                            out=P[:, h % 2, t, :], in0=B.view(("s", h, t))[:, 0:NODES], in1=LC[:, t, :], scale=-1.0,
                            scalar=3.0e38, op0=ALU.add, op1=ALU.min, accum_out=negm[:, h % 2, t:t + 1]))

                def inverse_sums(h):
                    dve.wait_ge(sig("exps_done"), H1 * NT * i + NT * (h + 1))
                    dve_loop_chain(dve, v.reciprocal(rinv[:, h % 2, :], psums[:, h % 2, :]))
                    v.tensor_tensor(rinv[:, h % 2, :], rinv[:, h % 2, :], has1[:, :], ALU.mult).then_inc(sig("rinv_ready"), 1)

                def transposed(h):
                    B.wait_filled(dve, ("pt", h, 1))
                    B.release(("pt", h, 1), v.tensor_copy(
                        PT[:, h % 2, 1000:2000].rearrange("p (b c) -> p b c", b=2),
                        B.view(("pt", h, 1)).rearrange("p (b c) -> p b c", b=2)[:, :, 0:500]))
                    B.wait_filled(dve, ("pt", h, 3))
                    B.release(("pt", h, 3), v.tensor_copy(PT[:, h % 2, 3000:3125], B.view(("pt", h, 3))[:, 0:TILE]))

                norm(mid, 2 * NT * i, XN, chain=dve_loop_chain)
                apply_conditioning(1)
                queries(0)
                masked(0)
                queries(1)
                inverse_sums(0)
                masked(1)
                dve.wait_ge(sig("ld_row0"), 16 * i + 16)
                for n, pair in enumerate(PAIRS):
                    row_bias(B, ("v", n), pair, V, ROWS[:, 0:1, :])
                inverse_sums(1)
                transposed(0)
                queries(2)
                masked(2)
                transposed(1)
                inverse_sums(2)
                queries(3)
                masked(3)
                transposed(2)
                inverse_sums(3)
                transposed(3)
                dve.wait_ge(sig("residual_biased1"), 2 * i + 1)
                norm(mid, 2 * NT * i + NT, XN, add_rows(B, "o", dve_loop_chain, 0), chain=dve_loop_chain)
                apply_conditioning(2)
                dve.wait_ge(sig("residual_biased1"), 2 * i + 2)
                for n, pair in enumerate(PAIRS):
                    B.wait_filled(dve, ("m2", n))
                    B.release(("m2", n), v.tensor_tensor(X[:, pair[0]:pair[-1] + 1, :], X[:, pair[0]:pair[-1] + 1, :],
                                                         bank_view(B, ("m2", n), pair), ALU.add))
                for n in range(3):
                    B.wait_evacuated(dve, ("m2", n))
            assert dve_loop_chain.count == dve_loop_chain.per_turn, dve_loop_chain.count

            make_log_counts(C2, "lc2_half")
            back = (sig("var_ready3"), sig("rstd_ready3"), sig("xn_ready3"))
            dve.wait_ge(sig("ld_x1"), 16)

            def block1_end(t):
                dve_chain(dve, v.tensor_tensor(X[:, t, :], X[:, t, :], XIN[:, t, :], ALU.add))

            norm(back, 0, X, block1_end)
            dve.wait_ge(sig("ln_done"), 2)
            dve_chain(dve, v.tensor_tensor(LC, LC, LTMP, ALU.add))
            dve_chain(dve, v.tensor_reduce(has2[:, :], LC, AX.X, ALU.max))
            dve_chain(dve, v.tensor_scalar(has2[:, :], has2[:, :], -0.5 * BIG, None, ALU.is_gt))
            for k in range(1, FT, 2):
                C.wait_filled(dve, ("t", 2, k))
                C.release(("t", 2, k), v.tensor_copy(YT[:, k, :], C.view(("t", 2, k), 128)[:, 0:NODES]))
            dve.wait_ge(sig("ld_rows3"), 16)
            for n, pair in enumerate(PAIRS):
                row_bias(C, ("h", n), pair, V, ROWS[:, 0:1, :])
            for n in range(3):
                C.wait_evacuated(dve, ("h", n))

            def block2_end(t):
                n = t // 2
                if t == 2 * n:
                    pair = PAIRS[n]
                    tiles = slice(pair[0], pair[-1] + 1)
                    dve_chain(dve, v.tensor_tensor(X[:, tiles, :], X[:, tiles, :], V[:, tiles, :], ALU.add))
                    C.wait_filled(dve, ("agg", n))
                    C.release(("agg", n), v.tensor_tensor(X[:, tiles, :], X[:, tiles, :], bank_view(C, ("agg", n), pair), ALU.add))
                    C.wait_evacuated(dve, ("agg", n))

            norm(back, NT, X, block2_end)
            for k in range(1, FT, 2):
                C.wait_filled(dve, ("t", 3, k))
                C.release(("t", 3, k), v.tensor_copy(YT[:, k, :], C.view(("t", 3, k), 128)[:, 0:NODES]))
            dve.wait_ge(sig("ld_aw"), 16)
            for n, pair in enumerate(PAIRS):
                row_bias(C, ("wx", n), pair, V, AW[:, 2:3, :])
            for n in range(3):
                C.wait_evacuated(dve, ("wx", n))
            dve.wait_ge(sig("ld_c"), 48)
            for t in range(NT):
                for half, dst in ((0, fcol), (1, gcol)):
                    dve_chain(dve, v.tensor_tensor(PROD[:, half, :], V[:, t, :], AW[:, half, :], ALU.mult))
                    last = v.tensor_reduce(dst[:, t, :], PROD[:, half, :].rearrange("p (h d) -> p h d", h=H3), AX.X, ALU.add)
            dve_chain(dve, last)
            v.tensor_tensor(fcol[:, :, :], fcol[:, :, :], ab[:, :].unsqueeze(1).to_broadcast([TILE, NT, H3]), ALU.add
                            ).then_inc(sig("fg_ready"), 1)

            def spread_g(h):
                if h >= 1:
                    C.wait_filled(dve, ("g", h - 1))
                v.tensor_copy(g_bc[:, :, :], gcol[:, :, h:h + 1].to_broadcast([TILE, NT, TILE])).then_inc(sig("g_spread"), 1)

            spread_g(0)
            spread_g(1)
            for h in range(H3):
                for t in range(NT):
                    if t < NT - 1:
                        dve.wait_ge(sig("z_ready"), (NT - 1) * h + t + 1)
                    else:
                        C.wait_evacuated(dve, ("g", h))
                    z = P[:, h % 2, t, :]
                    dve_chain(dve, v.scalar_tensor_tensor(z, z, 0.2, z, ALU.mult, ALU.max))
                    v.tensor_tensor_reduce(out=z, in0=z, in1=LC[:, t, :], scale=-1.0, scalar=3.0e38, op0=ALU.add,
                                           op1=ALU.min, accum_out=negm[:, h % 2, t:t + 1]).then_inc(sig("leaky_done"), 1)
                if h + 2 < H3:
                    spread_g(h + 2)
                dve.wait_ge(sig("exps_done3"), NT * (h + 1))
                dve_chain(dve, v.reciprocal(rinv[:, h % 2, :], psums[:, h % 2, :]))
                dve_chain(dve, v.tensor_tensor(rinv[:, h % 2, :], rinv[:, h % 2, :], has2[:, :], ALU.mult))
                C.wait_filled(dve, ("pt", h, 1))
                C.release(("pt", h, 1), v.tensor_copy(
                    PT[:, h % 2, 1000:2000].rearrange("p (b c) -> p b c", b=2),
                    C.view(("pt", h, 1)).rearrange("p (b c) -> p b c", b=2)[:, :, 0:500]))
                C.wait_filled(dve, ("pt", h, 3))
                C.release(("pt", h, 3), v.tensor_copy(PT[:, h % 2, 3000:3125], C.view(("pt", h, 3))[:, 0:TILE]))
                C.wait_filled(dve, ("av", h))
                C.release(("av", h), v.tensor_tensor(
                    OUT3[:, :, h * DH3:(h + 1) * DH3], C.view(("av", h))[:, 0:NT * DH3].rearrange("p (t d) -> p t d", t=NT),
                    rinv[:, h % 2, :].unsqueeze(2).to_broadcast([TILE, NT, DH3]), ALU.mult))
            C.wait_evacuated(dve, ("av", H3 - 1))

            def block3_end(t):
                dve_chain(dve, v.tensor_tensor(X[:, t, :], X[:, t, :], OUT3[:, t, :], ALU.add))

            norm(back, 2 * NT, X, block3_end, done=sig("out_ready"))

        @block.tensor
        def _(pe):
            mm = nc.tensor.matmul

            def wide(out_view, pairs, start=True):
                for lo, hi in ((0, 512), (512, NODES)):
                    for n, (w, r) in enumerate(pairs):
                        last = mm(out_view[:, lo:hi], w, r[:, lo:hi], start=n == 0, stop=n == len(pairs) - 1)
                return last

            def columns(r, key, weight, moving, tiles=FT, p=128):
                r.claim(pe, key)
                r.fill(wide(r.view(key, p), [(weight(k), moving[:, k, :]) for k in range(tiles)]))

            def rows(r, key, pair, moving, weight, tiles=FT):
                r.claim(pe, key)
                for b, t in enumerate(pair):
                    for k in range(tiles):
                        last = mm(r.view(key)[:, 512 * b:512 * b + 512], moving[:, k, TILE * t:TILE * (t + 1)], weight[:, k, :],
                                  start=k == 0, stop=k == tiles - 1)
                r.fill(last)

            def tile_columns(r, key, src, k):
                r.claim(pe, key)
                for t in range(NT):
                    place = r.view(key, 128)
                    if t < 4:
                        last = nc.tensor.transpose(place[:, TILE * t:TILE * (t + 1)], src[:, t, 128 * k:128 * (k + 1)],
                                                   ident[0:TILE, 0:TILE])
                    else:
                        cut = 512 - 4 * TILE
                        mm(place[:, 500:512], src[:, t, 128 * k:128 * (k + 1)], ident[0:TILE, 0:cut], start=True, stop=True)
                        last = mm(place[:, 512:NODES], src[:, t, 128 * k:128 * (k + 1)], ident[0:TILE, cut:TILE],
                                  start=True, stop=True)
                r.fill(last)

            def turn_tiles(r, key, group, tile):
                r.claim(pe, key)
                for m, f in enumerate(group):
                    j, t = divmod(f, NT)
                    o = 512 * (m // 4) + TILE * (m % 4)
                    last = nc.tensor.transpose(r.view(key)[:, o:o + TILE], tile(t, j), ident[0:TILE, 0:TILE])
                r.fill(last)

            pe.sem_inc(sig("onehot_slot_free"), 4)
            pe.sem_inc(sig("msg_slot_free"), HALF + 1)
            B.open(pe)
            pe.wait_ge(sig("ld_fw"), 32)
            pe.wait_ge(sig("sin_ready"), 1)
            A.claim(pe, ("hid",))
            A.fill(wide(A.view(("hid",), COND), [(fw1[:, :], EMB)]))
            A.wait_evacuated(pe, ("hid",))
            A.claim(pe, ("cond",))
            A.fill(wide(A.view(("cond",), 128), [(fw2[:, :], HIDC)]))
            pe.wait_ge(sig("ident_ready"), 1)
            pe.wait_ge(sig("xn_ready"), NT)
            for k in range(FT):
                tile_columns(A, ("t", k), XN, k)
            for k in range(FT):
                A.wait_evacuated(pe, ("t", k))
            pe.wait_ge(sig("ld_wqkv"), 16)
            for k in range(FT):
                columns(A, ("q", k), lambda c: WQKV[:, c, 128 * k:128 * (k + 1)], YT)
                columns(A, ("k", k), lambda c: WQKV[:, c, D + 128 * k:D + 128 * (k + 1)], YT)
            for n, pair in enumerate(PAIRS):
                rows(A, ("v", n), pair, YT, WQKV[:, :, 2 * D:3 * D])
            for key in (("k", FT - 1), ("v", 0), ("v", 1), ("v", 2)):
                A.wait_evacuated(pe, key)
            pe.wait_ge(sig("zeros_ready"), 1)

            def count_place(j):
                return ((512 * j, 0, 512), (2560 + TAIL * j if j < 4 else 3072, 512, NODES))

            for b in range(7):
                mm(ps[0:TILE, 512 * b:512 * b + 512], zero16[:, 0:TILE], zero16[:, :], start=True, stop=True)
            with pe.Fori(0, CHUNKS // 4) as i:
                for u in range(4):
                    pe.wait_ge(sig("onehot_ready"), 4 * i + (u + 1))
                    for j in range(NT):
                        for o, lo, hi in count_place(j):
                            last = mm(ps[0:TILE, o:o + hi - lo], OH16[:, 0, u, TILE * j:TILE * (j + 1)], OH16[:, 1, u, lo:hi],
                                      start=False, stop=True, skip_group_check=True)
                    last.then_inc(sig("onehot_slot_free"), 1)
            mm(ps[0:TILE, 3072:3584], zero16[:, 0:TILE], zero16[:, :], start=False, stop=True,
               skip_group_check=True).then_inc(sig("counts_done"), 1)
            pe.wait_ge(sig("counts_ready"), 1)
            for j in range(NT):
                for h in range(H0):
                    part = slice(DH0 * (h % 2), DH0 * (h % 2) + DH0)
                    key = ("s", j, h)
                    A.claim(pe, key)
                    A.fill(wide(A.view(key), [(KT[part, h // 2, TILE * j:TILE * (j + 1)], QT[part, h // 2, :])]))
            for h in range(H0 - 4, H0):
                A.wait_evacuated(pe, ("s", NT - 1, h))
            for b in range(6):
                mm(ps[0:TILE, 512 * b:512 * b + 512], zero32[:, 0:TILE], zero32[:, :], start=True, stop=True)
            with pe.Fori(0, CHUNKS // (2 * HALF)) as i:
                for hf in range(2):
                    for u in range(HALF):
                        pe.wait_ge(sig("msg_ready"), 2 * HALF * i + (HALF * hf + u + 1))
                        for j in range(NT):
                            onehot = OH32[:, u, TILE * j:TILE * (j + 1)]
                            mm(ps[0:TILE, 512 * j:512 * j + 512], onehot, MSG[:, u, :], start=False, stop=True,
                               skip_group_check=True)
                            last = mm(ps[0:TILE, 2560 + H0 * j:2560 + H0 * (j + 1)], onehot,
                                      p_ring[:, hf, u * H0:(u + 1) * H0], start=False, stop=True, skip_group_check=True)
                        last.then_inc(sig("msg_slot_free"), 1)
            mm(ps[0:TILE, 2560:3072], zero32[:, 0:TILE], zero32[:, :], start=False, stop=True,
               skip_group_check=True).then_inc(sig("agg_done"), 1)
            pe.wait_ge(sig("agg_ready"), 1)
            for n in range(4):
                turn_tiles(A, ("c1", n), TGROUPS[n], lambda t, j: C2[:, t, TILE * j:TILE * (j + 1)])
            for k in range(FT):
                tile_columns(A, ("at", k), V, k)
            for k in range(FT):
                A.wait_evacuated(pe, ("at", k))
            pe.wait_ge(sig("ld_wo0"), 16)
            for n, pair in enumerate(PAIRS):
                rows(A, ("o", n), pair, YT, WO0)
            pe.wait_ge(sig("xn_ready"), 2 * NT)
            for k in range(FT):
                tile_columns(A, ("t2", k), XN, k)
            for k in range(FT):
                A.wait_evacuated(pe, ("t2", k))
            pe.wait_ge(sig("ld_wup0"), 16)
            for f in range(FF0):
                columns(A, ("up", f), lambda c: WUP0[:, c, 128 * f:128 * (f + 1)], YT)
            for f in range(FF0 - 4, FF0):
                A.wait_evacuated(pe, ("up", f))
            pe.wait_ge(sig("ld_wdown0"), 16)
            for n, pair in enumerate(PAIRS):
                rows(A, ("down", n), pair, HT0, WDN0, FF0)
            for n in range(3):
                A.wait_evacuated(pe, ("down", n))

            def attend_head(r, h):
                for n in range(4):
                    turn_tiles(r, ("pt", h, n), TGROUPS[n], lambda t, j: P[:, h % 2, t, TILE * j:TILE * (j + 1)])
                for n in range(4):
                    r.wait_evacuated(pe, ("pt", h, n))

            with pe.Fori(0, LAYERS) as i:
                B.turn = i

                def make_conditioning(n):
                    for k in range(FT):
                        for q, name in ((2 * n - 2, "scale"), (2 * n - 1, "bias")):
                            key = (name, n, k)
                            B.claim(pe, key)
                            B.fill(wide(B.view(key, 128), [(condw[32 * q:32 * q + COND, 128 * k:128 * (k + 1)],
                                                           condT[32 * q:32 * q + COND, :])]))

                def arrived(name):
                    pe.wait_ge(sig("ld_" + name), 16 * i + 16)

                def make_scores(h):
                    columns(B, ("q", h), lambda c: WQ[:, c, 128 * h:128 * (h + 1)], YT)
                    columns(B, ("k", h), lambda c: WK[:, c, 128 * h:128 * (h + 1)], YT)
                    B.wait_evacuated(pe, ("q", h))
                    B.wait_evacuated(pe, ("k", h))
                    for t in range(NT):
                        key = ("s", h, t)
                        B.claim(pe, key)
                        B.fill(wide(B.view(key), [(QT[:, h, TILE * t:TILE * (t + 1)], KT[:, h, :])]))

                def make_output(h):
                    pe.wait_ge(sig("probs_normalised"), H1 * NT * i + NT * (h + 1))
                    attend_head(B, h)
                    key = ("av", h)
                    B.claim(pe, key)
                    B.fill(wide(B.view(key, 128), [(V[:, j, 128 * h:128 * (h + 1)], PT[:, h % 2, NODES * j:NODES * (j + 1)])
                                                   for j in range(NT)]))

                pe.wait_ge(sig("ld_condw"), 64 * i + 64)
                make_conditioning(1)
                pe.wait_ge(sig("xn_ready1"), 2 * NT * i + NT)
                for k in range(FT):
                    tile_columns(B, ("t", 1, k), XN, k)
                for k in range(FT):
                    B.wait_evacuated(pe, ("t", 1, k))
                arrived("wq")
                arrived("wk")
                make_scores(0)
                make_scores(1)
                arrived("wv")
                for n, pair in enumerate(PAIRS):
                    rows(B, ("v", n), pair, YT, WV)
                for n in range(3):
                    B.wait_evacuated(pe, ("v", n))
                make_output(0)
                make_scores(2)
                make_output(1)
                make_scores(3)
                make_output(2)
                make_conditioning(2)
                make_output(3)
                for h in range(H1):
                    B.wait_evacuated(pe, ("av", h))
                arrived("wo")
                for n, pair in enumerate(PAIRS):
                    rows(B, ("o", n), pair, OT, WO)
                pe.wait_ge(sig("xn_ready1"), 2 * NT * i + 2 * NT)
                for k in range(FT):
                    tile_columns(B, ("t", 2, k), XN, k)
                for k in range(FT):
                    B.wait_evacuated(pe, ("t", 2, k))
                arrived("m1")
                for f in range(FT):
                    columns(B, ("m1", f), lambda c: M1[:, c, 128 * f:128 * (f + 1)], YT)
                for f in range(FT):
                    B.wait_evacuated(pe, ("m1", f))
                arrived("m2")
                for n, pair in enumerate(PAIRS):
                    rows(B, ("m2", n), pair, HT, M2)
            B.turn = LAYERS - 1
            for n in range(3):
                B.wait_evacuated(pe, ("m2", n))
            pe.wait_ge(sig("xn_ready3"), NT)
            for k in range(FT):
                tile_columns(C, ("t", 2, k), X, k)
            for k in range(FT):
                C.wait_evacuated(pe, ("t", 2, k))
            pe.wait_ge(sig("ld_c"), 48)
            columns(C, ("hid",), lambda c: cw1[:, c, :], YT, p=HID2)
            C.wait_evacuated(pe, ("hid",))
            for n, pair in enumerate(PAIRS):
                rows(C, ("h", n), pair, HID2T.unsqueeze(1), cw2[:, :].unsqueeze(1), 1)
            for n in range(3):
                C.wait_evacuated(pe, ("h", n))
            for n, pair in enumerate(PAIRS):
                rows(C, ("agg", n), pair, C2, V, NT)
            pe.wait_ge(sig("xn_ready3"), 2 * NT)
            for k in range(FT):
                tile_columns(C, ("t", 3, k), X, k)
            for k in range(FT):
                C.wait_evacuated(pe, ("t", 3, k))
            pe.wait_ge(sig("ld_ws3"), 16)
            for n, pair in enumerate(PAIRS):
                rows(C, ("wx", n), pair, YT, WS3)
            for n in range(3):
                C.wait_evacuated(pe, ("wx", n))

            def g_rows(h):
                key = ("g", h)
                C.claim(pe, key)
                pe.wait_ge(sig("g_spread"), h + 1)
                place = C.view(key)
                for t in range(NT):
                    if t < 4:
                        last = mm(place[:, TILE * t:TILE * (t + 1)], g_bc[:, t, :], ident[0:TILE, 0:TILE], start=True, stop=True)
                    else:
                        cut = 512 - 4 * TILE
                        mm(place[:, 500:512], g_bc[:, t, :], ident[0:TILE, 0:cut], start=True, stop=True)
                        last = mm(place[:, 512:NODES], g_bc[:, t, :], ident[0:TILE, cut:TILE], start=True, stop=True)
                C.fill(last)

            g_rows(0)
            for h in range(H3):
                if h + 1 < H3:
                    g_rows(h + 1)
                pe.wait_ge(sig("exps_done3"), NT * (h + 1))
                attend_head(C, h)
                key = ("av", h)
                C.claim(pe, key)
                for t in range(NT):
                    for j in range(NT):
                        last = mm(C.view(key)[:, DH3 * t:DH3 * (t + 1)],
                                  PT[:, h % 2, NODES * j + TILE * t:NODES * j + TILE * (t + 1)],
                                  V[:, j, DH3 * h:DH3 * (h + 1)], start=j == 0, stop=j == NT - 1)
                C.fill(last)


def kernel(**inputs):
    import numpy as np
    import concourse.bacc as bacc
    from concourse.bass_utils import run_bass_kernel_spmd

    g = {k: np.asarray(v) for k, v in inputs.items()}

    def cols_of(vec):
        vec = np.asarray(vec, np.float32).reshape(-1)
        n = -(-vec.size // 128)
        return np.concatenate([vec, np.zeros(n * 128 - vec.size, np.float32)]).reshape(n, 128).T

    L0, L1, L2, L3 = ({k[7:]: v for k, v in g.items() if k.startswith(f"L{b}_gnn_")} for b in range(4))
    pad = np.zeros(32 - COND, np.float32)
    freq = np.arange(1, NFREQ + 1, dtype=np.float32) * np.float32(2.0 * np.pi / 16)
    zeros, ones = np.zeros(NFREQ, np.float32), np.ones(NFREQ, np.float32)
    parts = [cols_of(L0[k]) for k in ("ln1_g", "ln1_b", "ln2_g", "ln2_b")]
    parts += [cols_of(L0["bqkv"][:D]), cols_of(L0["bqkv"][D:2 * D]), cols_of(L0["b1"])]
    parts += [cols_of(L1["f_b1"]), cols_of(np.tile(np.concatenate([L1["f_b2"], pad]), 4)), cols_of(L2["b1"])]
    parts += [cols_of(np.concatenate([freq, freq])), cols_of(np.concatenate([zeros, ones * np.float32(0.25)])),
              cols_of(np.concatenate([zeros, ones * np.float32(np.pi / 2)]))]
    for layer in range(LAYERS):
        parts += [cols_of(L1[k][layer]) for k in ("s1_b", "b1_b", "bq", "bk", "s2_b", "b2_b", "m_b1")]
    cols = np.concatenate(parts, axis=1)
    f_w2 = np.tile(np.concatenate([L1["f_w2"], np.zeros((COND, 32 - COND), np.float32)], axis=1), (1, 4))

    def edges(a):
        return a.reshape(CHUNKS, TILE, -1).transpose(1, 0, 2).reshape(TILE, -1)

    arrays = dict(
        x=g["x"], src_t=edges(g["src"]), dst_t=edges(g["dst"]), attr_a=edges(g["edge_attr_8"]),
        attr_b=edges(g["edge_attr_8_n2"]), noise=g["node_vec1"], cols_d=cols,
        w_qkv=L0["Wqkv"], w_o0=L0["Wo"], w_up0=L0["W1"], w_down0=L0["W2"],
        rows0=np.stack([L0["bqkv"][2 * D:], L0["bo"], L0["b2"]]),
        f_w1=L1["f_w1"], f_w2=f_w2, cond_w=np.stack([L1[k] for k in ("s1_w", "b1_w", "s2_w", "b2_w")]),
        wq=L1["wq"], wk=L1["wk"], wv=L1["wv"], wo=L1["wo"], m_w1=L1["m_w1"], m_w2=L1["m_w2"],
        rows1=np.stack([L1["bv"], L1["bo"], L1["m_b2"]]),
        c_w1=L2["W1"], c_w2=L2["W2"], c_b2=L2["b2"],
        ws3=L3["Ws"].transpose(1, 0, 2).reshape(D, H3 * DH3),
        rows3=np.stack([L3["a_w"][:, :DH3].reshape(-1), L3["a_w"][:, DH3:].reshape(-1), L3["Wb"].reshape(-1)]),
        ab3=L3["a_b"],
    )
    nc = bacc.Bacc("TRN2", target_bir_lowering=False, num_devices=1)
    args = {}
    for name, a in arrays.items():
        arrays[name] = a = np.ascontiguousarray(a)
        args[name] = nc.dram_tensor("in_" + name, a.shape, mybir.dt.from_np(a.dtype), kind="ExternalInput").ap()
    out = nc.dram_tensor("out", (NODES, D), mybir.dt.float32, kind="ExternalOutput").ap()
    build(nc, **args, out=out)
    ran = run_bass_kernel_spmd(nc, [{"in_" + n: a for n, a in arrays.items()}], core_ids=[0])
    return ran.results[0]["out"]
```

```python
import concourse.bass as bass
from concourse import mybir
from contextlib import ExitStack

NODES, EDGES, D = 625, 10000, 512
TILE = 125
NT = NODES // TILE
CHUNKS = EDGES // TILE
FT = D // 128
DH0, H0 = 64, 8
FF0 = 4 * D // 128
LAYERS, H1, DH1 = 4, 4, 128
COND, NFREQ = 16, 32
HID2 = 64
H3, DH3 = 8, 64
STACK = 6 * COND
GROUPS = CHUNKS // 4
EPS = 1e-5
BIG = 1.0e30
HALF = 4
HALF_W = 314
W = 2 * HALF_W
PAD = W - NODES

COLS = {}
_n = 0
for _name, _width in (("ln1_g", FT), ("ln1_b", FT), ("ln2_g", FT), ("ln2_b", FT), ("bq", FT), ("bk", FT), ("b1", FF0),
                      ("f_b1", 1), ("f_b2", 1), ("c_b1", 1), ("freq", 1), ("turn", 1), ("angle", 1), ("part_c", 2), ("part_w", 2),
                      ("layers", LAYERS * 7 * FT)):
    COLS[_name] = _n
    _n += _width
NCOLS = _n
S1B, B1B, BQ, BK, S2B, B2B, MB1 = (FT * k for k in range(7))


class PsumRing:

    def __init__(self, ps, filled, evacuated, keys, opened=0):
        self.ps, self.filled, self.evacuated = ps, filled, evacuated
        self.order = {k: n for n, k in enumerate(keys)}
        self.total = len(self.order)
        self.turn = None
        self.opened = opened

    def view(self, key, p=TILE, p0=0):
        s = self.order[key] % 4
        return self.ps[p0:p0 + p, 1024 * s:1024 * s + 1024]

    def halves(self, key, p=TILE, p0=0):
        return self.view(key, p, p0).rearrange("p (b c) -> p b c", b=2)[:, :, 0:HALF_W]

    def blocks(self, key, n, p=TILE):
        return self.view(key, p).rearrange("p (b c) -> p b c", c=128)[:, 0:n, 0:TILE]

    def uses(self, s):
        return (self.total - s + 3) // 4

    def _value(self, local, per_turn):
        return local if self.turn is None else self.turn * per_turn + local

    def open(self, pe):
        for s in range(4):
            pe.sem_inc(self.evacuated[s], self.opened)

    def claim(self, pe, key):
        n = self.order[key]
        if n >= 4 or self.turn is not None:
            pe.wait_ge(self.evacuated[n % 4], self._value(n // 4 + self.opened, self.uses(n % 4)))

    def fill(self, matmul):
        matmul.then_inc(self.filled, 1)

    def wait_filled(self, eng, key):
        eng.wait_ge(self.filled, self._value(self.order[key] + 1, self.total))

    def release(self, key, instruction):
        instruction.then_inc(self.evacuated[self.order[key] % 4], 1)

    def wait_evacuated(self, eng, key):
        n = self.order[key]
        eng.wait_ge(self.evacuated[n % 4], self._value(n // 4 + 1 + self.opened, self.uses(n % 4)))


class Chain:

    def __init__(self, semaphore):
        self.semaphore, self.count, self.turn, self.per_turn = semaphore, 0, None, 0

    def __call__(self, eng, instruction):
        instruction.then_inc(self.semaphore, 1)
        self.count += 1
        eng.wait_ge(self.semaphore, self.count if self.turn is None else self.turn * self.per_turn + self.count)


def build(nc, x, src_t, dst_t, attr_a, attr_b, noise, cols_d,
          w_qkv, w_o0, w_up0, w_down0, rows0,
          f_w1, f_w2, cond_w, wq, wk, wv, wo, m_w1, m_w2, rows1,
          c_w1, c_w2, c_b2, ws3, rows3, ab3, out):
    f32, bf16, f16 = mybir.dt.float32, mybir.dt.bfloat16, mybir.dt.float16
    i32, u32 = mybir.dt.int32, mybir.dt.uint32
    ALU, ACT, AX = mybir.AluOpType, mybir.ActivationFunctionType, mybir.AxisListType

    logits_d = nc.dram_tensor("logits_scratch", (NODES * NODES, H0), f32, kind="Internal").ap()
    v0_d = nc.dram_tensor("value_scratch", (NODES, D), f32, kind="Internal").ap()
    c2_d = nc.dram_tensor("counts_scratch", (TILE, NT * W), f32, kind="Internal").ap()
    x1_d = nc.dram_tensor("block_input_scratch", (NODES, D), f32, kind="Internal").ap()

    with ExitStack() as ctx:
        def sem(name):
            return ctx.enter_context(nc.semaphore(name))

        def sbuf(name, shape, dt=f32):
            return ctx.enter_context(nc.sbuf_tensor(name, shape, dt))

        ARENA_WORDS = 48030
        arena = sbuf("arena", [128, ARENA_WORDS])
        arena_at = nc.sbuf_base - 4 * ARENA_WORDS

        def over(name, offset, shape, dt):
            return nc.alloc_sbuf_tensor_at(name, shape, dt, offset=arena_at + 4 * offset)

        def at(offset, *dims, p=128, p0=0):
            size = 1
            for d in dims:
                size *= d
            flat = arena[p0:p0 + p, offset:offset + size]
            if len(dims) == 1:
                return flat
            names = "abcd"[:len(dims)]
            return flat.rearrange("p (" + " ".join(names) + ") -> p " + " ".join(names), **dict(zip(names, dims)))

        def halves(row):
            return row.rearrange("p (b c) -> p b c", b=2)

        def tiled(row):
            return row[:, 0:row.shape[1] // TILE * TILE].rearrange("p (b c) -> p b c", c=TILE)

        R_X, R_Y, R_V, R_Q, R_K, R_O = (2560 * k for k in range(6))
        R_P = 15360
        R_PT = R_P + 2 * NT * W
        R_LC = R_PT + 2 * NT * W
        R_C = R_LC + NT * W
        R_W = R_C + NT * W
        R_B = R_W + 6 * FT * D

        X = at(R_X, NT, D, p=TILE)
        YT = at(R_Y, FT, W)
        V = at(R_V, NT, D, p=TILE)
        XN = V
        QT = at(R_Q, FT, W)
        KT = at(R_K, FT, W)
        OT = at(R_O, FT, W)
        P = at(R_P, 2, NT, W, p=TILE)
        PT = at(R_PT, 2, NT, W, p=TILE)
        LC = at(R_LC, NT, W, p=TILE)
        C2 = at(R_C, NT, W, p=TILE)
        ROWS = at(R_B, 3, D, p=TILE)
        WQKV = at(R_P, FT, 3 * D)
        STAGE = [at(R_P + 6144, NODES, H0, p=TILE), at(R_W, NODES, H0, p=TILE)]
        MASK = at(R_W + 5000, NT, W, p=TILE)
        WO0 = at(R_W + 8192, FT, D)
        TEMP = at(R_W + 10240, 3, W, p=TILE)
        ATTR = at(R_LC, 2, CHUNKS * H0, p=TILE)
        OH16 = at(R_LC + 1280, 8 * W, p=TILE).bitcast(bf16).rearrange("p (k r n) -> p k r n", k=2, r=2 * HALF)
        f32r = mybir.dt.float32r
        OHR = over("onehot_r", R_Q, [TILE, 2 * HALF, W], f32r)
        MSGR = over("messages_r", R_P + 2 * HALF * D, [TILE, 2 * HALF, 2, D], f32r)
        PR = over("edge_probs_r", R_O, [TILE, 2, HALF, 2, H0], f32r)
        FLAGS = at(R_K, NT, CHUNKS, p=TILE)
        VG = at(R_P, 2, HALF, D, p=TILE)
        HT0 = at(R_V, FF0, W)
        WUP0 = at(R_P, FT, 4 * D)
        WDN0 = at(R_W, FF0, D)
        M1, M2, WO, WV, WK, WQ = (at(R_W + FT * D * k, FT, D) for k in range(6))
        SC = KT
        BI = {1: OT, 2: QT}
        HT = QT
        XIN = at(R_O, NT, D, p=TILE)
        WS3 = at(R_W, FT, D)
        OT3 = at(R_O, FT, W)
        PROD = at(R_K, 2, D, p=TILE)
        HID2T = at(R_Q, W, p=HID2)
        g_bc = at(R_K + 2 * D, NT, TILE, p=TILE)
        AW = at(R_W + FT * D, 3, D, p=TILE)

        cols = sbuf("cols", [128, NCOLS])
        cols1 = sbuf("cols_plus_one", [128, LAYERS * 7 * FT])
        ident = sbuf("ident", [128, 128])
        iota16 = sbuf("iota_row", [128, W], f16)
        src_i = sbuf("src_idx", [TILE, CHUNKS], i32)
        dst_i = sbuf("dst_idx", [TILE, CHUNKS], i32)
        src_f = sbuf("src_f", [TILE, CHUNKS])
        dst_f = sbuf("dst_f", [TILE, CHUNKS])
        pair_f = sbuf("pair_f", [TILE, CHUNKS])
        pair_i = sbuf("pair_idx", [TILE, CHUNKS], i32)
        idx_ring = sbuf("idx_ring", [TILE, 2, 2, HALF], i32)
        lg_ring = sbuf("logit_ring", [TILE, 2, HALF * H0])
        sum_ring = sbuf("edge_logits", [TILE, 2, HALF * H0])
        p_ring = sbuf("edge_probs", [TILE, 2, HALF * H0])
        gmax = sbuf("attr_max", [TILE, 2])
        zero16 = sbuf("zero16", [1, 512], bf16)
        stats = sbuf("bn_stats", [TILE, NT, 6])
        mv = sbuf("mean_var", [TILE, NT, 2])
        rstd = sbuf("rstd", [TILE, NT])
        vare = sbuf("var_eps", [TILE, NT])
        lnc = sbuf("ln_consts", [TILE, 2])
        negm = sbuf("neg_max", [TILE, 2, NT])
        psums = sbuf("prob_sums", [TILE, 2, NT])
        rinv = sbuf("prob_rinv", [TILE, 2, NT])
        has1 = sbuf("has_edge_src", [TILE, NT])
        has2 = sbuf("has_edge_dst", [TILE, NT])
        negm0 = sbuf("neg_max0", [TILE, 3])
        den = sbuf("den", [TILE, NT, H0])
        rden = sbuf("rden", [TILE, NT, H0])
        condT = sbuf("cond_parts", [STACK, W], bf16)
        condw = sbuf("cond_weight_parts", [STACK, 4, D], bf16)
        tid = sbuf("dst_tile", [TILE, CHUNKS])
        gflag = sbuf("group_flags", [TILE, 2, NT * GROUPS])
        mask_f = sbuf("group_mask_f", [1, GROUPS])
        mask_i = sbuf("group_mask", [1, GROUPS], i32)
        fw1 = sbuf("f_w1", [2 * NFREQ, COND])
        fw2 = sbuf("f_w2", [COND, STACK])
        cw1 = sbuf("c_w1", [128, FT, HID2])
        cw2 = sbuf("c_w2", [HID2, D])
        fcol = sbuf("f_cols", [TILE, NT, H3])
        gcol = sbuf("g_cols", [TILE, NT, H3])
        ab = sbuf("ab3", [TILE, H3])
        NOISE, PHASE, TURNS, EMB = (at(R_O + 640 * k, W, p=2 * NFREQ) for k in range(4))
        HIDC = at(R_O, W, p=COND)
        CONDF = at(R_O + 640, W, p=STACK)
        CONDH = at(R_O + 1280, W // 2, p=STACK).bitcast(bf16)
        RAW = at(R_C, 4 * D, p=STACK)
        RAWH = at(R_C + 4 * D, 2 * D, p=STACK).bitcast(bf16)
        LTMP = at(R_P + 8192, NT, W, p=TILE)
        XIN0 = at(R_LC - 2560, NT, D, p=TILE)
        ps = ctx.enter_context(nc.psum_tensor("ps", [128, 4096], f32))

        S = {}

        def sig(name):
            if name not in S:
                S[name] = sem(name)
            return S[name]

        def ring(name, keys, opened=0):
            return PsumRing(ps, sig(name + "_filled"), [sig(f"{name}_evacuated{s}") for s in range(4)], keys, opened)

        PAIRS = [(0, 1), (2, 3), (4,)]
        A = ring("front", [("hid",), ("cond",)]
                 + [("t", k) for k in range(FT)]
                 + [(n, k) for k in range(FT) for n in "qk"]
                 + [("v", n) for n in range(3)]
                 + [("s", j, h) for j in range(NT) for h in range(H0)]
                 + [("c1", j) for j in range(NT)]
                 + [("at", k) for k in range(FT)] + [("o", n) for n in range(3)]
                 + [("t2", k) for k in range(FT)]
                 + [("up", f) for f in range(FF0)] + [("down", n) for n in range(3)])

        def attend(h):
            return [("pt", h, j) for j in range(NT)] + [("av", h)]

        def scores(h):
            return [("q", h), ("k", h)] + [("s", h, i) for i in range(NT)]

        def conditioning(n):
            return [(name, n, k) for k in range(FT) for name in ("scale", "bias")]

        B = ring("layer", conditioning(1) + [("t", 1, k) for k in range(FT)]
                 + scores(0) + scores(1) + [("v", n) for n in range(3)] + attend(0)
                 + scores(2) + attend(1) + scores(3) + attend(2) + conditioning(2) + attend(3)
                 + [("o", n) for n in range(3)]
                 + [("t", 2, k) for k in range(FT)]
                 + [("m1", f) for f in range(FT)] + [("m2", n) for n in range(3)], opened=1)

        def attend3(h):
            return [("pt", h, j) for j in range(NT)] + [("av", h)]

        C = ring("back", [("t", 2, k) for k in range(FT)] + [("hid",)] + [("h", n) for n in range(3)]
                 + [("agg", n) for n in range(3)]
                 + [("t", 3, k) for k in range(FT)] + [("wx", n) for n in range(3)]
                 + [("g", 0)] + [k for h in range(H3) for k in ([("g", h + 1)] if h + 1 < H3 else []) + attend3(h)]
                 + [("x", n) for n in range(3)])

        pe_chain, dve_chain, pool_chain, act_chain = (Chain(sig(n + "_chain")) for n in ("pe", "dve", "pool", "act"))
        dve_loop_chain, pool_loop_chain = Chain(sig("dve_loop_chain")), Chain(sig("pool_loop_chain"))

        block = ctx.enter_context(nc.Block())

        def part_wait(eng, name):
            eng.sem_inc(sig("parted_" + name), 1)

        def rows_view(dram):
            return dram.rearrange("(t p) n -> p t n", p=TILE)

        def feat_view(dram):
            return dram.rearrange("(k p) n -> p k n", p=128)

        def spread(dram_row, p=TILE):
            return dram_row.partition_broadcast(p)

        @block.sync
        def _(sp):
            def load(dst, src, name):
                sp.dma_start(dst, src).then_inc(sig("ld_" + name), 16)

            load(X, rows_view(x), "x")
            load(src_i[:, :], src_t, "idx")
            load(dst_i[:, :], dst_t, "idx")
            load(cols[:, :], cols_d, "cols")
            load(NOISE[:, 0:NODES], noise.rearrange("n o -> o n").partition_broadcast(2 * NFREQ), "noise")
            load(fw1[:, :], f_w1, "fw")
            load(fw2[:, :], f_w2, "fw")
            load(WQKV, feat_view(w_qkv), "wqkv")
            load(ROWS, rows0.partition_broadcast(TILE), "rows0")
            load(ATTR[:, 0, :], attr_a, "attr")
            load(ATTR[:, 1, :], attr_b, "attr")
            load(WO0, feat_view(w_o0), "wo0")
            load(cw1[:, :, :], feat_view(c_w1), "c")
            load(cw2[:, :], c_w2, "c")
            load(ab[:, :], ab3.partition_broadcast(TILE), "c")
            for n in range(3):
                A.wait_evacuated(sp, ("v", n))
            sp.dma_start(rows_view(v0_d), V).then_inc(sig("v0_stored"), 16)
            lg_v = logits_d.rearrange("(j p s) h -> j p (s h)", j=NT, p=TILE)
            for j in range(NT):
                sp.wait_ge(sig("stage_ready"), H0 * (j + 1))
                sp.dma_start(lg_v[j], STAGE[j % 2].rearrange("p s h -> p (s h)")).then_inc(sig(f"stage_stored{j % 2}"), 16)
            sp.wait_ge(sig("stage_stored1"), 16 * (NT // 2))
            load(WDN0, feat_view(w_down0), "wdown0")
            sp.wait_ge(sig("stage_stored0"), 16 * ((NT + 1) // 2))
            sp.wait_ge(sig("agg_done"), 1)
            load(WUP0, feat_view(w_up0), "wup0")
            sp.wait_ge(sig("lc_ready"), 1)
            load(XIN0, rows_view(x), "x0")
            sp.wait_ge(sig("counts_ready"), 1)
            sp.dma_start(c2_d, at(R_C, NT * W, p=TILE)).then_inc(sig("counts_stored"), 16)
            A.wait_filled(sp, ("o", 2))
            w_of = {"wq": (WQ, wq), "wk": (WK, wk), "wv": (WV, wv), "wo": (WO, wo), "m1": (M1, m_w1), "m2": (M2, m_w2)}

            def load_weight(name, layer):
                dst, src = w_of[name]
                load(dst, src[layer].rearrange("a (k p) n -> p (a k) n", p=128), name)

            def load_row(n, layer):
                load(ROWS[:, n, :], rows1[n, layer, :].partition_broadcast(TILE), f"row{n}")

            load_weight("wq", slice(0, 1))
            load_weight("wk", slice(0, 1))
            A.wait_filled(sp, ("down", 2))
            sp.wait_ge(sig("residual_biased"), 2)
            for name in ("wv", "wo", "m1", "m2"):
                load_weight(name, slice(0, 1))
            for n in range(3):
                load_row(n, slice(0, 1))
            sp.wait_ge(sig("x1_ready"), NT)
            sp.dma_start(rows_view(x1_d), X).then_inc(sig("x1_stored"), 16)
            with sp.Fori(0, LAYERS - 1) as i:
                B.turn = i
                nxt = bass.ds(i + 1, 1)
                B.wait_filled(sp, ("q", 3))
                load_weight("wq", nxt)
                B.wait_filled(sp, ("k", 3))
                load_weight("wk", nxt)
                B.wait_filled(sp, ("v", 2))
                load_weight("wv", nxt)
                B.wait_evacuated(sp, ("v", 2))
                load_row(0, nxt)
                sp.wait_ge(sig("residual_biased1"), 2 * i + 1)
                load_row(1, nxt)
                B.wait_filled(sp, ("o", 2))
                load_weight("wo", nxt)
                B.wait_filled(sp, ("m1", FT - 1))
                load_weight("m1", nxt)
                sp.wait_ge(sig("residual_biased1"), 2 * i + 2)
                load_row(2, nxt)
                B.wait_filled(sp, ("m2", 2))
                load_weight("m2", nxt)
            B.turn = LAYERS - 1
            B.wait_filled(sp, ("q", 3))
            sp.wait_ge(sig("residual_biased1"), 2 * LAYERS)
            load(ROWS[:, 0, :], c_b2.partition_broadcast(TILE), "rows3")
            B.wait_filled(sp, ("m2", 2))
            load(WS3, feat_view(ws3), "ws3")
            sp.wait_ge(sig("cond_parts_ready"), LAYERS + 1)
            load(at(R_C, NT * W, p=TILE), c2_d, "c2")
            load(AW, rows3.partition_broadcast(TILE), "aw")
            sp.wait_ge(sig("x1_stored"), 16)
            load(XIN, rows_view(x1_d), "x1")
            sp.wait_ge(sig("out_ready"), NT)
            sp.dma_start(rows_view(out), X).then_inc(sig("out_stored"), 16)
            sp.wait_ge(sig("out_stored"), 16)

        @block.gpsimd
        def _(pool):
            g = nc.gpsimd
            g.memset(zero16[:, :], 0.0).then_inc(sig("zeros_ready"), 1)
            g.memset(lnc[:, 0:1], EPS)
            g.memset(lnc[:, 1:2], -0.5)
            g.iota(iota16[:, :], pattern=[[1, W]], base=0, channel_multiplier=0,
                   allow_small_or_imprecise_dtypes=True).then_inc(sig("iota_ready"), 1)
            pool_chain(pool, g.memset(ident[:, :], 0.0))
            g.affine_select(out=ident[:, :], in_=ident[:, :], compare_op=ALU.not_equal, fill=1.0, base=0,
                            pattern=[[-1, 128]], channel_multiplier=1).then_inc(sig("ident_ready"), 1)

            def powers(sems, chain, base):
                var_ready, rstd_ready = sems
                for t in range(NT):
                    pool.wait_ge(var_ready, base + t + 1)
                    chain(pool, g.tensor_tensor(vare[:, t:t + 1], mv[:, t, 1:2], lnc[:, 0:1], ALU.add))
                    g.tensor_tensor(rstd[:, t:t + 1], vare[:, t:t + 1], lnc[:, 1:2], ALU.pow).then_inc(rstd_ready, 1)

            front = (sig("var_ready"), sig("rstd_ready"))
            powers(front, pool_chain, 0)
            pool.wait_ge(sig("gmax_part"), 1)
            g.partition_all_reduce(gmax[:, 1:2], gmax[:, 0:1], TILE, bass.bass_isa.ReduceOp.max).then_inc(sig("gmax_all"), 1)
            pool.wait_ge(sig("flags_part"), 1)
            g.partition_all_reduce(gflag[:, 1, :], gflag[:, 0, :], TILE, bass.bass_isa.ReduceOp.max).then_inc(sig("flags_all"), 1)
            pool.wait_ge(sig("xn_ready"), NT)
            pool.wait_ge(sig("ld_rows0"), 16)
            g.tensor_tensor(X, X, ROWS[:, 1:2, :].to_broadcast([TILE, NT, D]), ALU.add).then_inc(sig("residual_biased"), 1)
            for j in range(2):
                pool.wait_ge(sig(f"stage_stored{j}"), 16 * ((NT + 1 - j) // 2))
            pool.wait_ge(sig("v0_stored"), 16)
            pool.wait_ge(sig("pairs_ready"), 1)
            pool.sem_inc(sig("gather_slot_free"), 2)
            with pool.Fori(0, CHUNKS // (2 * HALF)) as i:
                for hf in range(2):
                    pool.wait_ge(sig("gather_slot_free"), 2 * i + (hf + 1))
                    now = bass.ds(2 * HALF * i + HALF * hf, HALF)
                    g.tensor_copy(idx_ring[:, hf, 0, :], src_i[:, now])
                    g.tensor_copy(idx_ring[:, hf, 1, :], pair_i[:, now]).then_inc(sig("idx_copied"), 1)
                    pool.wait_ge(sig("idx_copied"), 2 * i + (hf + 1))
                    part_wait(pool, "pool")
                    for u in range(HALF):
                        g.indirect_dma_start(VG[:, hf, u, :], None, v0_d,
                                             bass.IndirectOffsetOnAxis(ap=idx_ring[:, hf, 0, u:u + 1], axis=0)
                                             ).then_inc(sig(f"gathered{hf}"), 16)
                        g.indirect_dma_start(lg_ring[:, hf, u * H0:(u + 1) * H0], None, logits_d,
                                             bass.IndirectOffsetOnAxis(ap=idx_ring[:, hf, 1, u:u + 1], axis=0)
                                             ).then_inc(sig(f"gathered{hf}"), 16)
            pool.wait_ge(sig("counts_stored"), 16)
            A.wait_filled(pool, ("c1", NT - 1))
            for q in range(6):
                pool.dma_start(RAW[COND * q:COND * (q + 1), :], cond_w[0, :, :]).then_inc(sig("ld_raw"), 16)
            powers(front, pool_chain, NT)
            pool.wait_ge(sig("xn_ready"), 2 * NT)
            g.tensor_tensor(X, X, ROWS[:, 2:3, :].to_broadcast([TILE, NT, D]), ALU.add).then_inc(sig("residual_biased"), 1)
            powers(front, pool_chain, 2 * NT)
            def load_raw(layer):
                for q in range(6):
                    pool.dma_start(RAW[COND * q:COND * (q + 1), :], cond_w[layer, :, :].rearrange("a c n -> (a c) n")
                                   ).then_inc(sig("ld_raw"), 16)

            pool.wait_ge(sig("x1_stored"), 16)
            with pool.Fori(0, LAYERS) as i:
                B.turn = i
                pool.wait_ge(sig("cond_parts_ready"), i + 1)
                load_raw(bass.ds(i + 1, 1))
                pool_loop_chain.turn, pool_loop_chain.per_turn = i, 2 * NT
                for n in (1, 2):
                    powers((sig("var_ready1"), sig("rstd_ready1")), pool_loop_chain, 2 * NT * i + NT * (n - 1))
                    pool.wait_ge(sig("xn_ready1"), 2 * NT * i + NT * n)
                    pool.wait_ge(sig(f"ld_row{n}"), 16 * i + 16)
                    g.tensor_tensor(X, X, ROWS[:, n:n + 1, :].to_broadcast([TILE, NT, D]), ALU.add
                                    ).then_inc(sig("residual_biased1"), 1)
            assert pool_loop_chain.count == pool_loop_chain.per_turn
            for n in range(2):
                powers((sig("var_ready3"), sig("rstd_ready3")), pool_chain, n * NT)
            powers((sig("var_ready3"), sig("rstd_ready3")), pool_chain, 2 * NT)

        @block.scalar
        def _(act):
            a = nc.scalar

            def col(name, k=0, p=128):
                return cols[0:p, COLS[name] + k:COLS[name] + k + 1]

            act.wait_ge(sig("emb_ready"), 1)
            a.activation(EMB, TURNS, ACT.Sin).then_inc(sig("sin_ready"), 1)
            A.wait_filled(act, ("hid",))
            act.wait_ge(sig("sin_ready"), 1)
            A.release(("hid",), a.activation(halves(HIDC), A.halves(("hid",), COND), ACT.Silu, bias=col("f_b1", 0, COND)))
            A.wait_filled(act, ("cond",))
            A.release(("cond",), a.activation(halves(CONDF), A.halves(("cond",), STACK), ACT.Identity,
                                              bias=col("f_b2", 0, STACK)))
            A.wait_evacuated(act, ("cond",))
            a.activation(CONDH, CONDF, ACT.Copy).then_inc(sig("cond_high"), 1)
            act.wait_ge(sig("cond_rest"), 1)
            a.activation(CONDH, CONDF, ACT.Copy).then_inc(sig("cond_high"), 1)
            for k in range(FT):
                A.wait_filled(act, ("k", k))
                A.release(("k", k), a.activation(halves(KT[:, k, :]), A.halves(("k", k), 128), ACT.Identity,
                                                 bias=col("bk", k)))
            for n in range(NT * H0):
                j, h = divmod(n, H0)
                A.wait_evacuated(act, ("s", j, h))
                if h == 0 and j >= 2:
                    act.wait_ge(sig(f"stage_stored{j % 2}"), 16 * (j // 2))
                a.activation(STAGE[j % 2][:, :, h], TEMP[:, n % 3, 0:NODES], ACT.Identity, scale=-1.0,
                             bias=negm0[:, n % 3:n % 3 + 1]).then_inc(sig("stage_ready"), 1)
            with act.Fori(0, CHUNKS // (2 * HALF)) as i:
                for hf in range(2):
                    act.wait_ge(sig("edge_logits_ready"), 2 * i + (hf + 1))
                    a.activation(p_ring[:, hf, :], sum_ring[:, hf, :], ACT.Exp).then_inc(sig("edge_probs_ready"), 1)
                    act.wait_ge(sig("msg_group_free"), 2 * i + (hf + 2))
                    act.wait_ge(sig("edge_probs_ready"), 2 * i + (hf + 1))
                    a.activation(PR[:, hf, :, 0, :], p_ring[:, hf, :].rearrange("p (u h) -> p u h", u=HALF), ACT.Copy
                                 ).then_inc(sig("edge_probs_high"), 1)
                    for u in range(HALF):
                        act.wait_ge(sig("msg_full"), 2 * HALF * i + (HALF * hf + u + 1))
                        a.activation(MSGR[:, HALF * hf + u, 0, :], VG[:, hf, u, :], ACT.Copy).then_inc(sig("msg_high"), 1)
            act.wait_ge(sig("lc_half"), 1)
            a.activation(LC, LC, ACT.Ln).then_inc(sig("ln_done"), 1)
            for k in range(0, FT, 2):
                A.wait_filled(act, ("at", k))
                A.release(("at", k), a.activation(tiled(YT[:, k, :]), A.blocks(("at", k), NT, 128), ACT.Copy))
            for f in range(FF0):
                A.wait_filled(act, ("up", f))
                A.release(("up", f), a.activation(halves(HT0[:, f, :]), A.halves(("up", f), 128), ACT.Gelu,
                                                  bias=col("b1", f)))

            def raw_high():
                a.activation(RAWH, RAW, ACT.Copy).then_inc(sig("raw_high"), 1)

            act.wait_ge(sig("ld_raw"), 96)
            raw_high()
            act.wait_ge(sig("raw_rest"), 1)
            raw_high()

            def evac_columns(key, dst, bias, func=ACT.Identity):
                B.wait_filled(act, key)
                B.release(key, a.activation(halves(dst), B.halves(key, 128), func, bias=bias))

            with act.Fori(0, LAYERS) as i:
                B.turn = i

                def lcol(kind, k, table=cols, base=COLS["layers"]):
                    return table[:, bass.ds(i * (7 * FT) + (base + kind + k), 1)]

                def make_conditioning(n):
                    for k in range(FT):
                        evac_columns(("scale", n, k), SC[:, k, :], lcol((S1B, S2B)[n - 1], k, cols1, 0))
                        evac_columns(("bias", n, k), BI[n][:, k, :], lcol((B1B, B2B)[n - 1], k))

                def exps(h):
                    evac_columns(("k", h), KT[:, h, :], lcol(BK, h))
                    for t in range(NT):
                        B.wait_evacuated(act, ("s", h, t))
                        a.activation(P[:, h % 2, t, :], P[:, h % 2, t, :], ACT.Exp, scale=-1.0,
                                     bias=negm[:, h % 2, t:t + 1], accum_out=psums[:, h % 2, t:t + 1]
                                     ).then_inc(sig("exps_done"), 1)

                def outputs(h):
                    for j in (0, 2, 4):
                        B.wait_filled(act, ("pt", h, j))
                        B.release(("pt", h, j), a.activation(tiled(PT[:, h % 2, j, :]), B.blocks(("pt", h, j), NT), ACT.Copy))
                    B.wait_filled(act, ("av", h))
                    B.release(("av", h), a.activation(halves(OT[:, h, :]), B.halves(("av", h), 128), ACT.Copy))

                make_conditioning(1)
                exps(0)
                exps(1)
                outputs(0)
                exps(2)
                outputs(1)
                exps(3)
                outputs(2)
                make_conditioning(2)
                act.wait_ge(sig("ld_raw"), 96 * i + 192)
                raw_high()
                outputs(3)
                act.wait_ge(sig("raw_rest"), i + 2)
                raw_high()
                for f in range(FT):
                    evac_columns(("m1", f), HT[:, f, :], lcol(MB1, f), ACT.Relu)
            act.wait_ge(sig("lc2_half"), 1)
            a.activation(LC, LC, ACT.Ln).then_inc(sig("ln_done"), 1)
            for k in range(0, FT, 2):
                C.wait_filled(act, ("t", 2, k))
                C.release(("t", 2, k), a.activation(tiled(YT[:, k, :]), C.blocks(("t", 2, k), NT, 128), ACT.Copy))
            C.wait_filled(act, ("hid",))
            C.release(("hid",), a.activation(halves(HID2T), C.halves(("hid",), HID2), ACT.Relu, bias=col("c_b1", 0, HID2)))
            for k in range(0, FT, 2):
                C.wait_filled(act, ("t", 3, k))
                C.release(("t", 3, k), a.activation(tiled(YT[:, k, :]), C.blocks(("t", 3, k), NT, 128), ACT.Copy))
            act.wait_ge(sig("fg_ready"), 1)

            def edge_sums(h):
                C.wait_filled(act, ("g", h))
                if h >= 2:
                    C.wait_filled(act, ("pt", h - 2, NT - 1))
                for t in range(NT):
                    z = a.activation(tiled(P[:, h % 2, t, :]), C.blocks(("g", h), NT), ACT.Identity, bias=fcol[:, t, h:h + 1])
                    if t < NT - 1:
                        z.then_inc(sig("z_ready"), 1)
                    else:
                        C.release(("g", h), z)

            edge_sums(0)
            for h in range(H3):
                if h + 1 < H3:
                    edge_sums(h + 1)
                for t in range(NT):
                    act.wait_ge(sig("leaky_done"), NT * h + t + 1)
                    a.activation(P[:, h % 2, t, :], P[:, h % 2, t, :], ACT.Exp, scale=-1.0, bias=negm[:, h % 2, t:t + 1],
                                 accum_out=psums[:, h % 2, t:t + 1]).then_inc(sig("exps_done3"), 1)
                for j in (0, 2, 4):
                    C.wait_filled(act, ("pt", h, j))
                    C.release(("pt", h, j), a.activation(tiled(PT[:, h % 2, j, :]), C.blocks(("pt", h, j), NT), ACT.Copy))

        @block.vector
        def _(dve):
            v = nc.vector
            MAGIC = 12582912.0
            PI2 = (6.28125, 0.0019350051879882812, 3.0199159819567194e-07)

            def col(name, k=0, p=128):
                return cols[0:p, COLS[name] + k:COLS[name] + k + 1]

            def norm(sems, base, dst, before=None, chain=dve_chain, done=None):
                var_ready, rstd_ready, xn_ready = sems
                for t in range(NT + 1):
                    if t < NT:
                        if before:
                            before(t)
                        chain(dve, v.bn_stats(stats[:, t, :], X[:, t, :]))
                        part_wait(dve, "dve")
                        v.bn_aggr(mv[:, t, :], stats[:, t, :]).then_inc(var_ready, 1)
                    if t >= 1:
                        dve.wait_ge(rstd_ready, base + t)
                        v.tensor_scalar(dst[:, t - 1, :], X[:, t - 1, :], mv[:, t - 1, 0:1], rstd[:, t - 1:t],
                                        ALU.subtract, ALU.mult).then_inc(done or xn_ready, 1)

            front = (sig("var_ready"), sig("rstd_ready"), sig("xn_ready"))
            v.memset(YT[:, :, NODES:W], 0.0)
            dve_chain(dve, v.memset(NOISE[:, NODES:W], 0.0))
            dve.wait_ge(sig("ld_noise"), 16)
            dve.wait_ge(sig("ld_cols"), 16)
            v.tensor_scalar(cols1[:, :], cols[:, COLS["layers"]:NCOLS], 1.0, None, ALU.add)
            E = 2 * NFREQ
            dve_chain(dve, v.tensor_scalar(PHASE, NOISE, col("freq", 0, E), None, ALU.mult))
            dve_chain(dve, v.tensor_scalar(TURNS, PHASE, 0.15915494309189535, None, ALU.mult))
            dve_chain(dve, v.tensor_scalar(TURNS, TURNS, col("turn", 0, E), None, ALU.add))
            dve_chain(dve, v.tensor_scalar(TURNS, TURNS, MAGIC, None, ALU.add))
            dve_chain(dve, v.tensor_scalar(TURNS, TURNS, MAGIC, None, ALU.subtract))
            for part in PI2:
                dve_chain(dve, v.scalar_tensor_tensor(PHASE, TURNS, -part, PHASE, ALU.mult, ALU.add))
            dve_chain(dve, v.tensor_scalar(PHASE, PHASE, col("angle", 0, E), None, ALU.add))
            v.tensor_scalar(TURNS, PHASE, 3.1415925, -3.1415925, ALU.min, ALU.max).then_inc(sig("emb_ready"), 1)
            dve.wait_ge(sig("ld_idx"), 32)
            v.tensor_copy(src_f[:, :], src_i[:, :])
            dve_chain(dve, v.tensor_copy(dst_f[:, :], dst_i[:, :]))
            dve_chain(dve, v.scalar_tensor_tensor(pair_f[:, :], dst_f[:, :], float(NODES), src_f[:, :], ALU.mult, ALU.add))
            v.tensor_copy(pair_i[:, :], pair_f[:, :]).then_inc(sig("pairs_ready"), 1)
            dve.wait_ge(sig("ld_attr"), 32)
            dve_chain(dve, v.tensor_tensor(ATTR[:, 0, :], ATTR[:, 0, :], ATTR[:, 1, :], ALU.add))
            v.reduce_max(gmax[:, 0:1], ATTR[:, 0, :], AX.X).then_inc(sig("gmax_part"), 1)
            dve_chain(dve, v.tensor_scalar(tid[:, :], dst_f[:, :], float(TILE), None, ALU.is_ge))
            for j in range(2, NT):
                dve_chain(dve, v.scalar_tensor_tensor(tid[:, :], dst_f[:, :], float(TILE * j), tid[:, :], ALU.is_ge, ALU.add))
            for j in range(NT):
                last = v.tensor_scalar(FLAGS[:, j, :], tid[:, :], float(j), None, ALU.is_equal)
            dve_chain(dve, last)
            v.tensor_reduce(gflag[:, 0, :], FLAGS.rearrange("p j (g u) -> p (j g) u", u=4), AX.X, ALU.max
                            ).then_inc(sig("flags_part"), 1)
            dve.wait_ge(sig("ld_x"), 16)
            norm(front, 0, XN)
            dve.wait_ge(sig("gmax_all"), 1)
            dve_chain(dve, v.tensor_scalar(ATTR[:, 0, :], ATTR[:, 0, :], gmax[:, 1:2], None, ALU.subtract))
            dve.wait_ge(sig("flags_all"), 1)
            dve_chain(dve, v.tensor_copy(mask_f[:, :], gflag[0:1, 1, 0:GROUPS]))
            for j in range(1, NT):
                dve_chain(dve, v.scalar_tensor_tensor(mask_f[:, :], gflag[0:1, 1, GROUPS * j:GROUPS * (j + 1)], float(1 << j),
                                                      mask_f[:, :], ALU.mult, ALU.add))
            v.tensor_copy(mask_i[:, :], mask_f[:, :]).then_inc(sig("mask_ready"), 1)
            dve.wait_ge(sig("cond_high"), 1)
            v.scalar_tensor_tensor(CONDF, CONDH, col("part_c", 0, STACK), CONDF, ALU.mult, ALU.add).then_inc(sig("cond_rest"), 1)
            dve.wait_ge(sig("cond_high"), 2)
            v.scalar_tensor_tensor(condT[:, :], CONDH, col("part_c", 1, STACK), CONDF, ALU.mult, ALU.add)
            for k in range(FT):
                A.wait_filled(dve, ("t", k))
                A.release(("t", k), v.tensor_scalar(tiled(YT[:, k, :]), A.blocks(("t", k), NT, 128),
                                                    col("ln1_g", k), col("ln1_b", k), ALU.mult, ALU.add))
            for k in range(FT):
                A.wait_filled(dve, ("q", k))
                A.release(("q", k), v.tensor_scalar(halves(QT[:, k, :]), A.halves(("q", k), 128),
                                                    col("bq", k), float(D) ** -0.5, ALU.add, ALU.mult))

            def bank_view(r, key, pair):
                return r.view(key).rearrange("p (b c) -> p b c", b=2)[:, 0:len(pair), :]

            def row_bias(r, key, pair, dst, row):
                r.wait_filled(dve, key)
                r.release(key, v.tensor_tensor(dst[:, pair[0]:pair[-1] + 1, :], bank_view(r, key, pair),
                                               row.to_broadcast([TILE, len(pair), D]), ALU.add))

            dve.wait_ge(sig("ld_rows0"), 16)
            for n, pair in enumerate(PAIRS):
                row_bias(A, ("v", n), pair, V, ROWS[:, 0:1, :])
            dve.wait_ge(sig("iota_ready"), 1)
            with dve.Fori(0, GROUPS // 2) as i:
                for hf in range(2):
                    dve.wait_ge(sig("onehot_group_free"), 2 * i + (hf + 2))
                    for u in range(HALF * hf, HALF * hf + HALF):
                        c = bass.ds(2 * HALF * i + u, 1)
                        v.tensor_scalar(OH16[:, 0, u, :], iota16[0:TILE, :], dst_f[:, c], None, ALU.is_equal)
                        last = v.tensor_scalar(OH16[:, 1, u, :], iota16[0:TILE, :], src_f[:, c], None, ALU.is_equal)
                    last.then_inc(sig("onehot_ready"), 1)
            dve.wait_ge(sig("counts_done"), 1)
            for j in range(NT):
                v.tensor_copy(C2[:, j, 0:512], ps[0:TILE, 512 * j:512 * j + 512])
                last = v.tensor_copy(C2[:, j, 512:W], ps[0:TILE, 2560 + 128 * j:2560 + 128 * j + W - 512])
            last.then_inc(sig("counts_ready"), 1)
            dve.wait_ge(sig("counts_ready"), 1)
            dve_chain(dve, v.tensor_scalar(MASK, C2, 0.5, -BIG, ALU.is_lt, ALU.mult))
            for n in range(NT * H0):
                j, h = divmod(n, H0)
                A.wait_filled(dve, ("s", j, h))
                if n >= 3:
                    dve.wait_ge(sig("stage_ready"), n - 2)
                A.release(("s", j, h), v.tensor_tensor_reduce(
                    out=halves(TEMP[:, n % 3, :]), in0=A.halves(("s", j, h)), in1=halves(MASK[:, j, :]), scale=-1.0, scalar=3.0e38,
                    op0=ALU.add, op1=ALU.min, accum_out=negm0[:, n % 3:n % 3 + 1]))
            with dve.Fori(0, CHUNKS // (2 * HALF)) as i:
                for hf in range(2):
                    dve.wait_ge(sig(f"gathered{hf}"), 32 * HALF * i + 32 * HALF)
                    now = bass.ds(2 * HALF * H0 * i + HALF * H0 * hf, HALF * H0)
                    v.tensor_tensor(sum_ring[:, hf, :], lg_ring[:, hf, :], ATTR[:, 0, now], ALU.add
                                    ).then_inc(sig("edge_logits_ready"), 1)
                    dve.wait_ge(sig("msg_group_free"), 2 * i + (hf + 2))

                    def onehot(u):
                        v.tensor_scalar(OHR[:, HALF * hf + u, :], iota16[0:TILE, :],
                                        dst_f[:, bass.ds(2 * HALF * i + (HALF * hf + u), 1)], None, ALU.is_equal)

                    def message(u):
                        v.tensor_tensor(VG[:, hf, u, :].rearrange("p (h d) -> p h d", h=H0),
                                        VG[:, hf, u, :].rearrange("p (h d) -> p h d", h=H0),
                                        p_ring[:, hf, u * H0:(u + 1) * H0].unsqueeze(2).to_broadcast([TILE, H0, DH0]),
                                        ALU.mult).then_inc(sig("msg_full"), 1)

                    def message_low(u):
                        dve.wait_ge(sig("msg_high"), 2 * HALF * i + (HALF * hf + u + 1))
                        return v.tensor_tensor(MSGR[:, HALF * hf + u, 1, :], VG[:, hf, u, :],
                                               MSGR[:, HALF * hf + u, 0, :].bitcast(f32), ALU.subtract)

                    onehot(0)
                    dve.wait_ge(sig("edge_probs_ready"), 2 * i + (hf + 1))
                    message(0)
                    onehot(1)
                    message(1)
                    dve.wait_ge(sig("edge_probs_high"), 2 * i + (hf + 1))
                    v.tensor_tensor(PR[:, hf, :, 1, :], p_ring[:, hf, :].rearrange("p (u h) -> p u h", u=HALF),
                                    PR[:, hf, :, 0, :].bitcast(f32), ALU.subtract)
                    message(2)
                    message_low(0)
                    onehot(2)
                    message(3)
                    message_low(1)
                    onehot(3)
                    message_low(2)
                    message_low(3).then_inc(sig("msg_ready"), 1)
                    dve.wait_ge(sig("msg_ready"), 2 * i + (hf + 1))
                    dve.sem_inc(sig("gather_slot_free"), 1)
            dve.wait_ge(sig("agg_done"), 1)
            dve_chain(dve, v.tensor_reduce(den[:, :, :], ps[0:TILE, 2560:2560 + 2 * NT * H0].rearrange(
                "p (j k h) -> p j h k", j=NT, k=2), AX.X, ALU.add))
            dve_chain(dve, v.tensor_scalar(den[:, :, :], den[:, :, :], 1.0e-37, None, ALU.max))
            dve_chain(dve, v.reciprocal(rden[:, :, :], den[:, :, :]))
            for j in range(NT):
                last = v.tensor_tensor(V[:, j, :].rearrange("p (h d) -> p h d", h=H0),
                                       ps[0:TILE, 512 * j:512 * j + 512].rearrange("p (h d) -> p h d", h=H0),
                                       rden[:, j, :].unsqueeze(2).to_broadcast([TILE, H0, DH0]), ALU.mult)
            last.then_inc(sig("agg_ready"), 1)

            def make_log_counts(counts, name):
                dve_chain(dve, v.tensor_scalar(LTMP, counts, 0.5, -BIG, ALU.is_lt, ALU.mult))
                v.tensor_scalar(LC, counts, 1.0, None, ALU.max).then_inc(sig(name), 1)

            v.memset(LC[:, :, NODES:W], 0.0)
            for j in range(NT):
                A.wait_filled(dve, ("c1", j))
                A.release(("c1", j), v.tensor_copy(tiled(LC[:, j, :]), A.blocks(("c1", j), NT)))
            A.wait_evacuated(dve, ("c1", NT - 1))
            make_log_counts(LC, "lc_half")
            for k in range(1, FT, 2):
                A.wait_filled(dve, ("at", k))
                A.release(("at", k), v.tensor_copy(tiled(YT[:, k, :]), A.blocks(("at", k), NT, 128)))
            dve.wait_ge(sig("ln_done"), 1)
            dve_chain(dve, v.tensor_tensor(LC, LC, LTMP, ALU.add))
            dve_chain(dve, v.tensor_reduce(has1[:, :], LC, AX.X, ALU.max))
            v.tensor_scalar(has1[:, :], has1[:, :], -0.5 * BIG, None, ALU.is_gt).then_inc(sig("lc_ready"), 1)

            def add_rows(r, name, chain, n_bias):
                def before(t):
                    n = t // 2
                    if t == 2 * n:
                        r.wait_filled(dve, (name, n))
                        pair = PAIRS[n]
                        ins = v.tensor_tensor(X[:, pair[0]:pair[-1] + 1, :], X[:, pair[0]:pair[-1] + 1, :],
                                              bank_view(r, (name, n), pair), ALU.add)
                        r.release((name, n), ins)
                        r.wait_evacuated(dve, (name, n))
                return before

            dve.wait_ge(sig("residual_biased"), 1)
            norm(front, NT, XN, add_rows(A, "o", dve_chain, 0))
            for k in range(FT):
                A.wait_filled(dve, ("t2", k))
                A.release(("t2", k), v.tensor_scalar(tiled(YT[:, k, :]), A.blocks(("t2", k), NT, 128),
                                                     col("ln2_g", k), col("ln2_b", k), ALU.mult, ALU.add))
            dve.wait_ge(sig("residual_biased"), 2)
            dve.wait_ge(sig("ld_x0"), 16)
            add_down = add_rows(A, "down", dve_chain, 1)

            def block0_end(t):
                add_down(t)
                dve_chain(dve, v.tensor_tensor(X[:, t, :], X[:, t, :], XIN0[:, t, :], ALU.add))

            norm(front, 2 * NT, X, block0_end, done=sig("x1_ready"))
            dve.wait_ge(sig("x1_ready"), NT)

            v.memset(PT[:, :, :, NODES:W], 0.0).then_inc(sig("padding_ready"), 1)

            def raw_rest():
                v.scalar_tensor_tensor(RAW, RAWH, col("part_w", 0, STACK), RAW, ALU.mult, ALU.add).then_inc(sig("raw_rest"), 1)

            def weight_parts():
                v.scalar_tensor_tensor(condw[:, :, :].rearrange("p q n -> p (q n)"), RAWH, col("part_w", 1, STACK), RAW,
                                       ALU.mult, ALU.add).then_inc(sig("cond_parts_ready"), 1)

            dve.wait_ge(sig("raw_high"), 1)
            raw_rest()
            dve.wait_ge(sig("raw_high"), 2)
            weight_parts()

            with dve.Fori(0, LAYERS) as i:
                B.turn = i
                dve_loop_chain.turn, dve_loop_chain.per_turn = i, 2 * NT + 2 * FT + 2 * H1

                def lcol(kind, k):
                    return cols[:, bass.ds(i * (7 * FT) + (COLS["layers"] + kind + k), 1)]

                mid = (sig("var_ready1"), sig("rstd_ready1"), sig("xn_ready1"))

                def apply_conditioning(n):
                    for k in range(FT):
                        B.wait_evacuated(dve, ("scale", n, k))
                        B.wait_evacuated(dve, ("bias", n, k))
                        B.wait_filled(dve, ("t", n, k))
                        dve_loop_chain(dve, v.tensor_tensor(tiled(YT[:, k, :]), B.blocks(("t", n, k), NT, 128),
                                                            tiled(SC[:, k, :]), ALU.mult))
                        B.release(("t", n, k), v.tensor_tensor(YT[:, k, 0:NODES], YT[:, k, 0:NODES],
                                                                  BI[n][:, k, 0:NODES], ALU.add))

                def queries(h):
                    B.wait_filled(dve, ("q", h))
                    B.release(("q", h), v.tensor_scalar(halves(QT[:, h, :]), B.halves(("q", h), 128), lcol(BQ, h),
                                                        float(DH1) ** -0.5, ALU.add, ALU.mult))

                def masked(h):
                    if h >= 2:
                        B.wait_filled(dve, ("pt", h - 2, NT - 1))
                    for t in range(NT):
                        B.wait_filled(dve, ("s", h, t))
                        part_wait(dve, "dve")
                        B.release(("s", h, t), v.tensor_tensor_reduce(
                            out=halves(P[:, h % 2, t, :]), in0=B.halves(("s", h, t)), in1=halves(LC[:, t, :]), scale=-1.0,
                            scalar=3.0e38, op0=ALU.add, op1=ALU.min, accum_out=negm[:, h % 2, t:t + 1]))

                def normalise(h):
                    dve.wait_ge(sig("exps_done"), H1 * NT * i + NT * (h + 1))
                    dve_loop_chain(dve, v.reciprocal(rinv[:, h % 2, :], psums[:, h % 2, :]))
                    dve_loop_chain(dve, v.tensor_tensor(rinv[:, h % 2, :], rinv[:, h % 2, :], has1[:, :], ALU.mult))
                    for t in range(NT):
                        v.tensor_scalar(P[:, h % 2, t, :], P[:, h % 2, t, :], rinv[:, h % 2, t:t + 1], None,
                                        ALU.mult).then_inc(sig("probs_normalised"), 1)

                def transposed(h):
                    for j in (1, 3):
                        B.wait_filled(dve, ("pt", h, j))
                        B.release(("pt", h, j), v.tensor_copy(tiled(PT[:, h % 2, j, :]), B.blocks(("pt", h, j), NT)))

                norm(mid, 2 * NT * i, XN, chain=dve_loop_chain)
                apply_conditioning(1)
                queries(0)
                masked(0)
                queries(1)
                normalise(0)
                masked(1)
                dve.wait_ge(sig("ld_row0"), 16 * i + 16)
                for n, pair in enumerate(PAIRS):
                    row_bias(B, ("v", n), pair, V, ROWS[:, 0:1, :])
                normalise(1)
                transposed(0)
                queries(2)
                masked(2)
                transposed(1)
                normalise(2)
                queries(3)
                masked(3)
                transposed(2)
                normalise(3)
                transposed(3)
                dve.wait_ge(sig("raw_high"), 2 * i + 3)
                raw_rest()
                dve.wait_ge(sig("residual_biased1"), 2 * i + 1)
                norm(mid, 2 * NT * i + NT, XN, add_rows(B, "o", dve_loop_chain, 0), chain=dve_loop_chain)
                apply_conditioning(2)
                dve.wait_ge(sig("raw_high"), 2 * i + 4)
                weight_parts()
                dve.wait_ge(sig("residual_biased1"), 2 * i + 2)
                for n, pair in enumerate(PAIRS):
                    B.wait_filled(dve, ("m2", n))
                    B.release(("m2", n), v.tensor_tensor(X[:, pair[0]:pair[-1] + 1, :], X[:, pair[0]:pair[-1] + 1, :],
                                                         bank_view(B, ("m2", n), pair), ALU.add))
                for n in range(3):
                    B.wait_evacuated(dve, ("m2", n))
            assert dve_loop_chain.count == dve_loop_chain.per_turn, dve_loop_chain.count

            dve.wait_ge(sig("ld_c2"), 16)
            make_log_counts(C2, "lc2_half")
            back = (sig("var_ready3"), sig("rstd_ready3"), sig("xn_ready3"))
            dve.wait_ge(sig("ld_x1"), 16)

            def block1_end(t):
                dve_chain(dve, v.tensor_tensor(X[:, t, :], X[:, t, :], XIN[:, t, :], ALU.add))

            norm(back, 0, X, block1_end)
            dve.wait_ge(sig("ln_done"), 2)
            dve_chain(dve, v.tensor_tensor(LC, LC, LTMP, ALU.add))
            dve_chain(dve, v.tensor_reduce(has2[:, :], LC, AX.X, ALU.max))
            dve_chain(dve, v.tensor_scalar(has2[:, :], has2[:, :], -0.5 * BIG, None, ALU.is_gt))
            for k in range(1, FT, 2):
                C.wait_filled(dve, ("t", 2, k))
                C.release(("t", 2, k), v.tensor_copy(tiled(YT[:, k, :]), C.blocks(("t", 2, k), NT, 128)))
            dve.wait_ge(sig("ld_rows3"), 16)
            for n, pair in enumerate(PAIRS):
                row_bias(C, ("h", n), pair, V, ROWS[:, 0:1, :])
            for n in range(3):
                C.wait_evacuated(dve, ("h", n))

            def block2_end(t):
                n = t // 2
                if t == 2 * n:
                    pair = PAIRS[n]
                    tiles = slice(pair[0], pair[-1] + 1)
                    dve_chain(dve, v.tensor_tensor(X[:, tiles, :], X[:, tiles, :], V[:, tiles, :], ALU.add))
                    C.wait_filled(dve, ("agg", n))
                    C.release(("agg", n), v.tensor_tensor(X[:, tiles, :], X[:, tiles, :], bank_view(C, ("agg", n), pair), ALU.add))
                    C.wait_evacuated(dve, ("agg", n))

            norm(back, NT, X, block2_end)
            for k in range(1, FT, 2):
                C.wait_filled(dve, ("t", 3, k))
                C.release(("t", 3, k), v.tensor_copy(tiled(YT[:, k, :]), C.blocks(("t", 3, k), NT, 128)))
            dve.wait_ge(sig("ld_aw"), 16)
            for n, pair in enumerate(PAIRS):
                row_bias(C, ("wx", n), pair, V, AW[:, 2:3, :])
            for n in range(3):
                C.wait_evacuated(dve, ("wx", n))
            dve.wait_ge(sig("ld_c"), 48)
            for t in range(NT):
                for half, dst in ((0, fcol), (1, gcol)):
                    dve_chain(dve, v.tensor_tensor(PROD[:, half, :], V[:, t, :], AW[:, half, :], ALU.mult))
                    last = v.tensor_reduce(dst[:, t, :], PROD[:, half, :].rearrange("p (h d) -> p h d", h=H3), AX.X, ALU.add)
            dve_chain(dve, last)
            v.tensor_tensor(fcol[:, :, :], fcol[:, :, :], ab[:, :].unsqueeze(1).to_broadcast([TILE, NT, H3]), ALU.add
                            ).then_inc(sig("fg_ready"), 1)

            def spread_g(h):
                if h >= 1:
                    C.wait_filled(dve, ("g", h - 1))
                v.tensor_copy(g_bc[:, :, :], gcol[:, :, h:h + 1].to_broadcast([TILE, NT, TILE])).then_inc(sig("g_spread"), 1)

            def output(h):
                C.wait_filled(dve, ("av", h))
                p0 = DH3 * (h % 2)
                C.release(("av", h), v.tensor_copy(halves(OT3[p0:p0 + DH3, h // 2, :]), C.halves(("av", h), DH3, p0)))

            spread_g(0)
            spread_g(1)
            for h in range(H3):
                for t in range(NT):
                    if t < NT - 1:
                        dve.wait_ge(sig("z_ready"), (NT - 1) * h + t + 1)
                    else:
                        C.wait_evacuated(dve, ("g", h))
                    z = P[:, h % 2, t, :]
                    dve_chain(dve, v.scalar_tensor_tensor(z, z, 0.2, z, ALU.mult, ALU.max))
                    v.tensor_tensor_reduce(out=z, in0=z, in1=LC[:, t, :], scale=-1.0, scalar=3.0e38, op0=ALU.add,
                                           op1=ALU.min, accum_out=negm[:, h % 2, t:t + 1]).then_inc(sig("leaky_done"), 1)
                if h + 2 < H3:
                    spread_g(h + 2)
                if h >= 1:
                    output(h - 1)
                dve.wait_ge(sig("exps_done3"), NT * (h + 1))
                dve_chain(dve, v.reciprocal(rinv[:, h % 2, :], psums[:, h % 2, :]))
                dve_chain(dve, v.tensor_tensor(rinv[:, h % 2, :], rinv[:, h % 2, :], has2[:, :], ALU.mult))
                for t in range(NT):
                    v.tensor_scalar(P[:, h % 2, t, :], P[:, h % 2, t, :], rinv[:, h % 2, t:t + 1], None,
                                    ALU.mult).then_inc(sig("probs_normalised3"), 1)
                for j in (1, 3):
                    C.wait_filled(dve, ("pt", h, j))
                    C.release(("pt", h, j), v.tensor_copy(tiled(PT[:, h % 2, j, :]), C.blocks(("pt", h, j), NT)))
            output(H3 - 1)
            block3_end = add_rows(C, "x", dve_chain, 0)

            norm(back, 2 * NT, X, block3_end, done=sig("out_ready"))

        @block.tensor
        def _(pe):
            mm = nc.tensor.matmul

            def wide(out_view, pairs, start=True):
                for place, lo in ((0, 0), (512, HALF_W)):
                    for n, (w, r) in enumerate(pairs):
                        last = mm(out_view[:, place:place + HALF_W], w, r[:, lo:lo + HALF_W],
                                  start=n == 0, stop=n == len(pairs) - 1)
                return last

            def columns(r, key, weight, moving, tiles=FT, p=128):
                r.claim(pe, key)
                r.fill(wide(r.view(key, p), [(weight(k), moving[:, k, :]) for k in range(tiles)]))

            def rows(r, key, pair, moving, weight, tiles=FT):
                r.claim(pe, key)
                for b, t in enumerate(pair):
                    for k in range(tiles):
                        last = mm(r.view(key)[:, 512 * b:512 * b + 512], moving[:, k, TILE * t:TILE * (t + 1)], weight[:, k, :],
                                  start=k == 0, stop=k == tiles - 1)
                r.fill(last)

            def tile_columns(r, key, src, k):
                r.claim(pe, key)
                for t in range(NT):
                    last = nc.tensor.transpose(r.view(key, 128)[:, 128 * t:128 * t + TILE], src[:, t, 128 * k:128 * (k + 1)],
                                               ident[0:TILE, 0:TILE])
                r.fill(last)

            def turn_tiles(r, key, tile):
                r.claim(pe, key)
                for t in range(NT):
                    last = nc.tensor.transpose(r.view(key)[:, 128 * t:128 * t + TILE], tile(t), ident[0:TILE, 0:TILE])
                r.fill(last)

            pe.sem_inc(sig("onehot_group_free"), 3)
            pe.sem_inc(sig("msg_group_free"), 3)
            B.open(pe)
            pe.wait_ge(sig("ld_fw"), 32)
            pe.wait_ge(sig("sin_ready"), 1)
            A.claim(pe, ("hid",))
            A.fill(wide(A.view(("hid",), COND), [(fw1[:, :], EMB)]))
            A.wait_evacuated(pe, ("hid",))
            A.claim(pe, ("cond",))
            A.fill(wide(A.view(("cond",), STACK), [(fw2[:, :], HIDC)]))
            pe.wait_ge(sig("ident_ready"), 1)
            pe.wait_ge(sig("xn_ready"), NT)
            for k in range(FT):
                tile_columns(A, ("t", k), XN, k)
            for k in range(FT):
                A.wait_evacuated(pe, ("t", k))
            pe.wait_ge(sig("ld_wqkv"), 16)
            for k in range(FT):
                columns(A, ("q", k), lambda c: WQKV[:, c, 128 * k:128 * (k + 1)], YT)
                columns(A, ("k", k), lambda c: WQKV[:, c, D + 128 * k:D + 128 * (k + 1)], YT)
            for n, pair in enumerate(PAIRS):
                rows(A, ("v", n), pair, YT, WQKV[:, :, 2 * D:3 * D])
            for key in (("k", FT - 1), ("v", 0), ("v", 1), ("v", 2)):
                A.wait_evacuated(pe, key)
            pe.wait_ge(sig("zeros_ready"), 1)

            def count_place(j):
                return ((512 * j, 0, 512), (2560 + 128 * j, 512, W))

            for b in range(7):
                mm(ps[0:TILE, 512 * b:512 * b + 512], zero16[:, 0:TILE], zero16[:, :], start=True, stop=True)
            pe.wait_ge(sig("mask_ready"), 1)

            def group_end(name):
                mm(ps[0:TILE, 3584:3584 + 64], zero16[:, 0:TILE], zero16[:, 0:64], start=True, stop=True).then_inc(sig(name), 1)

            with pe.Fori(0, GROUPS // 2) as i:
                for hf in range(2):
                    pe.wait_ge(sig("onehot_ready"), 2 * i + (hf + 1))
                    reached = pe.value_load(mask_i[0:1, bass.ds(2 * i + hf, 1)], min_val=0, max_val=(1 << NT) - 1)
                    for j in range(NT):
                        with pe.If((reached & (1 << j)) > 0):
                            for u in range(HALF * hf, HALF * hf + HALF):
                                for o, lo, hi in count_place(j):
                                    mm(ps[0:TILE, o:o + hi - lo], OH16[:, 0, u, TILE * j:TILE * (j + 1)], OH16[:, 1, u, lo:hi],
                                       start=False, stop=True, skip_group_check=True)
                    group_end("onehot_group_free")
            group_end("counts_done")
            pe.wait_ge(sig("counts_ready"), 1)
            for j in range(NT):
                for h in range(H0):
                    part = slice(DH0 * (h % 2), DH0 * (h % 2) + DH0)
                    key = ("s", j, h)
                    A.claim(pe, key)
                    A.fill(wide(A.view(key), [(KT[part, h // 2, TILE * j:TILE * (j + 1)], QT[part, h // 2, :])]))
            for h in range(H0 - 4, H0):
                A.wait_evacuated(pe, ("s", NT - 1, h))
            for b in range(6):
                mm(ps[0:TILE, 512 * b:512 * b + 512], zero16[:, 0:TILE], zero16[:, :], start=True, stop=True)
            with pe.Fori(0, GROUPS // 2) as i:
                for hf in range(2):
                    pe.wait_ge(sig("msg_ready"), 2 * i + (hf + 1))
                    reached = pe.value_load(mask_i[0:1, bass.ds(2 * i + hf, 1)], min_val=0, max_val=(1 << NT) - 1)
                    for j in range(NT):
                        with pe.If((reached & (1 << j)) > 0):
                            for u in range(HALF):
                                onehot = OHR[:, HALF * hf + u, TILE * j:TILE * (j + 1)]
                                for part in range(2):
                                    mm(ps[0:TILE, 512 * j:512 * j + 512], onehot, MSGR[:, HALF * hf + u, part, :],
                                       start=False, stop=True, skip_group_check=True)
                                mm(ps[0:TILE, 2560 + 2 * H0 * j:2560 + 2 * H0 * (j + 1)], onehot,
                                   PR[:, hf, u, :, :].rearrange("p k h -> p (k h)"), start=False, stop=True, skip_group_check=True)
                    group_end("msg_group_free")
            group_end("agg_done")
            pe.wait_ge(sig("agg_ready"), 1)
            for j in range(NT):
                turn_tiles(A, ("c1", j), lambda t: C2[:, t, TILE * j:TILE * (j + 1)])
            for k in range(FT):
                tile_columns(A, ("at", k), V, k)
            for k in range(FT):
                A.wait_evacuated(pe, ("at", k))
            pe.wait_ge(sig("ld_wo0"), 16)
            for n, pair in enumerate(PAIRS):
                rows(A, ("o", n), pair, YT, WO0)
            pe.wait_ge(sig("xn_ready"), 2 * NT)
            for k in range(FT):
                tile_columns(A, ("t2", k), XN, k)
            for k in range(FT):
                A.wait_evacuated(pe, ("t2", k))
            pe.wait_ge(sig("ld_wup0"), 16)
            for f in range(FF0):
                columns(A, ("up", f), lambda c: WUP0[:, c, 128 * f:128 * (f + 1)], YT)
            for f in range(FF0 - 4, FF0):
                A.wait_evacuated(pe, ("up", f))
            pe.wait_ge(sig("ld_wdown0"), 16)
            for n, pair in enumerate(PAIRS):
                rows(A, ("down", n), pair, HT0, WDN0, FF0)
            for n in range(3):
                A.wait_evacuated(pe, ("down", n))

            def attend_head(r, h):
                for j in range(NT):
                    turn_tiles(r, ("pt", h, j), lambda t: P[:, h % 2, t, TILE * j:TILE * (j + 1)])
                for j in range(NT - 4, NT):
                    r.wait_evacuated(pe, ("pt", h, j))

            pe.wait_ge(sig("padding_ready"), 1)

            with pe.Fori(0, LAYERS) as i:
                B.turn = i

                def make_conditioning(n):
                    for k in range(FT):
                        for q, name in ((2 * n - 2, "scale"), (2 * n - 1, "bias")):
                            key = (name, n, k)
                            B.claim(pe, key)
                            B.fill(wide(B.view(key, 128), [(condw[:, q, 128 * k:128 * (k + 1)], condT[:, :])]))

                def arrived(name):
                    pe.wait_ge(sig("ld_" + name), 16 * i + 16)

                def make_scores(h):
                    columns(B, ("q", h), lambda c: WQ[:, c, 128 * h:128 * (h + 1)], YT)
                    columns(B, ("k", h), lambda c: WK[:, c, 128 * h:128 * (h + 1)], YT)
                    B.wait_evacuated(pe, ("q", h))
                    B.wait_evacuated(pe, ("k", h))
                    for t in range(NT):
                        key = ("s", h, t)
                        B.claim(pe, key)
                        B.fill(wide(B.view(key), [(QT[:, h, TILE * t:TILE * (t + 1)], KT[:, h, :])]))

                def make_output(h):
                    pe.wait_ge(sig("probs_normalised"), H1 * NT * i + NT * (h + 1))
                    attend_head(B, h)
                    key = ("av", h)
                    B.claim(pe, key)
                    B.fill(wide(B.view(key, 128), [(V[:, j, 128 * h:128 * (h + 1)], PT[:, h % 2, j, :])
                                                   for j in range(NT)]))

                pe.wait_ge(sig("cond_parts_ready"), i + 1)
                make_conditioning(1)
                pe.wait_ge(sig("xn_ready1"), 2 * NT * i + NT)
                for k in range(FT):
                    tile_columns(B, ("t", 1, k), XN, k)
                for k in range(FT):
                    B.wait_evacuated(pe, ("t", 1, k))
                arrived("wq")
                arrived("wk")
                make_scores(0)
                make_scores(1)
                arrived("wv")
                for n, pair in enumerate(PAIRS):
                    rows(B, ("v", n), pair, YT, WV)
                for n in range(3):
                    B.wait_evacuated(pe, ("v", n))
                make_output(0)
                make_scores(2)
                make_output(1)
                make_scores(3)
                make_output(2)
                make_conditioning(2)
                make_output(3)
                B.wait_evacuated(pe, ("av", H1 - 1))
                arrived("wo")
                for n, pair in enumerate(PAIRS):
                    rows(B, ("o", n), pair, OT, WO)
                pe.wait_ge(sig("xn_ready1"), 2 * NT * i + 2 * NT)
                for k in range(FT):
                    tile_columns(B, ("t", 2, k), XN, k)
                for k in range(FT):
                    B.wait_evacuated(pe, ("t", 2, k))
                arrived("m1")
                for f in range(FT):
                    columns(B, ("m1", f), lambda c: M1[:, c, 128 * f:128 * (f + 1)], YT)
                for f in range(FT):
                    B.wait_evacuated(pe, ("m1", f))
                arrived("m2")
                for n, pair in enumerate(PAIRS):
                    rows(B, ("m2", n), pair, HT, M2)
            B.turn = LAYERS - 1
            for n in range(3):
                B.wait_evacuated(pe, ("m2", n))
            pe.wait_ge(sig("xn_ready3"), NT)
            for k in range(FT):
                tile_columns(C, ("t", 2, k), X, k)
            for k in range(FT):
                C.wait_evacuated(pe, ("t", 2, k))
            pe.wait_ge(sig("ld_c"), 48)
            columns(C, ("hid",), lambda c: cw1[:, c, :], YT, p=HID2)
            C.wait_evacuated(pe, ("hid",))
            for n, pair in enumerate(PAIRS):
                rows(C, ("h", n), pair, HID2T.unsqueeze(1), cw2[:, :].unsqueeze(1), 1)
            for n in range(3):
                C.wait_evacuated(pe, ("h", n))
            pe.wait_ge(sig("ld_c2"), 16)
            for n, pair in enumerate(PAIRS):
                rows(C, ("agg", n), pair, C2, V, NT)
            pe.wait_ge(sig("xn_ready3"), 2 * NT)
            for k in range(FT):
                tile_columns(C, ("t", 3, k), X, k)
            for k in range(FT):
                C.wait_evacuated(pe, ("t", 3, k))
            pe.wait_ge(sig("ld_ws3"), 16)
            for n, pair in enumerate(PAIRS):
                rows(C, ("wx", n), pair, YT, WS3)
            for n in range(3):
                C.wait_evacuated(pe, ("wx", n))

            def g_rows(h):
                key = ("g", h)
                C.claim(pe, key)
                pe.wait_ge(sig("g_spread"), h + 1)
                for t in range(NT):
                    last = nc.tensor.transpose(C.view(key)[:, 128 * t:128 * t + TILE], g_bc[:, t, :], ident[0:TILE, 0:TILE])
                C.fill(last)

            g_rows(0)
            for h in range(H3):
                if h + 1 < H3:
                    g_rows(h + 1)
                pe.wait_ge(sig("probs_normalised3"), NT * (h + 1))
                attend_head(C, h)
                key = ("av", h)
                C.claim(pe, key)
                C.fill(wide(C.view(key, DH3, DH3 * (h % 2)), [(V[:, j, DH3 * h:DH3 * (h + 1)], PT[:, h % 2, j, :])
                                                              for j in range(NT)]))
            for h in range(H3 - 4, H3):
                C.wait_evacuated(pe, ("av", h))
            for n, pair in enumerate(PAIRS):
                key = ("x", n)
                C.claim(pe, key)
                for b, t in enumerate(pair):
                    for k in range(FT):
                        last = nc.tensor.transpose(C.view(key)[:, 512 * b + 128 * k:512 * b + 128 * (k + 1)],
                                                   OT3[:, k, TILE * t:TILE * (t + 1)], ident[:, :])
                C.fill(last)


def kernel(**inputs):
    import numpy as np
    import concourse.bacc as bacc
    from concourse.bass_utils import run_bass_kernel_spmd

    g = {k: np.asarray(v) for k, v in inputs.items()}

    def cols_of(vec):
        vec = np.asarray(vec, np.float32).reshape(-1)
        n = -(-vec.size // 128)
        return np.concatenate([vec, np.zeros(n * 128 - vec.size, np.float32)]).reshape(n, 128).T

    L0, L1, L2, L3 = ({k[7:]: v for k, v in g.items() if k.startswith(f"L{b}_gnn_")} for b in range(4))

    def part_cols(parts):
        first = np.repeat([0.0 if p == 0 else -1.0 for p in parts], COND)
        second = np.repeat([-1.0 if p == 2 else 0.0 for p in parts], COND)
        return [cols_of(first), cols_of(second)]

    freq = np.arange(1, NFREQ + 1, dtype=np.float32) * np.float32(2.0 * np.pi / 16)
    zeros, ones = np.zeros(NFREQ, np.float32), np.ones(NFREQ, np.float32)
    parts = [cols_of(L0[k]) for k in ("ln1_g", "ln1_b", "ln2_g", "ln2_b")]
    parts += [cols_of(L0["bqkv"][:D]), cols_of(L0["bqkv"][D:2 * D]), cols_of(L0["b1"])]
    parts += [cols_of(L1["f_b1"]), cols_of(np.tile(L1["f_b2"], 6)), cols_of(L2["b1"])]
    parts += [cols_of(np.concatenate([freq, freq])), cols_of(np.concatenate([zeros, ones * np.float32(0.25)])),
              cols_of(np.concatenate([zeros, ones * np.float32(np.pi / 2)]))]
    parts += part_cols((0, 0, 1, 0, 2, 1)) + part_cols((0, 1, 0, 2, 0, 1))
    for layer in range(LAYERS):
        parts += [cols_of(L1[k][layer]) for k in ("s1_b", "b1_b", "bq", "bk", "s2_b", "b2_b", "m_b1")]
    cols = np.concatenate(parts, axis=1)
    f_w2 = np.tile(L1["f_w2"], (1, 6))
    cond_w = np.stack([L1[k] for k in ("s1_w", "b1_w", "s2_w", "b2_w")], axis=2).reshape(LAYERS, COND, 4 * D)
    cond_w = np.concatenate([cond_w, np.zeros((1, COND, 4 * D), np.float32)])

    def edges(a):
        return a.reshape(CHUNKS, TILE, -1).transpose(1, 0, 2).reshape(TILE, -1)

    arrays = dict(
        x=g["x"], src_t=edges(g["src"]), dst_t=edges(g["dst"]), attr_a=edges(g["edge_attr_8"]),
        attr_b=edges(g["edge_attr_8_n2"]), noise=g["node_vec1"], cols_d=cols,
        w_qkv=L0["Wqkv"], w_o0=L0["Wo"], w_up0=L0["W1"], w_down0=L0["W2"],
        rows0=np.stack([L0["bqkv"][2 * D:], L0["bo"], L0["b2"]]),
        f_w1=L1["f_w1"], f_w2=f_w2, cond_w=cond_w,
        wq=L1["wq"], wk=L1["wk"], wv=L1["wv"], wo=L1["wo"], m_w1=L1["m_w1"], m_w2=L1["m_w2"],
        rows1=np.stack([L1["bv"], L1["bo"], L1["m_b2"]]),
        c_w1=L2["W1"], c_w2=L2["W2"], c_b2=L2["b2"],
        ws3=L3["Ws"].transpose(1, 0, 2).reshape(D, H3 * DH3),
        rows3=np.stack([L3["a_w"][:, :DH3].reshape(-1), L3["a_w"][:, DH3:].reshape(-1), L3["Wb"].reshape(-1)]),
        ab3=L3["a_b"],
    )
    nc = bacc.Bacc("TRN2", target_bir_lowering=False, num_devices=1)
    args = {}
    for name, a in arrays.items():
        arrays[name] = a = np.ascontiguousarray(a)
        args[name] = nc.dram_tensor("in_" + name, a.shape, mybir.dt.from_np(a.dtype), kind="ExternalInput").ap()
    out = nc.dram_tensor("out", (NODES, D), mybir.dt.float32, kind="ExternalOutput").ap()
    build(nc, **args, out=out)
    ran = run_bass_kernel_spmd(nc, [{"in_" + n: a for n, a in arrays.items()}], core_ids=[0])
    return ran.results[0]["out"]
```

```python
import concourse.bass as bass
from concourse import mybir
from contextlib import ExitStack

NODES, EDGES, D = 625, 10000, 512
TILE = 125
NT = NODES // TILE
CHUNKS = EDGES // TILE
FT = D // 128
DH0, H0 = 64, 8
FF0 = 4 * D // 128
LAYERS, H1, DH1 = 4, 4, 128
COND, NFREQ = 16, 32
HID2 = 64
H3, DH3 = 8, 64
STACK = 6 * COND
EPS = 1e-5
BIG = 1.0e30
HALF = 4
GROUPS = CHUNKS // HALF
HALF_W = 314
W = 2 * HALF_W

COLS = {}
_n = 0
for _name, _width in (("ln1_g", FT), ("ln1_b", FT), ("ln2_g", FT), ("ln2_b", FT), ("bq", FT), ("bk", FT), ("b1", FF0),
                      ("f_b1", 1), ("f_b2", 1), ("c_b1", 1), ("freq", 1), ("turn", 1), ("angle", 1), ("part_c", 2), ("part_w", 2),
                      ("layers", LAYERS * 7 * FT)):
    COLS[_name] = _n
    _n += _width
NCOLS = _n
S1B, B1B, BQ, BK, S2B, B2B, MB1 = (FT * k for k in range(7))


class PsumRing:

    def __init__(self, ps, filled, evacuated, keys, opened=0):
        self.ps, self.filled, self.evacuated = ps, filled, evacuated
        self.order = {k: n for n, k in enumerate(keys)}
        self.total = len(self.order)
        self.turn = None
        self.opened = opened

    def view(self, key, p=TILE, p0=0):
        s = self.order[key] % 4
        return self.ps[p0:p0 + p, 1024 * s:1024 * s + 1024]

    def halves(self, key, p=TILE, p0=0):
        return self.view(key, p, p0).rearrange("p (b c) -> p b c", b=2)[:, :, 0:HALF_W]

    def blocks(self, key, n, p=TILE):
        return self.view(key, p).rearrange("p (b c) -> p b c", c=128)[:, 0:n, 0:TILE]

    def uses(self, s):
        return (self.total - s + 3) // 4

    def _value(self, local, per_turn):
        return local if self.turn is None else self.turn * per_turn + local

    def open(self, pe):
        for s in range(4):
            pe.sem_inc(self.evacuated[s], self.opened)

    def claim(self, pe, key):
        n = self.order[key]
        if n >= 4 or self.turn is not None:
            pe.wait_ge(self.evacuated[n % 4], self._value(n // 4 + self.opened, self.uses(n % 4)))

    def fill(self, matmul):
        matmul.then_inc(self.filled, 1)

    def wait_filled(self, eng, key):
        eng.wait_ge(self.filled, self._value(self.order[key] + 1, self.total))

    def release(self, key, instruction):
        instruction.then_inc(self.evacuated[self.order[key] % 4], 1)

    def wait_evacuated(self, eng, key):
        n = self.order[key]
        eng.wait_ge(self.evacuated[n % 4], self._value(n // 4 + 1 + self.opened, self.uses(n % 4)))


class Chain:

    def __init__(self, semaphore):
        self.semaphore, self.count, self.turn, self.per_turn = semaphore, 0, None, 0

    def __call__(self, eng, instruction):
        instruction.then_inc(self.semaphore, 1)
        self.count += 1
        eng.wait_ge(self.semaphore, self.count if self.turn is None else self.turn * self.per_turn + self.count)


def build(nc, x, src_t, dst_t, attr_a, attr_b, noise, cols_d,
          w_qkv, w_o0, w_up0, w_down0, rows0,
          f_w1, f_w2, cond_w, wq, wk, wv, wo, m_w1, m_w2, rows1,
          c_w1, c_w2, c_b2, ws3, rows3, ab3, out):
    f32, bf16, f16 = mybir.dt.float32, mybir.dt.bfloat16, mybir.dt.float16
    i32 = mybir.dt.int32
    ALU, ACT, AX = mybir.AluOpType, mybir.ActivationFunctionType, mybir.AxisListType

    logits_d = nc.dram_tensor("logits_scratch", (NODES * NODES, H0), f32, kind="Internal").ap()
    v0_d = nc.dram_tensor("value_scratch", (NODES, D), f32, kind="Internal").ap()
    c2_d = nc.dram_tensor("counts_scratch", (TILE, NT * W), f32, kind="Internal").ap()
    x1_d = nc.dram_tensor("block_input_scratch", (NODES, D), f32, kind="Internal").ap()

    with ExitStack() as ctx:
        def sem(name):
            return ctx.enter_context(nc.semaphore(name))

        def sbuf(name, shape, dt=f32):
            return ctx.enter_context(nc.sbuf_tensor(name, shape, dt))

        ARENA_WORDS = 48030
        arena = sbuf("arena", [128, ARENA_WORDS])
        arena_at = nc.sbuf_base - 4 * ARENA_WORDS

        def over(name, offset, shape, dt):
            return nc.alloc_sbuf_tensor_at(name, shape, dt, offset=arena_at + 4 * offset)

        def at(offset, *dims, p=128, p0=0):
            size = 1
            for d in dims:
                size *= d
            flat = arena[p0:p0 + p, offset:offset + size]
            if len(dims) == 1:
                return flat
            names = "abcd"[:len(dims)]
            return flat.rearrange("p (" + " ".join(names) + ") -> p " + " ".join(names), **dict(zip(names, dims)))

        def halves(row):
            return row.rearrange("p (b c) -> p b c", b=2)

        def tiled(row):
            return row[:, 0:row.shape[1] // TILE * TILE].rearrange("p (b c) -> p b c", c=TILE)

        R_X, R_Y, R_V, R_Q, R_K, R_O = (2560 * k for k in range(6))
        R_P = 15360
        R_PT = R_P + 2 * NT * W
        R_LC = R_PT + 2 * NT * W
        R_C = R_LC + NT * W
        R_W = R_C + NT * W
        R_B = R_W + 6 * FT * D

        X = at(R_X, NT, D, p=TILE)
        YT = at(R_Y, FT, W)
        V = at(R_V, NT, D, p=TILE)
        XN = V
        QT = at(R_Q, FT, W)
        KT = at(R_K, FT, W)
        OT = at(R_O, FT, W)
        P = at(R_P, 2, NT, W, p=TILE)
        PT = at(R_PT, 2, NT, W, p=TILE)
        LC = at(R_LC, NT, W, p=TILE)
        C2 = at(R_C, NT, W, p=TILE)
        ROWS = at(R_B, 3, D, p=TILE)
        WQKV = at(R_P, FT, 3 * D)
        STAGE = [at(R_P + 6144, NODES, H0, p=TILE), at(R_W, NODES, H0, p=TILE)]
        MASK = at(R_W + 5000, NT, W, p=TILE)
        WO0 = at(R_W + 8192, FT, D)
        TEMP = at(R_W + 10240, 3, W, p=TILE)
        ATTR = at(R_LC, 2, CHUNKS * H0, p=TILE)
        KTZ = at(R_K, 2, FT, W)
        OH16 = at(R_LC + 1280, 4 * HALF * W, p=TILE).bitcast(bf16).rearrange("p (k r n) -> p k r n", k=2, r=4 * HALF)
        f32r = mybir.dt.float32r
        OHR = over("onehot_r", R_Q, [TILE, 2 * HALF, W], f32r)
        MSGR = over("messages_r", R_W, [TILE, 2 * HALF, 2, D], f32r)
        PR = over("edge_probs_r", R_O, [TILE, 2, HALF, 2, H0], f32r)
        FLAGS = at(R_P + 6144 + NODES * H0, NT, CHUNKS, p=TILE)
        VG = [at(R_P + HALF * D * r, HALF, D, p=TILE) for r in range(3)] + [at(R_Y, HALF, D, p=TILE)]
        HT0 = at(R_V, FF0, W)
        UP_CHUNKS = FF0 // 4
        UPW = [at(R_P + 2 * FT * D * n, FT, D) for n in range(2)]
        UPL = [over(f"up_low{n}", R_P + 2 * FT * D * n, [128, FT, D], f32r) for n in range(2)]
        UPH = [over(f"up_high{n}", R_P + 2 * FT * D * n + FT * D, [128, FT, D], f32r) for n in range(2)]
        YH0 = over("up_input_high", R_P + 4 * FT * D, [128, FT, W], f32r)
        DNW = [at(R_W + 2 * FT * D * n, FT, D) for n in range(2)]
        DNL = [over(f"down_low{n}", R_W + 2 * FT * D * n, [128, FT, D], f32r) for n in range(2)]
        DNH = [over(f"down_high{n}", R_W + 2 * FT * D * n + FT * D, [128, FT, D], f32r) for n in range(2)]
        HL0 = [over(f"hidden0_low{n}", R_V + 4 * W * n, [128, 4, W], f32r) for n in range(4)]
        HH0 = [over(f"hidden0_high{n}", R_P + 4 * W * n, [128, 4, W], f32r) for n in range(4)]
        EARLY = 6
        SLOT = {"wq": 2, "wk": 0, "wv": 1, "wo": 2, "m1": 0, "m2": 1}
        WEIGHT = [at(R_W + 2 * FT * D * n, FT, D) for n in range(3)]
        WLOW = [over(f"weight_low{n}", R_W + 2 * FT * D * n, [128, FT, D], f32r) for n in range(3)]
        WHIGH = [over(f"weight_high{n}", R_W + 2 * FT * D * n + FT * D, [128, FT, D], f32r) for n in range(3)]
        YL, YH = over("input_low", R_Y, [128, FT, W], f32r), over("input_high", R_PT, [128, FT, W], f32r)
        QL, KL = over("query_low", R_Q, [128, FT, W], f32r), over("key_low", R_K, [128, FT, W], f32r)
        QH, KH = (over(name, R_C + 4 + 2 * W * n, [128, 2, W], f32r) for n, name in enumerate(("query_high", "key_high")))
        OL, OH = over("attended_low", R_O, [128, FT, W], f32r), over("attended_high", R_Y, [128, FT, W], f32r)
        HL, HH = over("hidden_low", R_Q, [128, FT, W], f32r), over("hidden_high", R_K, [128, FT, W], f32r)
        SC = KT
        BI = {1: OT, 2: QT}
        HT = QT
        XIN = at(R_O, NT, D, p=TILE)
        WS3 = at(R_W, FT, D)
        OT3 = at(R_O, FT, W)
        PROD = at(R_K, D, p=TILE)
        PRODG = at(R_Q, NT, D, p=TILE)
        HID2T = at(R_Q, W, p=HID2)
        g_bc = at(R_K + 2 * D, NT, TILE, p=TILE)
        AW = at(R_W + 5 * FT * D, 3, D, p=TILE)

        cols = sbuf("cols", [128, NCOLS])
        cols1 = sbuf("cols_plus_one", [128, LAYERS * 7 * FT])
        ident = sbuf("ident", [128, 128])
        iota16 = sbuf("iota_row", [128, W], f16)
        src_i = sbuf("src_idx", [TILE, CHUNKS], i32)
        dst_i = sbuf("dst_idx", [TILE, CHUNKS], i32)
        src_f = sbuf("src_f", [TILE, CHUNKS])
        dst_f = sbuf("dst_f", [TILE, CHUNKS])
        pair_f = sbuf("pair_f", [TILE, CHUNKS])
        pair_i = sbuf("pair_idx", [TILE, CHUNKS], i32)
        idx_ring = sbuf("idx_ring", [TILE, 4, 2, HALF], i32)
        lg_ring = sbuf("logit_ring", [TILE, 4, HALF * H0])
        sum_ring = sbuf("edge_logits", [TILE, 2, HALF * H0])
        p_ring = sbuf("edge_probs", [TILE, 2, HALF * H0])
        gmax = sbuf("attr_max", [TILE, 2])
        zero16 = sbuf("zero16", [1, 512], bf16)
        stats = sbuf("bn_stats", [TILE, NT, 6])
        mv = sbuf("mean_var", [TILE, NT, 2])
        rstd = sbuf("rstd", [TILE, NT])
        vare = sbuf("var_eps", [TILE, NT])
        lnc = sbuf("ln_consts", [TILE, 2])
        negm = sbuf("neg_max", [TILE, 2, NT])
        psums = sbuf("prob_sums", [TILE, 2, NT])
        rinv = sbuf("prob_rinv", [TILE, 2, NT])
        has1 = sbuf("has_edge_src", [TILE, NT])
        has2 = sbuf("has_edge_dst", [TILE, NT])
        negm0 = sbuf("neg_max0", [TILE, 3])
        den = sbuf("den", [TILE, NT, H0])
        rden = sbuf("rden", [TILE, NT, H0])
        condT = sbuf("cond_parts", [STACK, W], bf16)
        condw = sbuf("cond_weight_parts", [STACK, 4, D], bf16)
        tid = sbuf("dst_tile", [TILE, CHUNKS])
        gflag = sbuf("group_flags", [TILE, 2, NT * GROUPS])
        mask_f = sbuf("group_mask_f", [1, GROUPS])
        mask_i = sbuf("group_mask", [1, GROUPS], i32)
        fw1 = sbuf("f_w1", [2 * NFREQ, COND])
        fw2 = sbuf("f_w2", [COND, STACK])
        cw1 = sbuf("c_w1", [128, FT, HID2])
        cw2 = sbuf("c_w2", [HID2, D])
        fcol = sbuf("f_cols", [TILE, NT, H3])
        gcol = sbuf("g_cols", [TILE, NT, H3])
        rinv3 = sbuf("prob_rinv3", [TILE, NT, H3])
        ab = sbuf("ab3", [TILE, H3])
        NOISE, PHASE, TURNS, EMB = (at(R_P + 6144 + 640 * k, W, p=2 * NFREQ) for k in range(4))
        HIDC = at(R_P + 6144 + 640 * 4, W, p=COND)
        CONDF = at(R_P + 6144 + 640 * 5, W, p=STACK)
        CONDH = at(R_P + 6144 + 640 * 6, W // 2, p=STACK).bitcast(bf16)
        RAW = at(R_C, 4 * D, p=STACK)
        RAWH = at(R_C + 4 * D, 2 * D, p=STACK).bitcast(bf16)
        LTMP = {"lc_half": at(R_W + 8192, NT, W, p=TILE), "lc2_half": at(R_P + 8192, NT, W, p=TILE)}
        XIN0 = at(R_Y, NT, D, p=TILE)
        ps = ctx.enter_context(nc.psum_tensor("ps", [128, 4096], f32))

        S = {}

        def sig(name):
            if name not in S:
                S[name] = sem(name)
            return S[name]

        def ring(name, keys, opened=0):
            return PsumRing(ps, sig(name + "_filled"), [sig(f"{name}_evacuated{s}") for s in range(4)], keys, opened)

        PAIRS = [(0, 1), (2, 3), (4,)]
        A = ring("front", [("t", k) for k in range(FT)]
                 + [(n, k) for k in range(FT - 1) for n in "qk"]
                 + [("hid",), ("q", FT - 1), ("k", FT - 1), ("cond",)]
                 + [("v", n) for n in range(3)]
                 + [("s", j, h) for j in range(NT) for h in range(H0)]
                 + [("at", k) for k in range(FT)] + [("o", n) for n in range(3)]
                 + [("c1", j) for j in range(NT)]
                 + [("t2", k) for k in range(FT)]
                 + [("up", f) for f in range(FF0)] + [("down", n) for n in range(3)])

        def turned(h):
            return [("pt", h, j) for j in range(NT)]

        def scores(h):
            return [("s", h, t) for t in range(NT)]

        def conditioning(n, tiles=range(FT)):
            return [(name, n, k) for k in tiles for name in ("scale", "bias")]

        B = ring("layer", conditioning(1) + [("t", 1, k) for k in range(FT)]
                 + [("q", 0), ("k", 0), ("q", 1), ("k", 1)] + scores(0) + [("q", 2), ("k", 2)] + scores(1)
                 + [("q", 3), ("k", 3)] + [("v", n) for n in range(3)]
                 + turned(0) + scores(2) + [("av", 0)] + turned(1) + scores(3) + [("av", 1)]
                 + turned(2) + conditioning(2, (0, 1)) + [("av", 2)] + turned(3) + conditioning(2, (2, 3)) + [("av", 3)]
                 + [("o", n) for n in range(3)]
                 + [("t", 2, k) for k in range(FT)]
                 + [("m1", f) for f in range(FT)] + [("m2", n) for n in range(3)], opened=1)

        C = ring("back", [("t", 2, k) for k in range(FT)] + [("hid",)] + [("h", n) for n in range(3)]
                 + [("agg", n) for n in range(3)]
                 + [("t", 3, k) for k in range(FT)] + [("wx", n) for n in range(3)]
                 + [("g", 0), ("g", 1)]
                 + [k for h in range(H3) for k in turned(h) + [("av", h)] + ([("g", h + 2)] if h + 2 < H3 else [])]
                 + [("x", n) for n in range(3)])

        dve_chain, pool_chain = Chain(sig("dve_chain")), Chain(sig("pool_chain"))
        dve_loop_chain, pool_loop_chain = Chain(sig("dve_loop_chain")), Chain(sig("pool_loop_chain"))

        block = ctx.enter_context(nc.Block())

        def part_wait(eng, name):
            eng.sem_inc(sig("parted_" + name), 1)

        def rows_view(dram):
            return dram.rearrange("(t p) n -> p t n", p=TILE)

        def feat_view(dram):
            return dram.rearrange("(k p) n -> p k n", p=128)

        @block.sync
        def _(sp):
            def load(dst, src, name):
                sp.dma_start(dst, src).then_inc(sig("ld_" + name), 16)

            def node_transfer(dst, src, name):
                for part in (slice(0, 112), slice(112, TILE)):
                    sp.dma_start(dst[part], src[part]).then_inc(sig(name), 16)

            node_transfer(X, rows_view(x), "ld_x")
            load(cols[:, :], cols_d, "cols")
            load(src_i[:, :], src_t, "idx")
            load(dst_i[:, :], dst_t, "idx")
            load(WQKV, feat_view(w_qkv), "wqkv")
            load(NOISE[:, 0:NODES], noise.rearrange("n o -> o n").partition_broadcast(2 * NFREQ), "noise")
            load(fw1[:, :], f_w1, "fw")
            load(fw2[:, :], f_w2, "fw")
            load(ROWS, rows0.partition_broadcast(TILE), "rows0")
            load(ATTR[:, 0, :], attr_a, "attr")
            load(ATTR[:, 1, :], attr_b, "attr")
            load(WO0, feat_view(w_o0), "wo0")
            load(cw1[:, :, :], feat_view(c_w1), "c")
            load(cw2[:, :], c_w2, "c")
            load(ab[:, :], ab3.partition_broadcast(TILE), "c")
            for n in range(3):
                A.wait_evacuated(sp, ("v", n))
            node_transfer(rows_view(v0_d), V, "v0_stored")
            lg_v = logits_d.rearrange("(j p s) h -> j p (s h)", j=NT, p=TILE)
            for j in range(NT):
                sp.wait_ge(sig("stage_ready"), H0 * (j + 1))
                node_transfer(lg_v[j], STAGE[j % 2].rearrange("p s h -> p (s h)"), f"stage_stored{j % 2}")
            sp.wait_ge(sig("agg_done"), 1)

            def load_up(c):
                load(UPW[c % 2], feat_view(w_up0)[:, :, D * c:D * (c + 1)], f"up{c % 2}")

            load_up(0)
            load_up(1)

            def load_down(c):
                load(DNW[c % 2], feat_view(w_down0)[:, 4 * c:4 * (c + 1), :], f"down{c % 2}")

            load_down(0)
            load_down(1)
            sp.wait_ge(sig("counts_ready"), 1)
            node_transfer(c2_d, at(R_C, NT * W, p=TILE), "counts_stored")
            A.wait_filled(sp, ("o", 2))
            w_of = {"wq": wq, "wk": wk, "wv": wv, "wo": wo, "m1": m_w1, "m2": m_w2}

            def load_weight(name, layer):
                load(WEIGHT[SLOT[name]], w_of[name][layer].rearrange("a (k p) n -> p (a k) n", p=128), name)

            def load_row(n, layer):
                load(ROWS[:, n, :], rows1[n, layer, :].partition_broadcast(TILE), f"row{n}")

            for c in range(2, UP_CHUNKS):
                A.wait_filled(sp, ("up", 4 * (c - 2) + 3))
                load_up(c)
            A.wait_filled(sp, ("up", FF0 - 1))
            sp.wait_ge(sig("hidden0_low"), 1)
            node_transfer(XIN0, rows_view(x), "ld_x0")
            sp.wait_ge(sig("down_chunk_done"), 1)
            load_down(2)
            sp.wait_ge(sig("lc_ready"), 1)
            load_weight("wq", slice(0, 1))
            sp.wait_ge(sig("down_chunk_done"), 2)
            load_down(3)
            A.wait_filled(sp, ("down", 2))
            sp.wait_ge(sig("residual_biased"), 2)
            for name in ("wk", "wv"):
                load_weight(name, slice(0, 1))
            for n in range(3):
                load_row(n, slice(0, 1))
            sp.wait_ge(sig("x1_ready"), NT)
            node_transfer(rows_view(x1_d), X, "x1_stored")
            def later_weights(now):
                B.wait_filled(sp, ("k", 3))
                load_weight("wo", now)
                load_weight("m1", now)
                B.wait_filled(sp, ("v", 2))
                load_weight("m2", now)

            with sp.Fori(0, LAYERS - 1) as i:
                B.turn = i
                nxt = bass.ds(i + 1, 1)
                later_weights(bass.ds(i, 1))
                B.wait_evacuated(sp, ("v", 2))
                load_row(0, nxt)
                sp.wait_ge(sig("residual_biased1"), 2 * i + 1)
                load_row(1, nxt)
                B.wait_filled(sp, ("o", 2))
                load_weight("wq", nxt)
                B.wait_filled(sp, ("m1", FT - 1))
                load_weight("wk", nxt)
                sp.wait_ge(sig("residual_biased1"), 2 * i + 2)
                load_row(2, nxt)
                B.wait_filled(sp, ("m2", 2))
                load_weight("wv", nxt)
            B.turn = LAYERS - 1
            later_weights(slice(LAYERS - 1, LAYERS))
            B.wait_evacuated(sp, ("v", 2))
            load(ROWS[:, 0, :], c_b2.partition_broadcast(TILE), "rows3")
            B.wait_filled(sp, ("o", 2))
            load_weight("wq", slice(LAYERS - 1, LAYERS))
            sp.wait_ge(sig("x1_stored"), 32)
            node_transfer(XIN, rows_view(x1_d), "ld_x1")
            sp.wait_ge(sig("cond_parts_ready"), LAYERS + 1)
            node_transfer(at(R_C, NT * W, p=TILE), c2_d, "ld_c2")
            sp.wait_ge(sig("wq_low"), LAYERS + 1)
            load(AW, rows3.partition_broadcast(TILE), "aw")
            B.wait_filled(sp, ("m1", FT - 1))
            load_weight("wk", slice(LAYERS - 1, LAYERS))
            sp.wait_ge(sig("wk_low"), LAYERS + 1)
            load(WS3, feat_view(ws3), "ws3")
            sp.wait_ge(sig("out_ready"), NT)
            node_transfer(rows_view(out), X, "out_stored")
            sp.wait_ge(sig("out_stored"), 32)

        @block.gpsimd
        def _(pool):
            g = nc.gpsimd
            g.memset(zero16[:, :], 0.0).then_inc(sig("zeros_ready"), 1)
            g.memset(lnc[:, 0:1], EPS)
            g.memset(lnc[:, 1:2], -0.5)
            g.iota(iota16[:, :], pattern=[[1, W]], base=0, channel_multiplier=0,
                   allow_small_or_imprecise_dtypes=True).then_inc(sig("iota_ready"), 1)
            pool_chain(pool, g.memset(ident[:, :], 0.0))
            g.affine_select(out=ident[:, :], in_=ident[:, :], compare_op=ALU.not_equal, fill=1.0, base=0,
                            pattern=[[-1, 128]], channel_multiplier=1).then_inc(sig("ident_ready"), 1)

            def powers(sems, chain, base):
                var_ready, rstd_ready = sems
                for t in range(NT):
                    pool.wait_ge(var_ready, base + t + 1)
                    chain(pool, g.tensor_tensor(vare[:, t:t + 1], mv[:, t, 1:2], lnc[:, 0:1], ALU.add))
                    g.tensor_tensor(rstd[:, t:t + 1], vare[:, t:t + 1], lnc[:, 1:2], ALU.pow).then_inc(rstd_ready, 1)

            front = (sig("var_ready"), sig("rstd_ready"))
            powers(front, pool_chain, 0)
            pool.wait_ge(sig("gmax_part"), 1)
            g.partition_all_reduce(gmax[:, 1:2], gmax[:, 0:1], TILE, bass.bass_isa.ReduceOp.max).then_inc(sig("gmax_all"), 1)
            pool.wait_ge(sig("flags_part"), 1)
            g.partition_all_reduce(gflag[:, 1, :], gflag[:, 0, :], TILE, bass.bass_isa.ReduceOp.max).then_inc(sig("flags_all"), 1)
            pool.wait_ge(sig("xn_ready"), NT)
            pool.wait_ge(sig("ld_rows0"), 16)
            g.tensor_tensor(X, X, ROWS[:, 1:2, :].to_broadcast([TILE, NT, D]), ALU.add).then_inc(sig("residual_biased"), 1)
            def gather(dst, table, name, index):
                for u in range(HALF):
                    g.indirect_dma_start(dst(u), None, table, bass.IndirectOffsetOnAxis(ap=index(u), axis=0)
                                         ).then_inc(sig(name), 16)

            def gather_values(half, index):
                gather(lambda u: VG[half % 4][:, u, :], v0_d, f"values_gathered{half % 4}", index)

            def gather_logits(half, index):
                gather(lambda u: lg_ring[:, half % 4, u * H0:(u + 1) * H0], logits_d, f"logits_gathered{half % 4}", index)

            pool.wait_ge(sig("v0_stored"), 32)
            pool.wait_ge(sig("ld_idx"), 32)
            for half in range(4):
                gather_values(half, lambda u: src_i[:, HALF * half + u:HALF * half + u + 1])
            pool.wait_ge(sig("pairs_ready"), 1)
            for j in range(2):
                pool.wait_ge(sig(f"stage_stored{j}"), 32 * ((NT + 1 - j) // 2))
            gather_logits(0, lambda u: pair_i[:, u:u + 1])
            g.tensor_copy(idx_ring[:, 1, 1, :], pair_i[:, HALF:2 * HALF]).then_inc(sig("idx_copied"), 1)
            pool.wait_ge(sig("idx_copied"), 1)
            with pool.Fori(0, GROUPS // 4 - 1) as i:
                for m in range(1, 5):
                    r, ahead = m % 4, (m + 3) % 4
                    gather_logits(r, lambda u: idx_ring[:, r, 1, u:u + 1])
                    pool.wait_ge(sig("gather_slot_free"), 4 * i + m)
                    g.tensor_copy(idx_ring[:, ahead, 0, :], src_i[:, bass.ds(4 * HALF * i + HALF * (m + 3), HALF)])
                    g.tensor_copy(idx_ring[:, (r + 1) % 4, 1, :], pair_i[:, bass.ds(4 * HALF * i + HALF * (m + 1), HALF)]
                                  ).then_inc(sig("idx_copied"), 1)
                    pool.wait_ge(sig("idx_copied"), 4 * i + (m + 1))
                    part_wait(pool, "pool")
                    gather_values(ahead, lambda u: idx_ring[:, ahead, 0, u:u + 1])
            for half in range(GROUPS - 3, GROUPS):
                gather_logits(half, lambda u: pair_i[:, HALF * half + u:HALF * half + u + 1])
            powers(front, pool_chain, NT)
            pool.wait_ge(sig("xn_ready"), 2 * NT)
            g.tensor_tensor(X, X, ROWS[:, 2:3, :].to_broadcast([TILE, NT, D]), ALU.add).then_inc(sig("residual_biased"), 1)
            pool.wait_ge(sig("counts_stored"), 32)
            A.wait_filled(pool, ("c1", NT - 1))
            for q in range(6):
                pool.dma_start(RAW[COND * q:COND * (q + 1), :], cond_w[0, :, :]).then_inc(sig("ld_raw"), 16)
            powers(front, pool_chain, 2 * NT)
            def load_raw(layer):
                for q in range(6):
                    pool.dma_start(RAW[COND * q:COND * (q + 1), :], cond_w[layer, :, :].rearrange("a c n -> (a c) n")
                                   ).then_inc(sig("ld_raw"), 16)

            pool.wait_ge(sig("x1_stored"), 32)
            with pool.Fori(0, LAYERS) as i:
                B.turn = i
                pool_loop_chain.turn, pool_loop_chain.per_turn = i, 2 * NT
                for n in (1, 2):
                    powers((sig("var_ready1"), sig("rstd_ready1")), pool_loop_chain, 2 * NT * i + NT * (n - 1))
                    for k in range(0, FT, 2):
                        B.wait_evacuated(pool, ("bias", n, k))
                        B.wait_evacuated(pool, ("t", n, k))
                        g.tensor_tensor(YT[:, k, 0:NODES], YT[:, k, 0:NODES], BI[n][:, k, 0:NODES], ALU.add
                                        ).then_inc(sig("input_even"), 1)
                    pool.wait_ge(sig("xn_ready1"), 2 * NT * i + NT * n)
                    pool.wait_ge(sig(f"ld_row{n}"), 16 * i + 16)
                    g.tensor_tensor(X, X, ROWS[:, n:n + 1, :].to_broadcast([TILE, NT, D]), ALU.add
                                    ).then_inc(sig("residual_biased1"), 1)
                    if n == 1:
                        B.wait_filled(pool, ("s", 3, NT - 1))
                        pool.wait_ge(sig("cond_parts_ready"), i + 1)
                        load_raw(bass.ds(i + 1, 1))
            assert pool_loop_chain.count == pool_loop_chain.per_turn
            for n in range(2):
                powers((sig("var_ready3"), sig("rstd_ready3")), pool_chain, n * NT)
            pool.wait_ge(sig("ld_aw"), 16)
            for n, pair in enumerate(PAIRS):
                C.wait_evacuated(pool, ("wx", n))
                for t in pair:
                    g.tensor_tensor(PRODG[:, t, :], V[:, t, :], AW[:, 1, :], ALU.mult).then_inc(sig("g_products"), 1)
            pool.wait_ge(sig("fg_ready"), 1)
            for h in range(H3):
                if h >= 1:
                    C.wait_filled(pool, ("g", h - 1))
                g.tensor_copy(g_bc[:, :, :], gcol[:, :, h:h + 1].to_broadcast([TILE, NT, TILE])).then_inc(sig("g_spread"), 1)
            powers((sig("var_ready3"), sig("rstd_ready3")), pool_chain, 2 * NT)

        @block.scalar
        def _(act):
            a = nc.scalar

            def col(name, k=0, p=128):
                return cols[0:p, COLS[name] + k:COLS[name] + k + 1]

            def tile_norm(k, gain, offset, name):
                A.wait_filled(act, (name, k))
                A.release((name, k), a.activation(tiled(YT[:, k, :]), A.blocks((name, k), NT, 128), ACT.Identity,
                                                  bias=col(offset, k), scale=col(gain, k)))

            def keys(k):
                A.wait_filled(act, ("k", k))
                for parity in range(2):
                    part = slice(DH0 * parity, DH0 * parity + DH0)
                    last = a.activation(halves(KTZ[part, parity, k, :]), A.halves(("k", k), DH0, DH0 * parity), ACT.Identity,
                                        bias=cols[part, COLS["bk"] + k:COLS["bk"] + k + 1])
                A.release(("k", k), last)

            act.wait_ge(sig("ld_cols"), 16)
            for k in range(0, FT, 2):
                tile_norm(k, "ln1_g", "ln1_b", "t")
            act.wait_ge(sig("emb_ready"), 1)
            a.activation(EMB, TURNS, ACT.Sin).then_inc(sig("sin_ready"), 1)
            for k in range(FT - 1):
                keys(k)
            A.wait_filled(act, ("hid",))
            act.wait_ge(sig("sin_ready"), 1)
            A.release(("hid",), a.activation(halves(HIDC), A.halves(("hid",), COND), ACT.Silu, bias=col("f_b1", 0, COND)))
            keys(FT - 1)
            A.wait_filled(act, ("cond",))
            A.release(("cond",), a.activation(halves(CONDF), A.halves(("cond",), STACK), ACT.Identity,
                                              bias=col("f_b2", 0, STACK)))
            A.wait_evacuated(act, ("cond",))
            a.activation(CONDH, CONDF, ACT.Copy).then_inc(sig("cond_high"), 1)
            act.wait_ge(sig("cond_rest"), 1)
            a.activation(CONDH, CONDF, ACT.Copy).then_inc(sig("cond_high"), 1)
            for n in range(NT * H0):
                j, h = divmod(n, H0)
                A.wait_evacuated(act, ("s", j, h))
                if h == 0 and j >= 2:
                    act.wait_ge(sig(f"stage_stored{j % 2}"), 32 * (j // 2))
                a.activation(STAGE[j % 2][:, :, h], TEMP[:, n % 3, 0:NODES], ACT.Identity, scale=-1.0,
                             bias=negm0[:, n % 3:n % 3 + 1]).then_inc(sig("stage_ready"), 1)
            def one_weight_high(name, weight, n):
                act.wait_ge(sig("ld_" + name), 16)
                a.activation(WHIGH[n][:, :, :], weight, ACT.Copy).then_inc(sig("lone_weight_high"), 1)

            act.wait_ge(sig("stage_ready"), NT * H0)
            one_weight_high("wo0", WO0, 2)
            with act.Fori(0, GROUPS // 4) as i:
                for r in range(4):
                    hf, half = r % 2, 4 * i + r
                    act.wait_ge(sig("edge_logits_ready"), half + 1)
                    a.activation(p_ring[:, hf, :], sum_ring[:, hf, :], ACT.Exp).then_inc(sig("edge_probs_ready"), 1)
                    act.wait_ge(sig("msg_group_free"), half + 2)
                    act.wait_ge(sig("edge_probs_ready"), half + 1)
                    a.activation(PR[:, hf, :, 0, :], p_ring[:, hf, :].rearrange("p (u h) -> p u h", u=HALF), ACT.Copy
                                 ).then_inc(sig("edge_probs_high"), 1)
                    for u in range(HALF):
                        act.wait_ge(sig("msg_full"), 4 * HALF * i + (HALF * r + u + 1))
                        a.activation(MSGR[:, HALF * hf + u, 0, :], VG[r][:, u, :], ACT.Copy).then_inc(sig("msg_high"), 1)
            for k in range(FT):
                A.wait_filled(act, ("at", k))
                a.activation(tiled(OH[:, k, :]), A.blocks(("at", k), NT, 128), ACT.Copy).then_inc(sig("evacuated_high"), 1)
            def up_high(c):
                act.wait_ge(sig(f"ld_up{c % 2}"), 16 * (c // 2 + 1))
                a.activation(UPH[c % 2][:, :, :], UPW[c % 2], ACT.Copy).then_inc(sig("up_high"), 1)

            up_high(0)
            up_high(1)
            for j in range(NT):
                A.wait_filled(act, ("c1", j))
                A.release(("c1", j), a.activation(tiled(LC[:, j, :]), A.blocks(("c1", j), NT), ACT.Copy))
            for k in range(0, FT, 2):
                tile_norm(k, "ln2_g", "ln2_b", "t2")
            for k in range(FT):
                A.wait_evacuated(act, ("t2", k))
                a.activation(YH0[:, k, :], YT[:, k, :], ACT.Copy).then_inc(sig("mlp_high"), 1)

            def down_high(c):
                act.wait_ge(sig(f"ld_down{c % 2}"), 16 * (c // 2 + 1))
                a.activation(DNH[c % 2][:, :, :], DNW[c % 2], ACT.Copy).then_inc(sig("down_high"), 1)

            def hidden_high(f):
                A.wait_filled(act, ("up", FF0 - 5 if f < EARLY else FF0 - 1))
                A.wait_evacuated(act, ("up", f))
                a.activation(HH0[f // 4][:, f % 4, :], HT0[:, f, :], ACT.Copy).then_inc(sig("mlp_high"), 1)

            for f in range(FF0):
                A.wait_filled(act, ("up", f))
                A.release(("up", f), a.activation(halves(HT0[:, f, :]), A.halves(("up", f), 128), ACT.Gelu,
                                                  bias=col("b1", f)))
                if f % 4 == 1 and 1 < f // 4 + 1 < UP_CHUNKS:
                    up_high(f // 4 + 1)
                if f in (3, 7):
                    down_high(f // 4)
                if f >= 13:
                    for m in range(EARLY // 3 * (f - 13), EARLY // 3 * (f - 12)):
                        hidden_high(m)
            for f in range(EARLY, FF0):
                hidden_high(f)

            act.wait_ge(sig("lc_half"), 1)
            a.activation(LC, LC, ACT.Ln).then_inc(sig("ln_done"), 1)
            for c in range(2, UP_CHUNKS):
                down_high(c)

            def raw_high():
                a.activation(RAWH, RAW, ACT.Copy).then_inc(sig("raw_high"), 1)

            act.wait_ge(sig("ld_raw"), 96)
            raw_high()
            act.wait_ge(sig("raw_rest"), 1)
            raw_high()

            def weight_high(name, layer):
                act.wait_ge(sig("ld_" + name), 16 * layer + 16)
                a.activation(WHIGH[SLOT[name]][:, :, :], WEIGHT[SLOT[name]], ACT.Copy).then_inc(sig(name + "_high"), 1)

            weight_high("wq", 0)
            weight_high("wk", 0)

            def evac_columns(key, dst, bias, func=ACT.Identity):
                B.wait_filled(act, key)
                B.release(key, a.activation(halves(dst), B.halves(key, 128), func, bias=bias))

            with act.Fori(0, LAYERS) as i:
                B.turn = i

                def lcol(kind, k, table=cols, base=COLS["layers"]):
                    return table[:, bass.ds(i * (7 * FT) + (base + kind + k), 1)]

                def make_conditioning(n, tiles=range(FT)):
                    for k in tiles:
                        evac_columns(("scale", n, k), SC[:, k, :], lcol((S1B, S2B)[n - 1], k, cols1, 0))
                        evac_columns(("bias", n, k), BI[n][:, k, :], lcol((B1B, B2B)[n - 1], k))

                def input_high(n):
                    for k in range(FT):
                        act.wait_ge(sig(("input_even", "input_odd")[k % 2]), FT * i + (FT // 2 * (n - 1) + k // 2 + 1))
                        a.activation(YH[:, k, :], YT[:, k, :], ACT.Copy).then_inc(sig("input_high"), 1)

                def query_key_high(h):
                    B.wait_evacuated(act, ("q", h))
                    a.activation(QH[:, h % 2, :], QT[:, h, :], ACT.Copy).then_inc(sig("query_high"), 1)
                    B.wait_filled(act, ("k", h))
                    a.activation(halves(KT[:, h, :]), B.halves(("k", h), 128), ACT.Identity, bias=lcol(BK, h))
                    B.release(("k", h), a.activation(halves(KH[:, h % 2, :]), B.halves(("k", h), 128), ACT.Identity, bias=lcol(BK, h)))

                def exps(h):
                    for t in range(NT):
                        B.wait_evacuated(act, ("s", h, t))
                        a.activation(P[:, h % 2, t, :], P[:, h % 2, t, :], ACT.Exp, scale=-1.0,
                                     bias=negm[:, h % 2, t:t + 1], accum_out=psums[:, h % 2, t:t + 1]
                                     ).then_inc(sig("exps_done"), 1)

                def transposed(h):
                    for j in (0, 2, 4):
                        B.wait_filled(act, ("pt", h, j))
                        B.release(("pt", h, j), a.activation(tiled(PT[:, h % 2, j, :]), B.blocks(("pt", h, j), NT), ACT.Copy))

                def outputs(h):
                    B.wait_filled(act, ("av", h))
                    a.activation(halves(OH[:, h, :]), B.halves(("av", h), 128), ACT.Copy).then_inc(sig("attended_high"), 1)

                make_conditioning(1)
                input_high(1)
                query_key_high(0)
                query_key_high(1)
                weight_high("wv", i)
                exps(0)
                query_key_high(2)
                exps(1)
                query_key_high(3)
                transposed(0)
                exps(2)
                weight_high("wo", i)
                outputs(0)
                transposed(1)
                exps(3)
                weight_high("m1", i)
                outputs(1)
                transposed(2)
                make_conditioning(2, (0, 1))
                weight_high("m2", i)
                outputs(2)
                transposed(3)
                make_conditioning(2, (2, 3))
                outputs(3)
                act.wait_ge(sig("ld_raw"), 96 * i + 192)
                raw_high()
                act.wait_ge(sig("raw_rest"), i + 2)
                raw_high()
                input_high(2)
                for f in range(FT):
                    B.wait_filled(act, ("m1", f))
                    a.activation(halves(HT[:, f, :]), B.halves(("m1", f), 128), ACT.Relu, bias=lcol(MB1, f))
                    B.release(("m1", f), a.activation(halves(HH[:, f, :]), B.halves(("m1", f), 128), ACT.Relu, bias=lcol(MB1, f)))
                    if f == 1:
                        weight_high("wq", i + 1)
                weight_high("wk", i + 1)
            for k in range(0, FT, 2):
                C.wait_filled(act, ("t", 2, k))
                C.release(("t", 2, k), a.activation(tiled(YT[:, k, :]), C.blocks(("t", 2, k), NT, 128), ACT.Copy))
            C.wait_filled(act, ("hid",))
            C.release(("hid",), a.activation(halves(HID2T), C.halves(("hid",), HID2), ACT.Relu, bias=col("c_b1", 0, HID2)))
            act.wait_ge(sig("lc2_half"), 1)
            a.activation(LC, LC, ACT.Ln).then_inc(sig("ln_done"), 1)
            one_weight_high("ws3", WS3, 0)
            for k in range(FT):
                C.wait_filled(act, ("t", 3, k))
                a.activation(tiled(YH[:, k, :]), C.blocks(("t", 3, k), NT, 128), ACT.Copy).then_inc(sig("evacuated_high"), 1)
            act.wait_ge(sig("fg_ready"), 1)

            def edge_sums(h):
                C.wait_filled(act, ("g", h))
                if h >= 2:
                    C.wait_filled(act, ("pt", h - 2, NT - 1))
                for t in range(NT):
                    z = a.activation(tiled(P[:, h % 2, t, :]), C.blocks(("g", h), NT), ACT.Identity, bias=fcol[:, t, h:h + 1])
                    if t < NT - 1:
                        z.then_inc(sig("z_ready"), 1)
                    else:
                        C.release(("g", h), z)

            def exps3(h):
                for t in range(NT):
                    act.wait_ge(sig("masked3"), NT * h + t + 1)
                    a.activation(P[:, h % 2, t, :], P[:, h % 2, t, :], ACT.Exp, scale=-1.0, bias=negm[:, h % 2, t:t + 1],
                                 accum_out=psums[:, h % 2, t:t + 1]).then_inc(sig("exps_done3"), 1)

            edge_sums(0)
            edge_sums(1)
            exps3(0)
            for h in range(H3):
                for j in (2, 3, 4):
                    C.wait_filled(act, ("pt", h, j))
                    C.release(("pt", h, j), a.activation(tiled(PT[:, h % 2, j, :]), C.blocks(("pt", h, j), NT), ACT.Copy))
                if h + 1 < H3:
                    exps3(h + 1)
                if h + 2 < H3:
                    edge_sums(h + 2)

        @block.vector
        def _(dve):
            v = nc.vector
            MAGIC = 12582912.0
            PI2 = (6.28125, 0.0019350051879882812, 3.0199159819567194e-07)

            def col(name, k=0, p=128):
                return cols[0:p, COLS[name] + k:COLS[name] + k + 1]

            def norm(sems, base, dst, before=None, chain=dve_chain, done=None):
                var_ready, rstd_ready, xn_ready = sems
                for t in range(NT + 1):
                    if t < NT:
                        if before:
                            before(t)
                        chain(dve, v.bn_stats(stats[:, t, :], X[:, t, :]))
                        part_wait(dve, "dve")
                        v.bn_aggr(mv[:, t, :], stats[:, t, :]).then_inc(var_ready, 1)
                    if t >= 1:
                        dve.wait_ge(rstd_ready, base + t)
                        v.tensor_scalar(dst[:, t - 1, :], X[:, t - 1, :], mv[:, t - 1, 0:1], rstd[:, t - 1:t],
                                        ALU.subtract, ALU.mult).then_inc(done or xn_ready, 1)

            front = (sig("var_ready"), sig("rstd_ready"), sig("xn_ready"))
            v.memset(YT[:, :, NODES:W], 0.0)
            v.memset(NOISE[:, NODES:W], 0.0)
            dve.wait_ge(sig("ld_x"), 32)
            norm(front, 0, XN)
            dve.wait_ge(sig("ld_cols"), 16)
            for k in range(1, FT, 2):
                A.wait_filled(dve, ("t", k))
                A.release(("t", k), v.tensor_scalar(tiled(YT[:, k, :]), A.blocks(("t", k), NT, 128),
                                                    col("ln1_g", k), col("ln1_b", k), ALU.mult, ALU.add))
            dve.wait_ge(sig("ld_noise"), 16)
            v.tensor_scalar(cols1[:, :], cols[:, COLS["layers"]:NCOLS], 1.0, None, ALU.add)
            E = 2 * NFREQ
            dve_chain(dve, v.tensor_scalar(PHASE, NOISE, col("freq", 0, E), None, ALU.mult))
            dve_chain(dve, v.tensor_scalar(TURNS, PHASE, 0.15915494309189535, None, ALU.mult))
            dve_chain(dve, v.tensor_scalar(TURNS, TURNS, col("turn", 0, E), None, ALU.add))
            dve_chain(dve, v.tensor_scalar(TURNS, TURNS, MAGIC, None, ALU.add))
            dve_chain(dve, v.tensor_scalar(TURNS, TURNS, MAGIC, None, ALU.subtract))
            for part in PI2:
                dve_chain(dve, v.scalar_tensor_tensor(PHASE, TURNS, -part, PHASE, ALU.mult, ALU.add))
            dve_chain(dve, v.tensor_scalar(PHASE, PHASE, col("angle", 0, E), None, ALU.add))
            v.tensor_scalar(TURNS, PHASE, 3.1415925, -3.1415925, ALU.min, ALU.max).then_inc(sig("emb_ready"), 1)

            def queries0(k):
                A.wait_filled(dve, ("q", k))
                A.release(("q", k), v.tensor_scalar(halves(QT[:, k, :]), A.halves(("q", k), 128),
                                                    col("bq", k), float(D) ** -0.5, ALU.add, ALU.mult))

            def onehot_pair(slot, c):
                v.tensor_scalar(OH16[:, 0, slot, :], iota16[0:TILE, :], dst_f[:, c], None, ALU.is_equal)
                return v.tensor_scalar(OH16[:, 1, slot, :], iota16[0:TILE, :], src_f[:, c], None, ALU.is_equal)

            def first_onehots(group):
                for slot in range(HALF * group, HALF * group + HALF):
                    last = onehot_pair(slot, slice(slot, slot + 1))
                last.then_inc(sig("onehot_ready"), 1)

            v.memset(KTZ[DH0:128, 0, :, :], 0.0)
            v.memset(KTZ[0:DH0, 1, :, :], 0.0)
            queries0(0)
            dve.wait_ge(sig("ld_idx"), 32)
            v.tensor_copy(src_f[:, :], src_i[:, :])
            dve_chain(dve, v.tensor_copy(dst_f[:, :], dst_i[:, :]))
            dve_chain(dve, v.scalar_tensor_tensor(pair_f[:, :], dst_f[:, :], float(NODES), src_f[:, :], ALU.mult, ALU.add))
            v.tensor_copy(pair_i[:, :], pair_f[:, :]).then_inc(sig("pairs_ready"), 1)
            queries0(1)
            dve.wait_ge(sig("ld_attr"), 32)
            dve_chain(dve, v.tensor_tensor(ATTR[:, 0, :], ATTR[:, 0, :], ATTR[:, 1, :], ALU.add))
            v.reduce_max(gmax[:, 0:1], ATTR[:, 0, :], AX.X).then_inc(sig("gmax_part"), 1)
            dve_chain(dve, v.tensor_scalar(tid[:, :], dst_f[:, :], float(TILE), None, ALU.is_ge))
            for j in range(2, NT):
                dve_chain(dve, v.scalar_tensor_tensor(tid[:, :], dst_f[:, :], float(TILE * j), tid[:, :], ALU.is_ge, ALU.add))
            for j in range(NT):
                last = v.tensor_scalar(FLAGS[:, j, :], tid[:, :], float(j), None, ALU.is_equal)
            dve_chain(dve, last)
            v.tensor_reduce(gflag[:, 0, :], FLAGS.rearrange("p j (g u) -> p (j g) u", u=4), AX.X, ALU.max
                            ).then_inc(sig("flags_part"), 1)
            dve.wait_ge(sig("iota_ready"), 1)
            first_onehots(0)
            queries0(2)
            first_onehots(1)
            first_onehots(2)
            queries0(3)
            first_onehots(3)
            dve.wait_ge(sig("gmax_all"), 1)
            dve_chain(dve, v.tensor_scalar(ATTR[:, 0, :], ATTR[:, 0, :], gmax[:, 1:2], None, ALU.subtract))
            dve.wait_ge(sig("flags_all"), 1)
            dve_chain(dve, v.tensor_copy(mask_f[:, :], gflag[0:1, 1, 0:GROUPS]))
            for j in range(1, NT):
                dve_chain(dve, v.scalar_tensor_tensor(mask_f[:, :], gflag[0:1, 1, GROUPS * j:GROUPS * (j + 1)], float(1 << j),
                                                      mask_f[:, :], ALU.mult, ALU.add))
            v.tensor_copy(mask_i[:, :], mask_f[:, :]).then_inc(sig("mask_ready"), 1)

            def bank_view(r, key, pair):
                return r.view(key).rearrange("p (b c) -> p b c", b=2)[:, 0:len(pair), :]

            def row_bias(r, key, pair, dst, row):
                r.wait_filled(dve, key)
                r.release(key, v.tensor_tensor(dst[:, pair[0]:pair[-1] + 1, :], bank_view(r, key, pair),
                                               row.to_broadcast([TILE, len(pair), D]), ALU.add))

            dve.wait_ge(sig("ld_rows0"), 16)
            for n, pair in enumerate(PAIRS):
                row_bias(A, ("v", n), pair, V, ROWS[:, 0:1, :])
            dve.wait_ge(sig("cond_high"), 1)
            v.scalar_tensor_tensor(CONDF, CONDH, col("part_c", 0, STACK), CONDF, ALU.mult, ALU.add).then_inc(sig("cond_rest"), 1)
            dve.wait_ge(sig("cond_high"), 2)
            v.scalar_tensor_tensor(condT[:, :], CONDH, col("part_c", 1, STACK), CONDF, ALU.mult, ALU.add)
            with dve.Fori(0, GROUPS // 4 - 1) as i:
                for r in range(4):
                    dve.wait_ge(sig("onehot_group_free"), 4 * i + (r + 1))
                    for slot in range(HALF * r, HALF * r + HALF):
                        last = onehot_pair(slot, bass.ds(4 * HALF * i + (4 * HALF + slot), 1))
                    last.then_inc(sig("onehot_ready"), 1)
            dve.wait_ge(sig("counts_done"), 1)
            for j in range(NT):
                v.tensor_copy(C2[:, j, 0:512], ps[0:TILE, 512 * j:512 * j + 512])
                last = v.tensor_copy(C2[:, j, 512:W], ps[0:TILE, 2560 + 128 * j:2560 + 128 * j + W - 512])
            last.then_inc(sig("counts_ready"), 1)
            dve.wait_ge(sig("counts_ready"), 1)
            dve_chain(dve, v.tensor_scalar(MASK, C2, 0.5, -BIG, ALU.is_lt, ALU.mult))
            for n in range(NT * H0):
                j, h = divmod(n, H0)
                A.wait_filled(dve, ("s", j, h))
                if n >= 3:
                    dve.wait_ge(sig("stage_ready"), n - 2)
                A.release(("s", j, h), v.tensor_tensor_reduce(
                    out=halves(TEMP[:, n % 3, :]), in0=A.halves(("s", j, h)), in1=halves(MASK[:, j, :]), scale=-1.0, scalar=3.0e38,
                    op0=ALU.add, op1=ALU.min, accum_out=negm0[:, n % 3:n % 3 + 1]))
            def one_weight_low(count, weight, n):
                dve.wait_ge(sig("lone_weight_high"), count)
                v.tensor_tensor(WLOW[n][:, :, :], weight, WHIGH[n][:, :, :].bitcast(f32), ALU.subtract
                                ).then_inc(sig("lone_weight_low"), 1)

            one_weight_low(1, WO0, 2)
            with dve.Fori(0, GROUPS // 4) as i:
                for r in range(4):
                    hf, half = r % 2, 4 * i + r
                    dve.wait_ge(sig(f"logits_gathered{r}"), 16 * HALF * i + 16 * HALF)
                    now = bass.ds(4 * HALF * H0 * i + HALF * H0 * r, HALF * H0)
                    v.tensor_tensor(sum_ring[:, hf, :], lg_ring[:, r, :], ATTR[:, 0, now], ALU.add
                                    ).then_inc(sig("edge_logits_ready"), 1)
                    dve.wait_ge(sig("msg_group_free"), half + 2)

                    def onehot(u):
                        v.tensor_scalar(OHR[:, HALF * hf + u, :], iota16[0:TILE, :],
                                        dst_f[:, bass.ds(4 * HALF * i + (HALF * r + u), 1)], None, ALU.is_equal)

                    def message(u):
                        v.tensor_tensor(VG[r][:, u, :].rearrange("p (h d) -> p h d", h=H0),
                                        VG[r][:, u, :].rearrange("p (h d) -> p h d", h=H0),
                                        p_ring[:, hf, u * H0:(u + 1) * H0].unsqueeze(2).to_broadcast([TILE, H0, DH0]),
                                        ALU.mult).then_inc(sig("msg_full"), 1)

                    def message_low(u):
                        dve.wait_ge(sig("msg_high"), 4 * HALF * i + (HALF * r + u + 1))
                        return v.tensor_tensor(MSGR[:, HALF * hf + u, 1, :], VG[r][:, u, :],
                                               MSGR[:, HALF * hf + u, 0, :].bitcast(f32), ALU.subtract)

                    onehot(0)
                    dve.wait_ge(sig("edge_probs_ready"), half + 1)
                    dve.wait_ge(sig(f"values_gathered{r}"), 16 * HALF * i + 16 * HALF)
                    message(0)
                    onehot(1)
                    message(1)
                    dve.wait_ge(sig("edge_probs_high"), half + 1)
                    v.tensor_tensor(PR[:, hf, :, 1, :], p_ring[:, hf, :].rearrange("p (u h) -> p u h", u=HALF),
                                    PR[:, hf, :, 0, :].bitcast(f32), ALU.subtract)
                    message(2)
                    message_low(0)
                    onehot(2)
                    message(3)
                    message_low(1)
                    onehot(3)
                    message_low(2)
                    message_low(3).then_inc(sig("msg_ready"), 1)
                    dve.wait_ge(sig("msg_ready"), half + 1)
                    dve.sem_inc(sig("gather_slot_free"), 1)
            dve.wait_ge(sig("agg_done"), 1)
            dve_chain(dve, v.tensor_reduce(den[:, :, :], ps[0:TILE, 2560:2560 + 2 * NT * H0].rearrange(
                "p (j k h) -> p j h k", j=NT, k=2), AX.X, ALU.add))
            dve_chain(dve, v.tensor_scalar(den[:, :, :], den[:, :, :], 1.0e-37, None, ALU.max))
            dve_chain(dve, v.reciprocal(rden[:, :, :], den[:, :, :]))
            for j in range(NT):
                v.tensor_tensor(V[:, j, :].rearrange("p (h d) -> p h d", h=H0),
                                       ps[0:TILE, 512 * j:512 * j + 512].rearrange("p (h d) -> p h d", h=H0),
                                       rden[:, j, :].unsqueeze(2).to_broadcast([TILE, H0, DH0]), ALU.mult).then_inc(sig("agg_ready"), 1)

            def make_log_counts(counts, name):
                dve_chain(dve, v.tensor_scalar(LTMP[name], counts, 0.5, -BIG, ALU.is_lt, ALU.mult))
                v.tensor_scalar(LC, counts, 1.0, None, ALU.max).then_inc(sig(name), 1)

            v.memset(LC[:, :, NODES:W], 0.0)
            v.memset(YT[:, :, NODES:W], 0.0)
            for k in range(FT):
                dve.wait_ge(sig("evacuated_high"), k + 1)
                A.release(("at", k), v.tensor_tensor(tiled(OL[:, k, :]), A.blocks(("at", k), NT, 128),
                                                     tiled(OH[:, k, :]).bitcast(f32), ALU.subtract))

            def add_rows(r, name):
                def before(t):
                    n = t // 2
                    if t == 2 * n:
                        r.wait_filled(dve, (name, n))
                        pair = PAIRS[n]
                        ins = v.tensor_tensor(X[:, pair[0]:pair[-1] + 1, :], X[:, pair[0]:pair[-1] + 1, :],
                                              bank_view(r, (name, n), pair), ALU.add)
                        r.release((name, n), ins)
                        r.wait_evacuated(dve, (name, n))
                return before

            def up_low(c):
                dve.wait_ge(sig("up_high"), c + 1)
                v.tensor_tensor(UPL[c % 2][:, :, :], UPW[c % 2], UPH[c % 2][:, :, :].bitcast(f32), ALU.subtract
                                ).then_inc(sig("up_low"), 1)

            up_low(0)
            up_low(1)
            dve.wait_ge(sig("residual_biased"), 1)
            norm(front, NT, XN, add_rows(A, "o"))
            for k in range(1, FT, 2):
                A.wait_filled(dve, ("t2", k))
                A.release(("t2", k), v.tensor_scalar(tiled(YT[:, k, :]), A.blocks(("t2", k), NT, 128),
                                                     col("ln2_g", k), col("ln2_b", k), ALU.mult, ALU.add))
            for k in range(FT):
                dve.wait_ge(sig("mlp_high"), k + 1)
                v.tensor_tensor(YL[:, k, :], YT[:, k, :], YH0[:, k, :].bitcast(f32), ALU.subtract
                                ).then_inc(sig("up_input_low"), 1)
            A.wait_evacuated(dve, ("c1", NT - 1))
            make_log_counts(LC, "lc_half")

            def down_low(c):
                dve.wait_ge(sig("down_high"), c + 1)
                v.tensor_tensor(DNL[c % 2][:, :, :], DNW[c % 2], DNH[c % 2][:, :, :].bitcast(f32), ALU.subtract
                                ).then_inc(sig("down_low"), 1)

            down_low(0)
            up_low(2)
            down_low(1)
            up_low(3)
            for f in range(FF0):
                dve.wait_ge(sig("mlp_high"), FT + f + 1)
                v.tensor_tensor(HL0[f // 4][:, f % 4, :], HT0[:, f, :], HH0[f // 4][:, f % 4, :].bitcast(f32), ALU.subtract
                                ).then_inc(sig("hidden0_low"), 1)
            dve.wait_ge(sig("ln_done"), 1)
            dve_chain(dve, v.tensor_tensor(LC, LC, LTMP["lc_half"], ALU.add))
            dve_chain(dve, v.tensor_reduce(has1[:, :], LC, AX.X, ALU.max))
            v.tensor_scalar(has1[:, :], has1[:, :], -0.5 * BIG, None, ALU.is_gt).then_inc(sig("lc_ready"), 1)
            for c in range(2, UP_CHUNKS):
                down_low(c)
            dve.wait_ge(sig("residual_biased"), 2)
            dve.wait_ge(sig("ld_x0"), 32)
            dve_chain(dve, v.tensor_tensor(X, X, XIN0, ALU.add))
            block0_end = add_rows(A, "down")

            def raw_rest():
                v.scalar_tensor_tensor(RAW, RAWH, col("part_w", 0, STACK), RAW, ALU.mult, ALU.add).then_inc(sig("raw_rest"), 1)

            def weight_parts():
                v.scalar_tensor_tensor(condw[:, :, :].rearrange("p q n -> p (q n)"), RAWH, col("part_w", 1, STACK), RAW,
                                       ALU.mult, ALU.add).then_inc(sig("cond_parts_ready"), 1)

            dve.wait_ge(sig("raw_high"), 1)
            raw_rest()
            dve.wait_ge(sig("raw_high"), 2)
            weight_parts()

            def weight_low(name, layer):
                dve.wait_ge(sig(name + "_high"), layer + 1)
                n = SLOT[name]
                v.tensor_tensor(WLOW[n][:, :, :], WEIGHT[n], WHIGH[n][:, :, :].bitcast(f32), ALU.subtract
                                ).then_inc(sig(name + "_low"), 1)

            weight_low("wq", 0)
            norm(front, 2 * NT, X, block0_end, done=sig("x1_ready"))
            dve.wait_ge(sig("x1_ready"), NT)

            v.memset(PT[:, :, :, NODES:W], 0.0).then_inc(sig("padding_ready"), 1)

            weight_low("wk", 0)

            with dve.Fori(0, LAYERS) as i:
                B.turn = i
                dve_loop_chain.turn, dve_loop_chain.per_turn = i, 2 * NT + 2 * H1

                def lcol(kind, k):
                    return cols[:, bass.ds(i * (7 * FT) + (COLS["layers"] + kind + k), 1)]

                mid = (sig("var_ready1"), sig("rstd_ready1"), sig("xn_ready1"))

                def apply_conditioning(n):
                    v.memset(YT[:, :, NODES:W], 0.0)
                    for k in range(FT):
                        B.wait_evacuated(dve, ("scale", n, k))
                        B.wait_evacuated(dve, ("bias", n, k))
                        B.wait_filled(dve, ("t", n, k))
                        B.release(("t", n, k), v.tensor_tensor(tiled(YT[:, k, :]), B.blocks(("t", n, k), NT, 128),
                                                               tiled(SC[:, k, :]), ALU.mult))
                        if k % 2 == 1:
                            B.wait_evacuated(dve, ("t", n, k))
                            v.tensor_tensor(YT[:, k, 0:NODES], YT[:, k, 0:NODES], BI[n][:, k, 0:NODES], ALU.add
                                            ).then_inc(sig("input_odd"), 1)
                    for k in range(FT):
                        dve.wait_ge(sig("input_high"), 2 * FT * i + (FT * (n - 1) + k + 1))
                        v.tensor_tensor(YL[:, k, :], YT[:, k, :], YH[:, k, :].bitcast(f32), ALU.subtract
                                        ).then_inc(sig("input_low"), 1)

                def attended_low(h):
                    dve.wait_ge(sig("attended_high"), H1 * i + (h + 1))
                    B.release(("av", h), v.tensor_tensor(halves(OL[:, h, :]), B.halves(("av", h), 128),
                                                         halves(OH[:, h, :].bitcast(f32)), ALU.subtract))

                def queries(h):
                    B.wait_filled(dve, ("q", h))
                    B.release(("q", h), v.tensor_scalar(halves(QT[:, h, :]), B.halves(("q", h), 128), lcol(BQ, h),
                                                        float(DH1) ** -0.5, ALU.add, ALU.mult))

                def query_key_low(h):
                    dve.wait_ge(sig("query_high"), H1 * i + (h + 1))
                    v.tensor_tensor(QL[:, h, :], QT[:, h, :], QH[:, h % 2, :].bitcast(f32), ALU.subtract)
                    B.wait_evacuated(dve, ("k", h))
                    v.tensor_tensor(KL[:, h, :], KT[:, h, :], KH[:, h % 2, :].bitcast(f32), ALU.subtract
                                    ).then_inc(sig("query_key_low"), 1)

                def masked(h):
                    if h >= 2:
                        B.wait_filled(dve, ("pt", h - 2, NT - 1))
                    for t in range(NT):
                        B.wait_filled(dve, ("s", h, t))
                        part_wait(dve, "dve")
                        B.release(("s", h, t), v.tensor_tensor_reduce(
                            out=halves(P[:, h % 2, t, :]), in0=B.halves(("s", h, t)), in1=halves(LC[:, t, :]), scale=-1.0,
                            scalar=3.0e38, op0=ALU.add, op1=ALU.min, accum_out=negm[:, h % 2, t:t + 1]))

                def normalise(h):
                    dve.wait_ge(sig("exps_done"), H1 * NT * i + NT * (h + 1))
                    dve_loop_chain(dve, v.reciprocal(rinv[:, h % 2, :], psums[:, h % 2, :]))
                    dve_loop_chain(dve, v.tensor_tensor(rinv[:, h % 2, :], rinv[:, h % 2, :], has1[:, :], ALU.mult))
                    for t in range(NT):
                        v.tensor_scalar(P[:, h % 2, t, :], P[:, h % 2, t, :], rinv[:, h % 2, t:t + 1], None,
                                        ALU.mult).then_inc(sig("probs_normalised"), 1)

                def transposed(h):
                    for j in (1, 3):
                        B.wait_filled(dve, ("pt", h, j))
                        B.release(("pt", h, j), v.tensor_copy(tiled(PT[:, h % 2, j, :]), B.blocks(("pt", h, j), NT)))

                norm(mid, 2 * NT * i, XN, chain=dve_loop_chain)
                apply_conditioning(1)
                queries(0)
                query_key_low(0)
                queries(1)
                query_key_low(1)
                masked(0)
                queries(2)
                normalise(0)
                query_key_low(2)
                masked(1)
                weight_low("wv", i)
                queries(3)
                query_key_low(3)
                dve.wait_ge(sig("ld_row0"), 16 * i + 16)
                for n, pair in enumerate(PAIRS):
                    if n == 2:
                        B.wait_filled(dve, ("v", n))
                        v.memset(PT[:, 0, :, NODES:W], 0.0)
                    row_bias(B, ("v", n), pair, V, ROWS[:, 0:1, :])
                    if n == 0:
                        normalise(1)
                transposed(0)
                masked(2)
                weight_low("wo", i)
                attended_low(0)
                transposed(1)
                normalise(2)
                masked(3)
                weight_low("m1", i)
                attended_low(1)
                transposed(2)
                normalise(3)
                weight_low("m2", i)
                attended_low(2)
                transposed(3)
                attended_low(3)
                dve.wait_ge(sig("raw_high"), 2 * i + 3)
                raw_rest()
                dve.wait_ge(sig("residual_biased1"), 2 * i + 1)
                norm(mid, 2 * NT * i + NT, XN, add_rows(B, "o"), chain=dve_loop_chain)
                apply_conditioning(2)
                dve.wait_ge(sig("raw_high"), 2 * i + 4)
                weight_parts()
                for f in range(FT):
                    B.wait_evacuated(dve, ("m1", f))
                    v.tensor_tensor(HL[:, f, :], HT[:, f, :], HH[:, f, :].bitcast(f32), ALU.subtract
                                    ).then_inc(sig("hidden_low"), 1)
                    if f == 2:
                        weight_low("wq", i + 1)
                weight_low("wk", i + 1)
                dve.wait_ge(sig("residual_biased1"), 2 * i + 2)
                for n, pair in enumerate(PAIRS):
                    B.wait_filled(dve, ("m2", n))
                    B.release(("m2", n), v.tensor_tensor(X[:, pair[0]:pair[-1] + 1, :], X[:, pair[0]:pair[-1] + 1, :],
                                                         bank_view(B, ("m2", n), pair), ALU.add))
                for n in range(3):
                    B.wait_evacuated(dve, ("m2", n))
            assert dve_loop_chain.count == dve_loop_chain.per_turn, dve_loop_chain.count

            back = (sig("var_ready3"), sig("rstd_ready3"), sig("xn_ready3"))
            dve.wait_ge(sig("ld_x1"), 32)

            v.memset(YT[:, :, NODES:W], 0.0)
            v.memset(PT[:, 0, :, NODES:W], 0.0)

            def block1_end(t):
                dve_chain(dve, v.tensor_tensor(X[:, t, :], X[:, t, :], XIN[:, t, :], ALU.add))

            norm(back, 0, X, block1_end)
            for k in range(1, FT, 2):
                C.wait_filled(dve, ("t", 2, k))
                C.release(("t", 2, k), v.tensor_copy(tiled(YT[:, k, :]), C.blocks(("t", 2, k), NT, 128)))
            dve.wait_ge(sig("ld_c2"), 32)
            make_log_counts(C2, "lc2_half")
            dve.wait_ge(sig("ld_rows3"), 16)
            for n, pair in enumerate(PAIRS):
                row_bias(C, ("h", n), pair, V, ROWS[:, 0:1, :])
            for n in range(3):
                C.wait_evacuated(dve, ("h", n))
            dve.wait_ge(sig("ln_done"), 2)
            dve_chain(dve, v.tensor_tensor(LC, LC, LTMP["lc2_half"], ALU.add))
            dve_chain(dve, v.tensor_reduce(has2[:, :], LC, AX.X, ALU.max))
            dve_chain(dve, v.tensor_scalar(has2[:, :], has2[:, :], -0.5 * BIG, None, ALU.is_gt))

            def block2_end(t):
                n = t // 2
                if t == 2 * n:
                    pair = PAIRS[n]
                    tiles = slice(pair[0], pair[-1] + 1)
                    dve_chain(dve, v.tensor_tensor(X[:, tiles, :], X[:, tiles, :], V[:, tiles, :], ALU.add))
                    C.wait_filled(dve, ("agg", n))
                    C.release(("agg", n), v.tensor_tensor(X[:, tiles, :], X[:, tiles, :], bank_view(C, ("agg", n), pair), ALU.add))
                    C.wait_evacuated(dve, ("agg", n))

            norm(back, NT, X, block2_end)
            one_weight_low(2, WS3, 0)
            for k in range(FT):
                dve.wait_ge(sig("evacuated_high"), FT + k + 1)
                C.release(("t", 3, k), v.tensor_tensor(tiled(YL[:, k, :]), C.blocks(("t", 3, k), NT, 128),
                                                       tiled(YH[:, k, :]).bitcast(f32), ALU.subtract))
            dve.wait_ge(sig("ld_aw"), 16)
            dve.wait_ge(sig("ld_c"), 48)
            for n, pair in enumerate(PAIRS):
                row_bias(C, ("wx", n), pair, V, AW[:, 2:3, :])
                C.wait_evacuated(dve, ("wx", n))
                for t in pair:
                    dve_chain(dve, v.tensor_tensor(PROD, V[:, t, :], AW[:, 0, :], ALU.mult))
                    dve_chain(dve, v.tensor_reduce(fcol[:, t, :], PROD.rearrange("p (h d) -> p h d", h=H3), AX.X, ALU.add))
                for t in pair:
                    dve.wait_ge(sig("g_products"), t + 1)
                    last = v.tensor_reduce(gcol[:, t, :], PRODG[:, t, :].rearrange("p (h d) -> p h d", h=H3), AX.X, ALU.add)
            dve_chain(dve, last)
            v.tensor_tensor(fcol[:, :, :], fcol[:, :, :], ab[:, :].unsqueeze(1).to_broadcast([TILE, NT, H3]), ALU.add
                            ).then_inc(sig("fg_ready"), 1)

            def output(h):
                C.wait_filled(dve, ("av", h))
                p0 = DH3 * (h % 2)
                C.release(("av", h), v.tensor_copy(halves(OT3[p0:p0 + DH3, h // 2, :]), C.halves(("av", h), DH3, p0)))


            def masked3(h):
                for t in range(NT):
                    if t < NT - 1:
                        dve.wait_ge(sig("z_ready"), (NT - 1) * h + t + 1)
                    else:
                        C.wait_evacuated(dve, ("g", h))
                    z = P[:, h % 2, t, :]
                    dve_chain(dve, v.scalar_tensor_tensor(z, z, 0.2, z, ALU.mult, ALU.max))
                    v.tensor_tensor_reduce(out=z, in0=z, in1=LC[:, t, :], scale=-1.0, scalar=3.0e38, op0=ALU.add,
                                           op1=ALU.min, accum_out=negm[:, h % 2, t:t + 1]).then_inc(sig("masked3"), 1)

            masked3(0)
            for h in range(H3):
                dve.wait_ge(sig("exps_done3"), NT * (h + 1))
                dve_chain(dve, v.reciprocal(rinv3[:, :, h], psums[:, h % 2, :]))
                v.tensor_tensor(rinv3[:, :, h], rinv3[:, :, h], has2[:, :], ALU.mult)
                if h >= 1:
                    output(h - 1)
                for j in (0, 1):
                    C.wait_filled(dve, ("pt", h, j))
                    C.release(("pt", h, j), v.tensor_copy(tiled(PT[:, h % 2, j, :]), C.blocks(("pt", h, j), NT)))
                if h + 1 < H3:
                    masked3(h + 1)
            output(H3 - 1)

            def block3_end(t):
                n = t // 2
                if t == 2 * n:
                    pair = PAIRS[n]
                    tiles = slice(pair[0], pair[-1] + 1)
                    C.wait_filled(dve, ("x", n))
                    for b, tile in enumerate(pair):
                        last = v.tensor_tensor(V[:, tile, :].rearrange("p (h d) -> p h d", h=H3),
                                               C.view(("x", n))[:, 512 * b:512 * b + 512].rearrange("p (h d) -> p h d", h=H3),
                                               rinv3[:, tile, :].unsqueeze(2).to_broadcast([TILE, H3, DH3]), ALU.mult)
                    C.release(("x", n), last)
                    C.wait_evacuated(dve, ("x", n))
                    dve_chain(dve, v.tensor_tensor(X[:, tiles, :], X[:, tiles, :], V[:, tiles, :], ALU.add))

            norm(back, 2 * NT, X, block3_end, done=sig("out_ready"))

        @block.tensor
        def _(pe):
            mm = nc.tensor.matmul

            def wide(out_view, pairs, arrived=None):
                for n, (w, r) in enumerate(pairs):
                    if arrived:
                        arrived(n)
                    for place, lo in ((0, 0), (512, HALF_W)):
                        last = mm(out_view[:, place:place + HALF_W], w, r[:, lo:lo + HALF_W],
                                  start=n == 0, stop=n == len(pairs) - 1)
                return last

            def columns(r, key, weight, moving, tiles=FT, p=128, arrived=None):
                r.claim(pe, key)
                if arrived and r.turn is not None:
                    part_wait(pe, "pe")
                r.fill(wide(r.view(key, p), [(weight(k), moving[:, k, :]) for k in range(tiles)], arrived))

            def rows(r, key, pair, moving, weight, tiles=FT, arrived=None):
                r.claim(pe, key)
                if arrived and r.turn is not None:
                    part_wait(pe, "pe")
                for k in range(tiles):
                    if arrived:
                        arrived(k)
                    for b, t in enumerate(pair):
                        last = mm(r.view(key)[:, 512 * b:512 * b + 512], moving[:, k, TILE * t:TILE * (t + 1)], weight[:, k, :],
                                  start=k == 0, stop=k == tiles - 1)
                r.fill(last)

            def split_columns(r, key, high, low, tile, x_high, x_low, high_ready, low_ready):
                r.claim(pe, key)
                part = slice(128 * tile, 128 * (tile + 1))
                for c in range(FT):
                    high_ready(c)
                    for w in (high, low):
                        for place, lo in ((0, 0), (512, HALF_W)):
                            mm(r.view(key, 128)[:, place:place + HALF_W], w[:, c, part], x_high[:, c, lo:lo + HALF_W],
                               start=c == 0 and w is high, stop=False)
                for c in range(FT):
                    low_ready(c)
                    for place, lo in ((0, 0), (512, HALF_W)):
                        last = mm(r.view(key, 128)[:, place:place + HALF_W], high[:, c, part], x_low[:, c, lo:lo + HALF_W],
                                  start=False, stop=c == FT - 1)
                r.fill(last)

            def split_rows(r, name, high, low, w_high, w_low, ready=None):
                for n, pair in enumerate(PAIRS):
                    key = (name, n)
                    r.claim(pe, key)
                    if ready and n == 0 and r.turn is not None:
                        part_wait(pe, "pe")
                    for c in range(FT):
                        if ready and n == 0:
                            ready(c)
                        for b, t in enumerate(pair):
                            tile = slice(TILE * t, TILE * (t + 1))
                            for m, (x_part, w_part) in enumerate(((high, w_high), (high, w_low), (low, w_high))):
                                last = mm(r.view(key)[:, 512 * b:512 * b + 512], x_part[:, c, tile], w_part[:, c, :],
                                          start=c == 0 and m == 0, stop=c == FT - 1 and m == 2)
                    r.fill(last)

            def all_rows(r, name, moving, weight, tiles=FT, arrived=None):
                for n, pair in enumerate(PAIRS):
                    rows(r, (name, n), pair, moving, weight, tiles, arrived if n == 0 else None)

            def out_of_psum(r, *name):
                return lambda k: r.wait_evacuated(pe, (*name, k))

            def norm_columns(r, name, src, ready, base):
                for k in range(FT):
                    r.claim(pe, (*name, k))
                for t in range(NT):
                    pe.wait_ge(sig(ready), base + t + 1)
                    for k in range(FT):
                        last = nc.tensor.transpose(r.view((*name, k), 128)[:, 128 * t:128 * t + TILE],
                                                   src[:, t, 128 * k:128 * (k + 1)], ident[0:TILE, 0:TILE])
                        if t == NT - 1:
                            r.fill(last)

            def turn_tiles(r, key, tile):
                r.claim(pe, key)
                for t in range(NT):
                    last = nc.tensor.transpose(r.view(key)[:, 128 * t:128 * t + TILE], tile(t), ident[0:TILE, 0:TILE])
                r.fill(last)

            pe.sem_inc(sig("msg_group_free"), 3)
            B.open(pe)
            pe.wait_ge(sig("ident_ready"), 1)
            norm_columns(A, ("t",), XN, "xn_ready", 0)
            pe.wait_ge(sig("ld_wqkv"), 16)

            def query_key(k):
                columns(A, ("q", k), lambda c: WQKV[:, c, 128 * k:128 * (k + 1)], YT,
                        arrived=out_of_psum(A, "t") if k == 0 else None)
                columns(A, ("k", k), lambda c: WQKV[:, c, D + 128 * k:D + 128 * (k + 1)], YT)

            for k in range(FT - 1):
                query_key(k)
            pe.wait_ge(sig("ld_fw"), 32)
            pe.wait_ge(sig("sin_ready"), 1)
            A.claim(pe, ("hid",))
            A.fill(wide(A.view(("hid",), COND), [(fw1[:, :], EMB)]))
            query_key(FT - 1)
            A.wait_evacuated(pe, ("hid",))
            A.claim(pe, ("cond",))
            A.fill(wide(A.view(("cond",), STACK), [(fw2[:, :], HIDC)]))
            all_rows(A, "v", YT, WQKV[:, :, 2 * D:3 * D])
            for key in (("k", FT - 1), ("cond",), ("v", 0), ("v", 1), ("v", 2)):
                A.wait_evacuated(pe, key)
            pe.wait_ge(sig("zeros_ready"), 1)

            def count_place(j):
                return ((512 * j, 0, 512), (2560 + 128 * j, 512, W))

            for b in range(7):
                mm(ps[0:TILE, 512 * b:512 * b + 512], zero16[:, 0:TILE], zero16[:, :], start=True, stop=True)
            pe.wait_ge(sig("mask_ready"), 1)

            def group_end(name):
                mm(ps[0:TILE, 3584:3584 + 64], zero16[:, 0:TILE], zero16[:, 0:64], start=True, stop=True).then_inc(sig(name), 1)

            with pe.Fori(0, GROUPS // 4) as i:
                for r in range(4):
                    pe.wait_ge(sig("onehot_ready"), 4 * i + (r + 1))
                    reached = pe.value_load(mask_i[0:1, bass.ds(4 * i + r, 1)], min_val=0, max_val=(1 << NT) - 1)
                    for j in range(NT):
                        with pe.If((reached & (1 << j)) > 0):
                            for u in range(HALF * r, HALF * r + HALF):
                                for o, lo, hi in count_place(j):
                                    mm(ps[0:TILE, o:o + hi - lo], OH16[:, 0, u, TILE * j:TILE * (j + 1)], OH16[:, 1, u, lo:hi],
                                       start=False, stop=True, skip_group_check=True)
                    group_end("onehot_group_free")
            group_end("counts_done")
            pe.wait_ge(sig("counts_ready"), 1)
            for j in range(NT):
                for h in range(H0):
                    key = ("s", j, h)
                    A.claim(pe, key)
                    A.fill(wide(A.view(key), [(KTZ[:, h % 2, h // 2, TILE * j:TILE * (j + 1)], QT[:, h // 2, :])]))
            for h in range(H0 - 4, H0):
                A.wait_evacuated(pe, ("s", NT - 1, h))
            for b in range(6):
                mm(ps[0:TILE, 512 * b:512 * b + 512], zero16[:, 0:TILE], zero16[:, :], start=True, stop=True)
            with pe.Fori(0, GROUPS // 2) as i:
                for hf in range(2):
                    pe.wait_ge(sig("msg_ready"), 2 * i + (hf + 1))
                    reached = pe.value_load(mask_i[0:1, bass.ds(2 * i + hf, 1)], min_val=0, max_val=(1 << NT) - 1)
                    for j in range(NT):
                        with pe.If((reached & (1 << j)) > 0):
                            for u in range(HALF):
                                onehot = OHR[:, HALF * hf + u, TILE * j:TILE * (j + 1)]
                                for part in range(2):
                                    mm(ps[0:TILE, 512 * j:512 * j + 512], onehot, MSGR[:, HALF * hf + u, part, :],
                                       start=False, stop=True, skip_group_check=True)
                                mm(ps[0:TILE, 2560 + 2 * H0 * j:2560 + 2 * H0 * (j + 1)], onehot,
                                   PR[:, hf, u, :, :].rearrange("p k h -> p (k h)"), start=False, stop=True, skip_group_check=True)
                    group_end("msg_group_free")
            group_end("agg_done")
            pe.wait_ge(sig("agg_ready"), NT)
            norm_columns(A, ("at",), V, "agg_ready", 0)
            pe.wait_ge(sig("lone_weight_low"), 1)
            split_rows(A, "o", OH, OL, WHIGH[2], WLOW[2], out_of_psum(A, "at"))
            for j in range(NT):
                turn_tiles(A, ("c1", j), lambda t: C2[:, t, TILE * j:TILE * (j + 1)])
            norm_columns(A, ("t2",), XN, "xn_ready", NT)
            for f in range(FF0):
                pe.wait_ge(sig("up_low"), f // 4 + 1)
                split_columns(A, ("up", f), UPH[f // 4 % 2], UPL[f // 4 % 2], f % 4, YH0, YL,
                              lambda c: pe.wait_ge(sig("mlp_high"), c + 1), lambda c: pe.wait_ge(sig("up_input_low"), c + 1))
            for n in range(3):
                A.claim(pe, ("down", n))

            def down(f, pair_n):
                w_high, w_low, c = DNH[f // 4 % 2], DNL[f // 4 % 2], f % 4
                for b, t in enumerate(PAIRS[pair_n]):
                    tile = slice(TILE * t, TILE * (t + 1))
                    for m, (x_part, w_part) in enumerate(((HH0[f // 4], w_high), (HH0[f // 4], w_low), (HL0[f // 4], w_high))):
                        last = mm(A.view(("down", pair_n))[:, 512 * b:512 * b + 512], x_part[:, c, tile], w_part[:, c, :],
                                  start=f == 0 and m == 0, stop=f == FF0 - 1 and m == 2)
                return last

            for c in range(UP_CHUNKS - 1):
                pe.wait_ge(sig("down_low"), c + 1)
                for f in range(4 * c, 4 * c + 4):
                    pe.wait_ge(sig("hidden0_low"), f + 1)
                    for n in range(3):
                        last = down(f, n)
                last.then_inc(sig("down_chunk_done"), 1)
            pe.wait_ge(sig("down_low"), UP_CHUNKS)
            pe.wait_ge(sig("hidden0_low"), FF0)
            for n in range(3):
                for f in range(FF0 - 4, FF0):
                    last = down(f, n)
                A.fill(last)
            for n in range(3):
                A.wait_evacuated(pe, ("down", n))

            def turn_head(r, h):
                for j in range(NT):
                    turn_tiles(r, ("pt", h, j), lambda t: P[:, h % 2, t, TILE * j:TILE * (j + 1)])

            pe.wait_ge(sig("padding_ready"), 1)

            with pe.Fori(0, LAYERS) as i:
                B.turn = i

                def make_conditioning(n, tiles=range(FT)):
                    for k in tiles:
                        for q, name in ((2 * n - 2, "scale"), (2 * n - 1, "bias")):
                            key = (name, n, k)
                            B.claim(pe, key)
                            B.fill(wide(B.view(key, 128), [(condw[:, q, 128 * k:128 * (k + 1)], condT[:, :])]))

                def arrived(name):
                    pe.wait_ge(sig(name + "_low"), i + 1)

                def input_part(name, n, wait):
                    return lambda c: wait and pe.wait_ge(sig(name), 2 * FT * i + (FT * (n - 1) + c + 1))

                def columns3(key, name, n, wait=False):
                    split_columns(B, key, WHIGH[SLOT[name]], WLOW[SLOT[name]], key[1], YH, YL,
                                  input_part("input_high", n, wait), input_part("input_low", n, wait))

                def rows3(name, weight, high, low, ready=None):
                    split_rows(B, name, high, low, WHIGH[SLOT[weight]], WLOW[SLOT[weight]], ready)

                def query_key1(h):
                    columns3(("q", h), "wq", 1, h == 0)
                    columns3(("k", h), "wk", 1)

                def make_scores(h):
                    pe.wait_ge(sig("query_key_low"), H1 * i + (h + 1))
                    for t in range(NT):
                        key = ("s", h, t)
                        B.claim(pe, key)
                        tile = slice(TILE * t, TILE * (t + 1))
                        qh, kh, ql, kl = QH[:, h % 2, tile], KH[:, h % 2, :], QL[:, h, tile], KL[:, h, :]
                        B.fill(wide(B.view(key), [(qh, kh), (qh, kl), (ql, kh)]))

                def turn(h):
                    pe.wait_ge(sig("probs_normalised"), H1 * NT * i + NT * (h + 1))
                    turn_head(B, h)

                def weigh(h):
                    key = ("av", h)
                    B.claim(pe, key)
                    part_wait(pe, "pe")
                    B.fill(wide(B.view(key, 128), [(V[:, j, 128 * h:128 * (h + 1)], PT[:, h % 2, j, :]) for j in range(NT)],
                                out_of_psum(B, "pt", h)))

                pe.wait_ge(sig("cond_parts_ready"), i + 1)
                make_conditioning(1)
                norm_columns(B, ("t", 1), XN, "xn_ready1", 2 * NT * i)
                arrived("wq")
                arrived("wk")
                query_key1(0)
                query_key1(1)
                make_scores(0)
                query_key1(2)
                make_scores(1)
                query_key1(3)
                arrived("wv")
                rows3("v", "wv", YH, YL)
                turn(0)
                make_scores(2)
                for n in range(3):
                    B.wait_evacuated(pe, ("v", n))
                weigh(0)
                turn(1)
                make_scores(3)
                weigh(1)
                turn(2)
                make_conditioning(2, (0, 1))
                weigh(2)
                turn(3)
                make_conditioning(2, (2, 3))
                weigh(3)
                arrived("wo")
                rows3("o", "wo", OH, OL, out_of_psum(B, "av"))
                norm_columns(B, ("t", 2), XN, "xn_ready1", 2 * NT * i + NT)
                arrived("m1")
                for f in range(FT):
                    columns3(("m1", f), "m1", 2, f == 0)
                arrived("m2")
                rows3("m2", "m2", HH, HL, lambda f: pe.wait_ge(sig("hidden_low"), FT * i + (f + 1)))
            B.turn = LAYERS - 1
            for n in range(3):
                B.wait_evacuated(pe, ("m2", n))
            norm_columns(C, ("t", 2), X, "xn_ready3", 0)
            pe.wait_ge(sig("ld_c"), 48)
            columns(C, ("hid",), lambda c: cw1[:, c, :], YT, p=HID2, arrived=out_of_psum(C, "t", 2))
            C.wait_evacuated(pe, ("hid",))
            all_rows(C, "h", HID2T.unsqueeze(1), cw2[:, :].unsqueeze(1), 1)
            for n in range(3):
                C.wait_evacuated(pe, ("h", n))
            pe.wait_ge(sig("ld_c2"), 32)
            all_rows(C, "agg", C2, V, NT)
            norm_columns(C, ("t", 3), X, "xn_ready3", NT)
            pe.wait_ge(sig("lone_weight_low"), 2)
            split_rows(C, "wx", YH, YL, WHIGH[0], WLOW[0], out_of_psum(C, "t", 3))
            for n in range(3):
                C.wait_evacuated(pe, ("wx", n))

            def g_rows(h):
                key = ("g", h)
                C.claim(pe, key)
                pe.wait_ge(sig("g_spread"), h + 1)
                for t in range(NT):
                    last = nc.tensor.transpose(C.view(key)[:, 128 * t:128 * t + TILE], g_bc[:, t, :], ident[0:TILE, 0:TILE])
                C.fill(last)

            g_rows(0)
            g_rows(1)
            for h in range(H3):
                pe.wait_ge(sig("exps_done3"), NT * (h + 1))
                turn_head(C, h)
                key = ("av", h)
                C.claim(pe, key)
                C.fill(wide(C.view(key, DH3, DH3 * (h % 2)), [(V[:, j, DH3 * h:DH3 * (h + 1)], PT[:, h % 2, j, :])
                                                              for j in range(NT)], out_of_psum(C, "pt", h)))
                if h + 2 < H3:
                    g_rows(h + 2)
            for h in range(H3 - 4, H3):
                C.wait_evacuated(pe, ("av", h))
            for n, pair in enumerate(PAIRS):
                key = ("x", n)
                C.claim(pe, key)
                for b, t in enumerate(pair):
                    for k in range(FT):
                        last = nc.tensor.transpose(C.view(key)[:, 512 * b + 128 * k:512 * b + 128 * (k + 1)],
                                                   OT3[:, k, TILE * t:TILE * (t + 1)], ident[:, :])
                C.fill(last)


def kernel(**inputs):
    import numpy as np
    import concourse.bacc as bacc
    from concourse.bass_utils import run_bass_kernel_spmd

    g = {k: np.asarray(v) for k, v in inputs.items()}

    def cols_of(vec):
        vec = np.asarray(vec, np.float32).reshape(-1)
        n = -(-vec.size // 128)
        return np.concatenate([vec, np.zeros(n * 128 - vec.size, np.float32)]).reshape(n, 128).T

    L0, L1, L2, L3 = ({k[7:]: v for k, v in g.items() if k.startswith(f"L{b}_gnn_")} for b in range(4))

    def part_cols(parts):
        first = np.repeat([0.0 if p == 0 else -1.0 for p in parts], COND)
        second = np.repeat([-1.0 if p == 2 else 0.0 for p in parts], COND)
        return [cols_of(first), cols_of(second)]

    freq = np.arange(1, NFREQ + 1, dtype=np.float32) * np.float32(2.0 * np.pi / 16)
    zeros, ones = np.zeros(NFREQ, np.float32), np.ones(NFREQ, np.float32)
    parts = [cols_of(L0[k]) for k in ("ln1_g", "ln1_b", "ln2_g", "ln2_b")]
    parts += [cols_of(L0["bqkv"][:D]), cols_of(L0["bqkv"][D:2 * D]), cols_of(L0["b1"])]
    parts += [cols_of(L1["f_b1"]), cols_of(np.tile(L1["f_b2"], 6)), cols_of(L2["b1"])]
    parts += [cols_of(np.concatenate([freq, freq])), cols_of(np.concatenate([zeros, ones * np.float32(0.25)])),
              cols_of(np.concatenate([zeros, ones * np.float32(np.pi / 2)]))]
    parts += part_cols((0, 0, 1, 0, 2, 1)) + part_cols((0, 1, 0, 2, 0, 1))
    for layer in range(LAYERS):
        parts += [cols_of(L1[k][layer]) for k in ("s1_b", "b1_b", "bq", "bk", "s2_b", "b2_b", "m_b1")]
    cols = np.concatenate(parts, axis=1)
    f_w2 = np.tile(L1["f_w2"], (1, 6))
    cond_w = np.stack([L1[k] for k in ("s1_w", "b1_w", "s2_w", "b2_w")], axis=2).reshape(LAYERS, COND, 4 * D)
    cond_w = np.concatenate([cond_w, np.zeros((1, COND, 4 * D), np.float32)])

    def edges(a):
        return a.reshape(CHUNKS, TILE, -1).transpose(1, 0, 2).reshape(TILE, -1)

    arrays = dict(
        x=g["x"], src_t=edges(g["src"]), dst_t=edges(g["dst"]), attr_a=edges(g["edge_attr_8"]),
        attr_b=edges(g["edge_attr_8_n2"]), noise=g["node_vec1"], cols_d=cols,
        w_qkv=L0["Wqkv"], w_o0=L0["Wo"], w_up0=L0["W1"], w_down0=L0["W2"],
        rows0=np.stack([L0["bqkv"][2 * D:], L0["bo"], L0["b2"]]),
        f_w1=L1["f_w1"], f_w2=f_w2, cond_w=cond_w,
        wq=L1["wq"], wk=L1["wk"], wv=L1["wv"], wo=L1["wo"], m_w1=L1["m_w1"], m_w2=L1["m_w2"],
        rows1=np.stack([L1["bv"], L1["bo"], L1["m_b2"]]),
        c_w1=L2["W1"], c_w2=L2["W2"], c_b2=L2["b2"],
        ws3=L3["Ws"].transpose(1, 0, 2).reshape(D, H3 * DH3),
        rows3=np.stack([L3["a_w"][:, :DH3].reshape(-1), L3["a_w"][:, DH3:].reshape(-1), L3["Wb"].reshape(-1)]),
        ab3=L3["a_b"],
    )
    nc = bacc.Bacc("TRN2", target_bir_lowering=False, num_devices=1)
    args = {}
    for name, a in arrays.items():
        arrays[name] = a = np.ascontiguousarray(a)
        args[name] = nc.dram_tensor("in_" + name, a.shape, mybir.dt.from_np(a.dtype), kind="ExternalInput").ap()
    out = nc.dram_tensor("out", (NODES, D), mybir.dt.float32, kind="ExternalOutput").ap()
    build(nc, **args, out=out)
    ran = run_bass_kernel_spmd(nc, [{"in_" + n: a for n, a in arrays.items()}], core_ids=[0])
    return ran.results[0]["out"]
```
